# Optimizing a Trainium2 kernel written in Bass

```python
import numpy as np
import jax
import jax.numpy as jnp

def _softmax(x, axis=-1):
    return jax.nn.softmax(x, axis=axis)

def _gelu(x):
    return jax.nn.gelu(x, approximate=True)

def _silu(x):
    return jax.nn.silu(x)

def _sigmoid(x):
    return jax.nn.sigmoid(x)

def _layernorm(x, axis=-1, eps=1e-05):
    m = jnp.mean(x, axis=axis, keepdims=True)
    v = jnp.var(x, axis=axis, keepdims=True)
    return (x - m) / jnp.sqrt(v + eps)

def _scatter_add(tgt, idx, src, axis=0):
    return tgt.at[idx].add(src)

def _segment_sum(src, seg, n):
    return jax.ops.segment_sum(src, seg, n)
kernel_name = 'mk_xattn_ffn_d2_seqx_r2_d22390'

def setup_inputs(seed: int=0):
    np.random.seed(seed)
    _w = jnp.asarray

    def _rec_inputs():
        import jax
        import jax.numpy as jnp
        _rk = jax.random.key(seed)
        x = -0.000125 + 0.9999 * jax.random.normal(jax.random.fold_in(_rk, 1), (16, 256, 2048), jnp.float32)
        _lenS = 256 - jax.random.randint(jax.random.fold_in(_rk, 7), (16,), 0, max(1, 256 // 4) + 1, jnp.int32)
        _lenS2 = 256 - jax.random.randint(jax.random.fold_in(_rk, 8), (16,), 0, max(1, 256 // 4) + 1, jnp.int32)
        _ctx_4096P = jax.random.normal(jax.random.fold_in(_rk, 11), (16, 16, 2048), jnp.float32)
        _ctx_4096c = jax.random.dirichlet(jax.random.fold_in(_rk, 511), 0.3 * jnp.ones((16,), jnp.float32), (16, 256))
        _ctx_4096t = jnp.einsum('bsk,bkd->bsd', _ctx_4096c, _ctx_4096P)
        _ctx_4096t = _ctx_4096t * jax.lax.rsqrt(jnp.mean(jnp.square(_ctx_4096t)) + 1e-12) * 0.953939
        ctx_4096 = -1.52775e-05 + 0.999936 * (_ctx_4096t + 0.3 * jax.random.normal(jax.random.fold_in(_rk, 611), (16, 256, 2048), jnp.float32))
        return (x, ctx_4096)
    x, ctx_4096 = _rec_inputs()

    def _L0_xattn_setup():
        import jax, jax.numpy as jnp
        import numpy as np
        H = 8
        C = 2

        def _autocorrelation(Q, K, V):
            B, L, D = Q.shape
            d = D // H
            q = Q.reshape(B, L, H, d).transpose(0, 2, 1, 3)
            k = K.reshape(B, L, H, d).transpose(0, 2, 1, 3)
            v = V.reshape(B, L, H, d).transpose(0, 2, 1, 3)
            qf = jnp.fft.fft(q, axis=2)
            kf = jnp.fft.fft(k, axis=2)
            corr = jnp.fft.ifft(qf * jnp.conj(kf), axis=2).real
            topk = int(C * np.log(L))
            w, idx = jax.lax.top_k(corr.transpose(0, 1, 3, 2), topk)
            w = jax.nn.softmax(w, axis=-1)
            pos = jnp.arange(L)[:, None]
            out = jnp.zeros_like(v)
            for i in range(topk):
                g = jnp.minimum(idx[:, :, None, :, i] + pos, L - 1)
                out = out + w[:, :, None, :, i] * jnp.take_along_axis(v, g, axis=2)
            return out.transpose(0, 2, 1, 3).reshape(B, L, D)
        key = jax.random.key(seed)
        k1, k2, k3 = jax.random.split(key, 3)
        B, L, D = (16, 256, 2048)
        Q = jax.random.normal(k1, (B, L, D), dtype=jnp.float32)
        K = jax.random.normal(k2, (B, L, D), dtype=jnp.float32)
        V = jax.random.normal(k3, (B, L, D), dtype=jnp.float32)
        return {'Q': Q, 'K': K, 'V': V}
    _L0_xattn_all = _L0_xattn_setup()
    _L0_xattn_in = {k: v for k, v in _L0_xattn_all.items() if k in ()}
    del _L0_xattn_all

    def _L0_ffn_setup():
        import jax, jax.numpy as jnp
        import numpy as np
        RANKS = (8, 16, 32, 64)
        TOPK = 1
        SCALING = 1.0 / 4
        key = jax.random.key(seed)
        ks = jax.random.split(key, 7)
        D_IN, D_OUT, MAX_R, N_RANKS = (2048, 2048, 64, len(RANKS))
        B_, S_ = (4, 1024)
        return {'hidden_states': jax.random.normal(ks[0], (B_, S_, D_IN), jnp.float32), 'W': jax.random.normal(ks[1], (D_OUT, D_IN), jnp.float32) * 0.02, 'b': jax.random.normal(ks[2], (D_OUT,), jnp.float32) * 0.02, 'A': jax.random.normal(ks[3], (MAX_R, D_IN), jnp.float32) * 0.02, 'B': jnp.zeros((D_OUT, MAX_R), jnp.float32) + jax.random.normal(ks[4], (D_OUT, MAX_R), jnp.float32) * 0.02, 'gate_w': jax.random.normal(ks[5], (N_RANKS, D_IN), jnp.float32) * 0.02, 'gate_b': jax.random.normal(ks[6], (N_RANKS,), jnp.float32) * 0.02}
    _L0_ffn_all = _L0_ffn_setup()
    _L0_ffn_in = {k: v for k, v in _L0_ffn_all.items() if k in ('W', 'b', 'A', 'B', 'gate_w', 'gate_b')}
    del _L0_ffn_all

    def _L1_xattn_setup():
        import jax, jax.numpy as jnp
        import numpy as np
        import math
        EPS = 1e-05
        LAMBDA = 0.6

        def _crucial_k(C):
            f = math.floor(LAMBDA * C)
            return f + f % 2

        def _conv1d(y, w):
            return jax.lax.conv_general_dilated(y, w, window_strides=(1,), padding=((3, 3),), dimension_numbers=('NCH', 'OIH', 'NCH'))

        def _norm_active(z, gamma, beta):
            mu = jnp.mean(z, axis=(0, 2), keepdims=True)
            var = jnp.mean((z - mu) ** 2, axis=(0, 2), keepdims=True)
            zn = (z - mu) * jax.lax.rsqrt(var + EPS)
            zn = zn * gamma.reshape(1, -1, 1) + beta.reshape(1, -1, 1)
            return jax.nn.sigmoid(jax.nn.relu(zn))
        key = jax.random.key(seed)
        k1, k2, k3 = jax.random.split(key, 3)
        B, C, L = (32, 128, 2048)
        x = jax.random.normal(k1, (B, C, L), dtype=jnp.float32)
        channel_map = jax.random.normal(k2, (B, C, L), dtype=jnp.float32)
        fan_in = 2 * 7
        bound = 1.0 / math.sqrt(fan_in)
        conv_w = jax.random.uniform(k3, (1, 2, 7), jnp.float32, -bound, bound)
        bn_gamma = jnp.ones((1,), jnp.float32)
        bn_beta = jnp.zeros((1,), jnp.float32)
        return {'x': x, 'channel_map': channel_map, 'conv_w': conv_w, 'bn_gamma': bn_gamma, 'bn_beta': bn_beta}
    _L1_xattn_all = _L1_xattn_setup()
    _L1_xattn_in = {k: v for k, v in _L1_xattn_all.items() if k in ('conv_w', 'bn_gamma', 'bn_beta')}
    del _L1_xattn_all

    def _L1_ffn_setup():
        import jax, jax.numpy as jnp
        import numpy as np
        K_TOP = 8
        key = jax.random.key(seed)
        k1, k2, k3 = jax.random.split(key, 3)
        B, S, H, E = (4, 2048, 2048, 64)
        hidden_states = jax.random.normal(k1, (B, S, H), dtype=jnp.float32)
        router_weight = jax.random.normal(k2, (E, H), dtype=jnp.float32)
        router_bias = jnp.zeros((E,), dtype=jnp.float32)
        expert_bias = jax.random.normal(k3, (E, H), dtype=jnp.float32) * 0.1
        return {'hidden_states': hidden_states, 'router_weight': router_weight, 'router_bias': router_bias, 'expert_bias': expert_bias}
    _L1_ffn_all = _L1_ffn_setup()
    _L1_ffn_in = {k: v for k, v in _L1_ffn_all.items() if k in ('router_weight', 'router_bias', 'expert_bias')}
    del _L1_ffn_all
    return {'x': x, 'ctx_4096': ctx_4096, 'L0_ffn_W': _L0_ffn_in['W'], 'L0_ffn_b': _L0_ffn_in['b'], 'L0_ffn_A': _L0_ffn_in['A'], 'L0_ffn_B': _L0_ffn_in['B'], 'L0_ffn_gate_w': _L0_ffn_in['gate_w'], 'L0_ffn_gate_b': _L0_ffn_in['gate_b'], 'L1_xattn_conv_w': _L1_xattn_in['conv_w'], 'L1_xattn_bn_gamma': _L1_xattn_in['bn_gamma'], 'L1_xattn_bn_beta': _L1_xattn_in['bn_beta'], 'L1_ffn_router_weight': _L1_ffn_in['router_weight'], 'L1_ffn_router_bias': _L1_ffn_in['router_bias'], 'L1_ffn_expert_bias': _L1_ffn_in['expert_bias']}

def reference(x, ctx_4096, L0_ffn_W, L0_ffn_b, L0_ffn_A, L0_ffn_B, L0_ffn_gate_w, L0_ffn_gate_b, L1_xattn_conv_w, L1_xattn_bn_gamma, L1_xattn_bn_beta, L1_ffn_router_weight, L1_ffn_router_bias, L1_ffn_expert_bias):
    import jax
    import jax.numpy as jnp

    def _L0_xattn_ref(Q, K, V):
        import jax, jax.numpy as jnp
        import numpy as np
        H = 8
        C = 2

        def _autocorrelation(Q, K, V):
            B, L, D = Q.shape
            d = D // H
            q = Q.reshape(B, L, H, d).transpose(0, 2, 1, 3)
            k = K.reshape(B, L, H, d).transpose(0, 2, 1, 3)
            v = V.reshape(B, L, H, d).transpose(0, 2, 1, 3)
            qf = jnp.fft.fft(q, axis=2)
            kf = jnp.fft.fft(k, axis=2)
            corr = jnp.fft.ifft(qf * jnp.conj(kf), axis=2).real
            topk = int(C * np.log(L))
            w, idx = jax.lax.top_k(corr.transpose(0, 1, 3, 2), topk)
            w = jax.nn.softmax(w, axis=-1)
            pos = jnp.arange(L)[:, None]
            out = jnp.zeros_like(v)
            for i in range(topk):
                g = jnp.minimum(idx[:, :, None, :, i] + pos, L - 1)
                out = out + w[:, :, None, :, i] * jnp.take_along_axis(v, g, axis=2)
            return out.transpose(0, 2, 1, 3).reshape(B, L, D)
        return _autocorrelation(Q, K, V)

    def _L0_ffn_ref(hidden_states, W, b, A, B, gate_w, gate_b):
        import jax, jax.numpy as jnp
        import numpy as np
        RANKS = (8, 16, 32, 64)
        TOPK = 1
        SCALING = 1.0 / 4
        bsz, seq, d_in = hidden_states.shape
        out = jnp.einsum('bsd,od->bso', hidden_states, W) + b
        x = hidden_states.reshape(-1, d_in)
        scores = x @ gate_w.T + gate_b
        probs = jax.nn.softmax(scores, axis=-1)
        routing_weights, selected = jax.lax.top_k(probs, TOPK)
        routing_weights = routing_weights / jnp.sum(routing_weights, axis=-1, keepdims=True)
        lora_outputs = jnp.stack([x @ A[:r, :].T @ B[:, :r].T for r in RANKS], axis=1)
        sel = jnp.take_along_axis(lora_outputs, selected[:, :, None], axis=1)
        final = jnp.sum(sel * routing_weights[:, :, None], axis=1)
        return out + final.reshape(bsz, seq, -1)

    def _L1_xattn_ref(x, channel_map, conv_w, bn_gamma, bn_beta):
        import jax, jax.numpy as jnp
        import numpy as np
        import math
        EPS = 1e-05
        LAMBDA = 0.6

        def _crucial_k(C):
            f = math.floor(LAMBDA * C)
            return f + f % 2

        def _conv1d(y, w):
            return jax.lax.conv_general_dilated(y, w, window_strides=(1,), padding=((3, 3),), dimension_numbers=('NCH', 'OIH', 'NCH'))

        def _norm_active(z, gamma, beta):
            mu = jnp.mean(z, axis=(0, 2), keepdims=True)
            var = jnp.mean((z - mu) ** 2, axis=(0, 2), keepdims=True)
            zn = (z - mu) * jax.lax.rsqrt(var + EPS)
            zn = zn * gamma.reshape(1, -1, 1) + beta.reshape(1, -1, 1)
            return jax.nn.sigmoid(jax.nn.relu(zn))
        B, C, L = x.shape
        k = _crucial_k(C)
        cm = jnp.moveaxis(channel_map, 1, 2)
        _, topk_idx = jax.lax.top_k(cm, k)
        b_idx = jnp.arange(B)[:, None, None]
        l_idx = jnp.arange(L)[None, :, None]
        mask = jnp.zeros((B, L, C), x.dtype).at[b_idx, l_idx, topk_idx].set(1.0)
        crucial_channels = jnp.moveaxis(mask, 2, 1)
        subcrucial_channels = 1.0 - crucial_channels
        crucial_features = crucial_channels * x
        subcrucial_features = subcrucial_channels * x
        c_max = jnp.max(crucial_features, axis=1, keepdims=True)
        c_avg = jnp.mean(crucial_features, axis=1, keepdims=True) * (C / k)
        s_max = jnp.max(subcrucial_features, axis=1, keepdims=True)
        s_avg = jnp.mean(subcrucial_features, axis=1, keepdims=True) * (C / (C - k))
        crucial_x = jnp.concatenate([c_max, c_avg], axis=1)
        subcrucial_x = jnp.concatenate([s_max, s_avg], axis=1)
        A_S1 = _norm_active(_conv1d(crucial_x, conv_w), bn_gamma, bn_beta)
        A_S2 = _norm_active(_conv1d(subcrucial_x, conv_w), bn_gamma, bn_beta)
        return crucial_features * A_S1 + subcrucial_features * A_S2

    def _L1_ffn_ref(hidden_states, router_weight, router_bias, expert_bias):
        import jax, jax.numpy as jnp
        import numpy as np
        K_TOP = 8
        B, S, H = hidden_states.shape
        E = router_weight.shape[0]
        T = B * S
        flat = hidden_states.reshape(T, H)
        logits = jnp.einsum('th,eh->te', flat, router_weight) + router_bias
        scores = jax.nn.softmax(logits, axis=-1)
        topk_w, topk_idx = jax.lax.top_k(scores, K_TOP)
        w_sum = topk_w.sum(axis=-1, keepdims=True)
        w_dense = jnp.zeros((T, E), dtype=scores.dtype).at[jnp.arange(T)[:, None], topk_idx].add(topk_w)
        bias_mix = jnp.einsum('te,eh->th', w_dense, expert_bias)
        out = flat * w_sum + bias_mix
        return out.reshape(B, S, H)
    x = x + _L0_xattn_ref(_layernorm(x, axis=-1), ctx_4096, ctx_4096)
    x = x + _L0_ffn_ref(_layernorm(x, axis=-1), L0_ffn_W, L0_ffn_b, L0_ffn_A, L0_ffn_B, L0_ffn_gate_w, L0_ffn_gate_b)
    x = x + _L1_xattn_ref(_layernorm(x, axis=-1), ctx_4096, L1_xattn_conv_w, L1_xattn_bn_gamma, L1_xattn_bn_beta)
    x = x + _L1_ffn_ref(_layernorm(x, axis=-1), L1_ffn_router_weight, L1_ffn_router_bias, L1_ffn_expert_bias)
    return x

_drawn_inputs = setup_inputs


def setup_inputs(seed=0):
    import zlib

    import numpy as np

    out = dict(_drawn_inputs(seed))
    spreads = {'L1_ffn_router_bias': (0.0, 2.0)}
    factors = {'L0_ffn_b': 4.682, 'L0_ffn_gate_b': 30.389}
    for name, (base, spread) in spreads.items():
        noise = np.random.default_rng([zlib.crc32(name.encode()), seed]).standard_normal(out[name].shape)
        drawn = base * np.exp(spread * noise) if base else spread * noise
        out[name] = jnp.asarray(drawn.astype(out[name].dtype))
    for name, factor in factors.items():
        out[name] = (out[name] * factor).astype(out[name].dtype)
    return out
```

```python
import numpy as np
import concourse.bass as bass
from concourse import mybir
from concourse.alu_op_type import AluOpType as ALU
from contextlib import ExitStack

FP32 = mybir.dt.float32
FP32R = mybir.dt.float32r
FP16 = mybir.dt.float16
UINT8 = mybir.dt.uint8
ACT = mybir.ActivationFunctionType
AX = mybir.AxisListType
P = 128
EPS = 1e-5
W_SCALE = 64.0


def dft_constants(L):
    F = L // 2
    t = np.arange(L)[:, None].astype(np.float64)
    f = np.arange(F)[None, :].astype(np.float64)
    alt = (-1.0) ** np.arange(L)
    cos_e, sin_e = np.cos(2 * np.pi * t * f / L), np.sin(2 * np.pi * t * f / L)
    cos_e[:, 0] = alt
    q = np.concatenate([cos_e, sin_e], 1)
    q[:, F] = 0.0
    k = q.copy()
    k[:, F] = 1.0
    k[L - 1, F] = 1.0 + L
    we = q.copy()
    we[:, F] = 1.0
    wo_ = np.pi * t * (2 * f + 1) / L
    wo = np.concatenate([np.cos(wo_), np.sin(wo_)], 1)
    vo = wo.copy()
    vo[L - 1] -= wo.sum(0)
    p = np.arange(L)[None, :].astype(np.float64)
    fc = np.arange(F)[:, None].astype(np.float64)
    ce, se = np.cos(2 * np.pi * fc * p / L), np.sin(2 * np.pi * fc * p / L)
    ic = np.concatenate([2 * ce, -2 * se], 0) / L
    ic[0] = alt / L
    ic[F] = 0.0
    ie = np.concatenate([2 * ce, 2 * se], 0) / (2 * L)
    ie[0] = alt / (2 * L)
    ie[F] = -1.0 / (2 * L)
    a = np.pi * (2 * fc + 1) * p / L
    io = np.concatenate([2 * np.cos(a), 2 * np.sin(a)], 0) / (2 * L)
    return q, k, we, vo, wo, ic, ie, io


def counted(eng, n):
    return n if isinstance(n, int) else eng.snap(eng.to_reg(n))


def attention_phase(nc, x, ctx, xT, dft, x1):
    NB, L, D = x.shape
    TT = L // P
    CW = 512
    CH = D // CW
    CT = CW // P
    TOPK = int(2 * np.log(L))
    STEPS = 2 * CH
    ITS = NB // 2
    LAST = NB * CH
    NEG = -3.0e38
    AFTER_LN, AFTER_F, AFTER_C, AFTER_T, AFTER_I = 1, 2, 3, 4, 5

    stack = ExitStack()
    sb = lambda name, shape, dt=FP32: stack.enter_context(nc.sbuf_tensor(name, shape, dt))
    pb = lambda name, shape: stack.enter_context(nc.psum_tensor(name, shape, FP32))
    sems = []

    def sem(name):
        sems.append(nc.alloc_semaphore(name))
        return sems[-1]
    with stack:
        m_q, m_k, m_we, m_vo, m_wo, m_ic = (sb("m_" + n, [P, TT, L]) for n in ("q", "k", "we", "vo", "wo", "ic"))
        m_iz = sb("m_iz", [P, 2 * TT, L])
        ident = sb("ident", [P, P])
        not_slot0 = sb("not_slot0", [P, 1])
        eps = sb("eps", [P, 1])
        xn = [sb(f"xn{i}", [P, TT, D]) for i in range(2)]
        cx = [sb(f"cx{i}", [P, TT, CW]) for i in range(4)]
        xt = [sb(f"xt{i}", [P, CT, L]) for i in range(2)]
        qf = [sb(f"qf{i}", [P, 2, CW]) for i in range(2)]
        kf = [sb(f"kf{i}", [P, 3, CW]) for i in range(4)]
        vf = [sb(f"vf{i}", [P, 3, CW]) for i in range(4)]
        pr = sb("pr", [P, 4, CW])
        pf = [sb(f"pf{i}", [P, 2, CW]) for i in range(2)]
        co = [sb(f"co{i}", [P, CT, L]) for i in range(2)]
        wk = [sb(f"wk{i}", [P, CT, L]) for i in range(2)]
        top = [sb(f"top{i}", [P, CT, 16]) for i in range(2)]
        nmax = [sb(f"nmax{i}", [P, CT]) for i in range(2)]
        wsum = [sb(f"wsum{i}", [P, CT]) for i in range(2)]
        wrec = [sb(f"wrec{i}", [P, CT]) for i in range(2)]
        wt = sb("wt", [P, TT, CW])
        zf = [sb(f"zf{i}", [P, 4, CW]) for i in range(2)]
        xo = [sb(f"xo{i}", [P, CT, L]) for i in range(2)]
        st = sb("st", [P, TT, D // 512, 6])
        mv = sb("mv", [P, TT, 2])
        std = sb("std", [P, TT])
        rstd = sb("rstd", [P, TT])
        nmr = sb("nmr", [P, TT])
        bx, by, bz, bu = (pb(n, [P, 2, 512]) for n in ("bx", "by", "bz", "bu"))

        consts_in = sem("consts_in")
        x_in = [sem(f"x_in{i}") for i in range(2)]
        cx_in = [sem(f"cx_in{i}") for i in range(4)]
        xt_in = [sem(f"xt_in{i}") for i in range(2)]
        x1_out = [sem(f"x1_out{i}") for i in range(2)]
        const_set, ln_bn, ln_mv, ln_std, ln_rstd, ln_scale, x_normed = map(sem, (
            "const_set", "ln_bn", "ln_mv", "ln_std", "ln_rstd", "ln_scale", "x_normed"))
        q_mm, k_mm, v_mm, c_mm, t_mm, we_mm, wo_mm, i_mm = map(sem, (
            "q_mm", "k_mm", "v_mm", "c_mm", "t_mm", "we_mm", "wo_mm", "i_mm"))
        q_sb, k_part, k_sb, v_sb, c_sb, wt_sb, e_sb, w_sb = map(sem, (
            "q_sb", "k_part", "k_sb", "v_sb", "c_sb", "wt_sb", "e_sb", "w_sb"))
        p_mul, p_sum, top_a, top_cut, top_b, nmax_ok, w_cut, w_rec, ze_mul, ze_sum, zo_mul, zo_sum, x1_sum = map(sem, (
            "p_mul", "p_sum", "top_a", "top_cut", "top_b", "nmax_ok", "w_cut", "w_rec", "ze_mul", "ze_sum", "zo_mul", "zo_sum", "x1_sum"))
        N_CONST = 8
        block = stack.enter_context(nc.Block())

        def steps(eng, step, drain):
            for k in range(STEPS):
                step(0, k)
            if ITS > 1:
                with eng.Fori(1, ITS) as it:
                    for k in range(STEPS):
                        step(it, k)
            for k in range(drain):
                step(ITS, k)

        def chunk(it, k, lag):
            h = STEPS * it + (k - lag)
            return None if isinstance(h, int) and not 0 <= h < LAST else h

        def batch(it, k):
            b = 2 * it + k // CH
            return None if k % CH or (isinstance(b, int) and b >= NB) else b

        def dram_batch(ap, it, k, lag):
            return ap[bass.ds(2 * it + (k - lag) // CH, 1), :, :].rearrange("a p n -> p (a n)")

        @block.sync
        def _(sp):
            for tile, m in zip((m_q, m_k, m_we, m_vo, m_wo, m_ic, m_iz), dft[:7]):
                sp.dma_start(tile[:], m.rearrange("(a p) n -> p a n", p=P)).then_inc(consts_in, 16)
            sp.dma_start(ident[:], dft[7]).then_inc(consts_in, 16)

            def step(it, k):
                b = batch(it, k)
                if b is not None:
                    if not isinstance(b, int) or b >= 2:
                        sp.wait_ge(v_mm, CH * (b - 1))
                        sp.wait_ge(q_mm, CH * (b - 1))
                    sp.dma_start(xn[(k // CH) % 2][:], x[bass.ds(b, 1), :, :].rearrange("a (t p) n -> p (a t) n", p=P)).then_inc(x_in[(k // CH) % 2], 16)
                h = chunk(it, k, 1)
                if h is not None:
                    s = (k - 1) % 4
                    if not isinstance(h, int) or h >= 4:
                        sp.wait_ge(v_mm, h - 3)
                    c = (k - 1) % CH
                    sp.dma_start(cx[s][:], ctx[bass.ds(2 * it + (k - 1) // CH, 1), :, c * CW:(c + 1) * CW].rearrange("a (t p) n -> p (a t) n", p=P)).then_inc(cx_in[s], 16)
                h = chunk(it, k, 3)
                if h is not None:
                    s = (k - 3) % 2
                    if not isinstance(h, int) or h >= 2:
                        sp.wait_ge(x1_sum, h - 1)
                    c = (k - 3) % CH
                    sp.dma_start(xt[s][:], xT[bass.ds(2 * it + (k - 3) // CH, 1), c * CW:(c + 1) * CW, :].rearrange("a (j p) t -> p (a j) t", p=P)).then_inc(xt_in[s], 16)
            steps(sp, step, 3)

        @block.gpsimd
        def _(pool):
            pool.memset(not_slot0[:], 1.0).then_inc(const_set, 1)
            pool.memset(eps[:], EPS).then_inc(const_set, 1)
            pool.wait_ge(const_set, 2)
            pool.memset(not_slot0[0:1, :], 0.0).then_inc(const_set, 1)

            def step(it, k):
                h = chunk(it, k, AFTER_I)
                if h is None:
                    return
                s, c = (k - AFTER_I) % 2, (k - AFTER_I) % CH
                n_ready = counted(pool, h + 1)
                pool.wait_ge(const_set, 3)
                pool.wait_ge(x1_sum, n_ready)
                bb = (k - AFTER_I) // CH
                pool.dma_start(x1[bass.ds(it + bb // 2, 1), :, c * CT:(c + 1) * CT, bb % 2 * L:(bb % 2 + 1) * L].rearrange("a p j t -> p (a j) t"), xo[s][:]).then_inc(x1_out[s], 16)
            steps(pool, step, AFTER_I)
            for s in range(2):
                pool.wait_ge(x1_out[s], 16 * (LAST // 2))

        @block.tensor
        def _(pe):
            pe.wait_ge(consts_in, 16 * N_CONST)

            def transform(out, mats, src, done):
                for m in range(2):
                    for a in range(TT):
                        mm = pe.matmul(out[:, m, :], mats[:, a, m * P:(m + 1) * P], src[:, a, :], start=a == 0, stop=a == TT - 1)
                mm.then_inc(done, 1)

            def step(it, k):
                h = chunk(it, k, AFTER_F)
                if h is not None:
                    kk = k - AFTER_F
                    slot, c = (kk // CH) % 2, kk % CH
                    src = xn[slot][:, :, c * CW:(c + 1) * CW]
                    if c == 0:
                        pe.wait_ge(x_normed, TT * (2 * it + kk // CH + 1))
                    if not isinstance(h, int) or h >= 2:
                        pe.wait_ge(c_sb, h - 1)
                    elif h == 1:
                        pe.wait_ge(q_sb, 1)
                    transform(bx, m_q, src, q_mm)
                    pe.wait_ge(cx_in[kk % 4], 16 * (2 * it + kk // 4 + 1))
                    if not isinstance(h, int) or h >= 3:
                        pe.wait_ge(ze_mul, 2 * (h - 2))
                    elif h >= 1:
                        pe.wait_ge(k_sb, h)
                    transform(by, m_k, cx[kk % 4], k_mm)
                    if not isinstance(h, int) or h >= 3:
                        pe.wait_ge(zo_mul, 2 * (h - 2))
                    elif h >= 1:
                        pe.wait_ge(v_sb, h)
                    transform(bz, m_vo, cx[kk % 4], v_mm)
                h = chunk(it, k, AFTER_T)
                if h is not None:
                    s = (k - AFTER_T) % 2
                    pe.wait_ge(w_sb, CT * (h + 1))
                    if not isinstance(h, int) or h >= 2:
                        pe.wait_ge(x1_sum, h - 1)
                    elif h == 1:
                        pe.wait_ge(wt_sb, 1)
                    for a in range(TT):
                        for j in range(CT):
                            mm = pe.transpose(bu[:, a, j * P:(j + 1) * P], wk[s][:, j, a * P:(a + 1) * P], ident[:])
                    mm.then_inc(t_mm, 1)
                h = chunk(it, k, AFTER_C)
                if h is not None:
                    s = (k - AFTER_C) % 2
                    pe.wait_ge(p_sum, 2 * (h + 1))
                    g = chunk(it, k, AFTER_F)
                    if g is not None:
                        pe.wait_ge(q_sb, g + 1)
                    else:
                        pe.wait_ge(q_sb, LAST)
                        pe.wait_ge(c_sb, h)
                    for j in range(CT):
                        for a in range(TT):
                            mm = pe.matmul(bx[:, j // 2, (j % 2) * L:(j % 2 + 1) * L], pf[s][:, a, j * P:(j + 1) * P], m_ic[:, a, :], start=a == 0, stop=a == TT - 1)
                    mm.then_inc(c_mm, 1)
                h = chunk(it, k, AFTER_T)
                if h is not None:
                    g = chunk(it, k, AFTER_F)
                    n = LAST if g is None else g + 1
                    pe.wait_ge(wt_sb, h + 1)
                    if g is None:
                        pe.wait_ge(zo_mul, 2 * h)
                        pe.wait_ge(ze_mul, 2 * h)
                    pe.wait_ge(k_sb, n)
                    transform(by, m_we, wt, we_mm)
                    pe.wait_ge(v_sb, n)
                    transform(bz, m_wo, wt, wo_mm)
                h = chunk(it, k, AFTER_I)
                if h is not None:
                    s = (k - AFTER_I) % 2
                    pe.wait_ge(ze_sum, 2 * (h + 1))
                    pe.wait_ge(zo_sum, 2 * (h + 1))
                    g = chunk(it, k, AFTER_T)
                    pe.wait_ge(wt_sb, LAST if g is None else g + 1)
                    if g is None:
                        pe.wait_ge(x1_sum, h)
                    for j in range(CT):
                        for a in range(2 * TT):
                            mm = pe.matmul(bu[:, j // 2, (j % 2) * L:(j % 2 + 1) * L], zf[s][:, a, j * P:(j + 1) * P], m_iz[:, a, :], start=a == 0, stop=a == 2 * TT - 1)
                    mm.then_inc(i_mm, 1)
            steps(pe, step, AFTER_I)

        @block.scalar
        def _(act):
            act.wait_ge(const_set, 3)

            def step(it, k):
                b = batch(it, k - AFTER_LN) if k >= AFTER_LN else None
                if b is not None:
                    act.wait_ge(ln_scale, b + 1)
                    for a in range(TT):
                        tile = xn[((k - AFTER_LN) // CH) % 2][:, a, :]
                        act.activation(tile, tile, ACT.Identity, bias=nmr[:, a:a + 1], scale=rstd[:, a:a + 1]).then_inc(x_normed, 1)
                h = chunk(it, k, AFTER_F)
                if h is not None:
                    kk = k - AFTER_F
                    s, s4 = kk % 2, kk % 4
                    act.wait_ge(q_mm, h + 1)
                    if not isinstance(h, int) or h >= 2:
                        act.wait_ge(p_mul, 2 * (h - 1))
                    act.activation(qf[s][:], bx[:], ACT.Copy).then_inc(q_sb, 1)
                    act.wait_ge(k_mm, h + 1)
                    if not isinstance(h, int) or h >= 4:
                        act.wait_ge(ze_mul, 2 * (h - 3))
                    act.activation(kf[s4][:, 0, :], by[:, 0, :], ACT.Copy).then_inc(k_part, 1)
                    act.activation(kf[s4][:, 2, :], by[:, 0, :], ACT.Copy).then_inc(k_part, 1)
                    act.activation(kf[s4][:, 1, :], by[:, 1, :], ACT.Copy, scale=not_slot0[:]).then_inc(k_part, 1)
                    act.wait_ge(k_part, 3 * h + 3)
                    act.activation(kf[s4][0:1, 2, :], by[0:1, 1, :], ACT.Copy).then_inc(k_sb, 1)
                    act.wait_ge(v_mm, h + 1)
                    if not isinstance(h, int) or h >= 4:
                        act.wait_ge(zo_mul, 2 * (h - 3))
                    act.activation(vf[s4][:, 0:2, :], bz[:], ACT.Copy)
                    act.activation(vf[s4][:, 2, :], bz[:, 0, :], ACT.Copy).then_inc(v_sb, 1)
                h = chunk(it, k, AFTER_T)
                if h is not None:
                    act.wait_ge(t_mm, h + 1)
                    if not isinstance(h, int) or h >= 1:
                        act.wait_ge(wo_mm, h)
                    act.activation(wt[:], bu[:], ACT.Copy).then_inc(wt_sb, 1)
                h = chunk(it, k, AFTER_C)
                if h is not None:
                    s = (k - AFTER_C) % 2
                    act.wait_ge(c_mm, h + 1)
                    if not isinstance(h, int) or h >= 2:
                        act.wait_ge(w_cut, CT * (h - 1))
                    act.activation(co[s][:].rearrange("p (a j) t -> p a (j t)", a=2), bx[:], ACT.Copy).then_inc(c_sb, 1)
                    act.wait_ge(c_sb, h + 1)
                    act.wait_ge(nmax_ok, h + 1)
                    for j in range(CT):
                        act.activation(wk[s][:, j, :], co[s][:, j, :], ACT.Exp, bias=nmax[s][:, j:j + 1]).then_inc(e_sb, 1)
                    act.wait_ge(w_rec, h + 1)
                    for j in range(CT):
                        act.activation(wk[s][:, j, :], wk[s][:, j, :], ACT.Copy, scale=wrec[s][:, j:j + 1]).then_inc(w_sb, 1)
                b = batch(it, k)
                if b is not None:
                    act.wait_ge(ln_mv, TT * (b + 1))
                    act.activation(std[:], mv[:, :, 1], ACT.Sqrt, bias=eps[:]).then_inc(ln_std, 1)
            steps(act, step, AFTER_I)

        @block.vector
        def _(dve):
            def products(src, spectrum, scratch, out, mul, added, h):
                dve.tensor_tensor(scratch[:, 0:2, :], src, spectrum[:, 0:2, :], ALU.mult).then_inc(mul, 1)
                dve.tensor_tensor(scratch[:, 2:4, :], src, spectrum[:, 1:3, :], ALU.mult).then_inc(mul, 1)
                dve.wait_ge(mul, 2 * h + 1)
                dve.tensor_tensor(out[:, 0, :], scratch[:, 0, :], scratch[:, 1, :], ALU.add).then_inc(added, 1)
                dve.wait_ge(mul, 2 * h + 2)
                dve.tensor_tensor(out[:, 1, :], scratch[:, 2, :], scratch[:, 3, :], ALU.subtract).then_inc(added, 1)

            def step(it, k):
                b = batch(it, k)
                if b is not None:
                    slot = (k // CH) % 2
                    dve.wait_ge(x_in[slot], 16 * (it + 1))
                    for a in range(TT):
                        for n in range(D // 512):
                            dve.bn_stats(st[:, a, n, :], xn[slot][:, a, n * 512:(n + 1) * 512]).then_inc(ln_bn, 1)
                    n_ready = counted(dve, TT * (D // 512) * (b + 1))
                    dve.wait_ge(consts_in, 16 * N_CONST)
                    dve.wait_ge(ln_bn, n_ready)
                    for a in range(TT):
                        dve.bn_aggr(mv[:, a, :], st[:, a, :, :]).then_inc(ln_mv, 1)
                b = batch(it, k - AFTER_LN) if k >= AFTER_LN else None
                if b is not None:
                    dve.wait_ge(ln_std, b + 1)
                    if not isinstance(b, int) or b >= 1:
                        dve.wait_ge(x_normed, TT * b)
                    dve.reciprocal(rstd[:], std[:]).then_inc(ln_rstd, 1)
                    dve.wait_ge(ln_rstd, b + 1)
                    dve.scalar_tensor_tensor(nmr[:], mv[:, :, 0], -1.0, rstd[:], ALU.mult, ALU.mult).then_inc(ln_scale, 1)
                h = chunk(it, k, AFTER_F)
                if h is not None:
                    kk = k - AFTER_F
                    dve.wait_ge(q_sb, h + 1)
                    dve.wait_ge(k_sb, h + 1)
                    if not isinstance(h, int) or h >= 3:
                        dve.wait_ge(zo_sum, 2 * (h - 2))
                    elif h >= 1:
                        dve.wait_ge(p_sum, 2 * h)
                    if not isinstance(h, int) or h >= 2:
                        dve.wait_ge(c_mm, h - 1)
                    products(qf[kk % 2][:], kf[kk % 4], pr, pf[kk % 2], p_mul, p_sum, h)
                h = chunk(it, k, AFTER_C)
                if h is not None:
                    s = (k - AFTER_C) % 2
                    n_ready, n_used = counted(dve, h + 1), counted(dve, h - 1)
                    dve.wait_ge(consts_in, 16 * N_CONST)
                    if not isinstance(h, int) or h >= 2:
                        dve.wait_ge(t_mm, n_used)
                    dve.wait_ge(c_sb, n_ready)
                    for j in range(CT):
                        dve.max(top[s][:, j, 0:8], co[s][:, j, :]).then_inc(top_a, 1)
                    for j in range(CT):
                        n_ready = counted(dve, CT * h + j + 1)
                        dve.wait_ge(consts_in, 16 * N_CONST)
                        dve.wait_ge(top_a, n_ready)
                        dve.match_replace(wk[s][:, j, :], top[s][:, j, 0:8], co[s][:, j, :], NEG).then_inc(top_cut, 1)
                    for j in range(CT):
                        n_ready = counted(dve, CT * h + j + 1)
                        dve.wait_ge(consts_in, 16 * N_CONST)
                        dve.wait_ge(top_cut, n_ready)
                        dve.max(top[s][:, j, 8:16], wk[s][:, j, :]).then_inc(top_b, 1)
                    dve.wait_ge(top_b, CT * (h + 1))
                    dve.tensor_scalar(nmax[s][:], top[s][:, :, 0], -1.0, None, ALU.mult).then_inc(nmax_ok, 1)
                h = chunk(it, k, AFTER_T)
                if h is not None:
                    s4, s = (k - AFTER_T) % 4, (k - AFTER_T) % 2
                    g = chunk(it, k, AFTER_F)
                    dve.wait_ge(p_sum, 2 * LAST if g is None else 2 * (g + 1))
                    if not isinstance(h, int) or h >= 2:
                        dve.wait_ge(i_mm, h - 1)
                    dve.wait_ge(we_mm, h + 1)
                    products(by[:], kf[s4], pr, zf[s][:, 0:2, :], ze_mul, ze_sum, h)
                    dve.wait_ge(ze_sum, 2 * (h + 1))
                    dve.wait_ge(wo_mm, h + 1)
                    products(bz[:], vf[s4], pr, zf[s][:, 2:4, :], zo_mul, zo_sum, h)
                h = chunk(it, k, AFTER_C)
                if h is not None:
                    s = (k - AFTER_C) % 2
                    for j in range(CT):
                        dve.wait_ge(e_sb, CT * h + j + 1)
                        dve.scalar_tensor_tensor(wk[s][:, j, :], co[s][:, j, :], top[s][:, j, TOPK - 1:TOPK], wk[s][:, j, :], ALU.is_ge, ALU.mult, accum_out=wsum[s][:, j:j + 1]).then_inc(w_cut, 1)
                    dve.wait_ge(w_cut, CT * (h + 1))
                    dve.reciprocal(wrec[s][:], wsum[s][:]).then_inc(w_rec, 1)
                h = chunk(it, k, AFTER_I)
                if h is not None:
                    s = (k - AFTER_I) % 2
                    dve.wait_ge(i_mm, h + 1)
                    dve.wait_ge(xt_in[s], 16 * (4 * it + (k - AFTER_I) // 2 + 1))
                    if not isinstance(h, int) or h >= 2:
                        dve.wait_ge(x1_out[s], 16 * (4 * it + (k - AFTER_I) // 2))
                    dve.tensor_tensor(xo[s][:].rearrange("p (a j) t -> p a (j t)", a=2), bu[:], xt[s][:].rearrange("p (a j) t -> p a (j t)", a=2), ALU.add).then_inc(x1_sum, 1)
            steps(dve, step, AFTER_I)
    nc.clear_and_free_semaphores(sems)
    nc.all_engine_barrier()


def split_weights_phase(nc, wT, loraT, w_split, lora_aug):
    D, O = wT.shape
    R = loraT.shape[0]
    KT, OT, NC = D // P, O // P, O // 512
    stack = ExitStack()
    sb = lambda name, shape, dt=FP32: stack.enter_context(nc.sbuf_tensor(name, shape, dt))
    sems = []

    def sem(name):
        sems.append(nc.alloc_semaphore(name))
        return sems[-1]
    with stack:
        w = [sb(f"w_f32_{i}", [P, OT, P]) for i in range(2)]
        hl = [sb(f"w_hl_{i}", [P, OT, 2, P], FP16) for i in range(2)]
        minus = sb("minus", [P, R + 1], FP16)
        aug = sb("aug_row", [R + 1, O])
        sums = stack.enter_context(nc.psum_tensor("w_sums", [R + 1, NC, 512], FP32))
        w_in = [sem(f"w0_in{i}") for i in range(2)]
        w_out = [sem(f"w0_out{i}") for i in range(2)]
        hi_ok, lo_ok, sums_mm, minus_set, b_in, row_ok, row_out = map(sem, (
            "w0_hi", "w0_lo", "w0_sums", "w0_minus", "w0_b_in", "w0_row", "w0_row_out"))
        block = stack.enter_context(nc.Block())

        def tiles(eng, step):
            step(0, 0, 0)
            step(1, 1, 0)
            with eng.Fori(1, KT // 2 - 1) as it:
                step(2 * it, 0, it)
                step(2 * it + 1, 1, it)
            step(KT - 2, 0, KT // 2 - 1)
            step(KT - 1, 1, KT // 2 - 1)

        @block.sync
        def _(sp):
            sp.dma_start(aug[0:R, :], loraT).then_inc(b_in, 16)

            def step(k, s, it):
                if not isinstance(k, int) or k >= 2:
                    sp.wait_ge(lo_ok, k - 1)
                sp.dma_start(w[s][:], wT[bass.ds(k * P, P), :].rearrange("p (o n) -> p o n", n=P)).then_inc(w_in[s], 16)
            tiles(sp, step)
            sp.wait_ge(row_ok, NC)
            sp.wait_ge(b_in, 16)
            sp.dma_start(lora_aug, aug[:]).then_inc(row_out, 16)
            sp.wait_ge(row_out, 16)

        @block.gpsimd
        def _(pool):
            pool.memset(minus[:], 0.0).then_inc(minus_set, 1)
            pool.wait_ge(minus_set, 1)
            pool.memset(minus[:, R:R + 1], -1.0).then_inc(minus_set, 1)

            def step(k, s, it):
                pool.wait_ge(lo_ok, k + 1)
                pool.dma_start(w_split[:, :, bass.ds(k, 1), :].rearrange("o p a n -> p o (a n)"), hl[s][:].rearrange("p o a n -> p o (a n)")).then_inc(w_out[s], 16)
            tiles(pool, step)
            for s in range(2):
                pool.wait_ge(w_out[s], 16 * (KT // 2))

        @block.scalar
        def _(act):
            def step(k, s, it):
                act.wait_ge(w_in[s], 16 * (it + 1))
                if not isinstance(k, int) or k >= 2:
                    act.wait_ge(w_out[s], 16 * it)
                    act.wait_ge(sums_mm, k - 1)
                act.activation(hl[s][:, :, 0, :], w[s][:], ACT.Copy, scale=W_SCALE).then_inc(hi_ok, 1)
            tiles(act, step)

        @block.vector
        def _(dve):
            def step(k, s, it):
                dve.wait_ge(hi_ok, k + 1)
                for o in range(0, OT, 8):
                    i = dve.scalar_tensor_tensor(hl[s][:, o:o + 8, 1, :], w[s][:, o:o + 8, :], W_SCALE, hl[s][:, o:o + 8, 0, :], ALU.mult, ALU.subtract)
                i.then_inc(lo_ok, 1)
            tiles(dve, step)
            for c in range(NC):
                dve.wait_ge(sums_mm, KT)
                dve.tensor_copy(aug[R:R + 1, c * 512:(c + 1) * 512], sums[R:R + 1, c, :]).then_inc(row_ok, 1)

        @block.tensor
        def _(pe):
            pe.wait_ge(minus_set, 2)

            def step(k, s, it):
                pe.wait_ge(lo_ok, k + 1)
                first, last = isinstance(k, int) and k == 0, isinstance(k, int) and k == KT - 1
                for c in range(NC):
                    for part in range(2):
                        mm = pe.matmul(sums[:, c, :], minus[:], hl[s][:, 4 * c:4 * c + 4, part, :], start=first and part == 0, stop=last and part == 1)
                mm.then_inc(sums_mm, 1)
            tiles(pe, step)
    nc.clear_and_free_semaphores(sems)
    nc.all_engine_barrier()


def ffn_phase(nc, x1, w_split, lora_aug, bias, gateT, gate_b, ctxT, ident_d, xn3, rows3, masks, feat, keep):
    NPAIR, _, KT, T = x1.shape
    L = T // 2
    D = KT * P
    OT = KT
    R = lora_aug.shape[0] - 1
    NG = gateT.shape[1] - R
    RANKS = (8, 16, 32, 64)
    QT = T // P
    LAG, RING = 3, 5
    WR = 2
    CR = 4
    NEG = -3.0e38

    stack = ExitStack()
    sb = lambda name, shape, dt=FP32: stack.enter_context(nc.sbuf_tensor(name, shape, dt))
    sems = []

    def sem(name):
        sems.append(nc.alloc_semaphore(name))
        return sems[-1]
    with stack:
        xr = [sb(f"xr{i}", [P, KT, T]) for i in range(2)]
        xh, xl = sb("xh", [P, KT, T], FP16), sb("xl", [P, KT, T], FP16)
        sq = sb("sq", [P, KT // 2, T])
        ws = [sb(f"ws{i}", [P, KT, 2, P], FP16) for i in range(WR)]
        mk = [sb(f"mk{i}", [P, KT, T], UINT8) for i in range(2)]
        ct = [sb(f"ct{i}", [P, T]) for i in range(CR)]
        wk = sb("wk2", [P, L])
        top = sb("top2", [P, 8])
        aug = sb("aug", [R + 1, OT * P])
        g32 = sb("g32", [P, KT, R + NG])
        gh, gl = sb("gh", [P, KT, R + NG], FP16), sb("gl", [P, KT, R + NG], FP16)
        gsum = sb("gsum", [1, R + NG])
        gb = sb("gb", [P, NG])
        bcol = sb("bcol", [P, OT])
        ident = sb("ident2", [P, P])
        ones = sb("ones", [P, P])
        minus1 = sb("minus1", [P, 1], FP16)
        eps = sb("eps2", [P, 2])
        red = sb("red", [P, 3, T])
        mean2, r2, msq = sb("mean2", [P, T]), sb("r2", [P, T]), sb("msq", [P, T])
        mean3, s3, r3 = sb("mean3", [P, T]), sb("s3", [P, T]), sb("r3", [P, T])
        ev = [sb(f"ev{i}", [P, T]) for i in range(2)]
        low = sb("low", [P, QT, R])
        rc, mx = sb("rc", [P, QT]), sb("mx", [P, QT])
        sc, nb = sb("sc", [P, QT, NG]), sb("nb", [P, QT, NG])
        arhs = sb("arhs", [R + 1, T])
        cf = [sb(f"cf{i}", [P, L]) for i in range(2)]
        sf = [sb(f"sf{i}", [P, L]) for i in range(2)]
        junk = sb("junk", [P, L])
        fp = sb("feat_pair", [P, 4, 2, KT])
        acc = [stack.enter_context(nc.psum_tensor(f"acc{i}", [P, T], FP32)) for i in range(RING)]
        ps_s, ps_q, ps_g = (stack.enter_context(nc.psum_tensor(n, [P, 512], FP32)) for n in ("ps_s", "ps_q", "ps_g"))
        raw = ps_g[:, 0:QT * (R + NG)].rearrange("p (q r) -> p q r", q=QT)
        rcol = ps_g[:, QT * (R + NG):QT * (R + NG) + QT]

        x_in = [sem(f"x1_in{i}") for i in range(2)]
        w_in = [sem(f"w_in{i}") for i in range(WR)]
        c_in = [sem(f"c_in{i}") for i in range(CR)]
        x_out = [sem(f"xn3_out{i}") for i in range(2)]
        m_out = [sem(f"mask_out{i}") for i in range(2)]
        (k_in, k_set, g_hi, g_lo, gsum_mm, gsum_ok, hi_ok, lo_ok, sum2_red, sq2, sq2_red, st2_mm, mean2_ok, msq2_ok, var2_ok,
         std2, r2_ok, g_mm, rcol_mm, rc_ok, sc_ok, low_ok, low_t, arhs_ok, arow_ok, main_mm, out_mm, ev_ok, x2_ok,
         sum3_red, sq3, sq3_red, st3_mm, mean3_ok, msq3_ok, var3_ok, std3, r3_ok, cent_ok, xn3_ok, cmax_ok, smax_ok, csum_ok, xsum_ok,
         top_ok, cut_ok, mask_ok, row_out, feat_ok) = map(sem, (
             "k2_in", "k2_set", "g_hi", "g_lo", "gsum_mm", "gsum_ok", "x_hi", "x_lo", "sum2_red", "sq2", "sq2_red", "st2_mm", "mean2_ok", "msq2_ok", "var2_ok",
             "std2", "r2_ok", "g_mm", "rcol_mm", "rc_ok", "sc_ok", "low_ok", "low_t", "arhs_ok", "arow_ok", "main_mm", "out_mm", "ev_ok", "x2_ok",
             "sum3_red", "sq3", "sq3_red", "st3_mm", "mean3_ok", "msq3_ok", "var3_ok", "std3", "r3_ok", "cent_ok", "xn3_ok", "cmax_ok", "smax_ok", "csum_ok", "xsum_ok",
             "top_ok", "cut_ok", "mask_ok", "row_out", "feat_ok"))
        block = stack.enter_context(nc.Block())
        SC_STEPS = 6

        def pairs(eng, pair, tail):
            pair(0, 0, 0)
            pair(1, 1, 0)
            if NPAIR > 2:
                with eng.Fori(1, NPAIR // 2) as it:
                    pair(2 * it, 0, it)
                    pair(2 * it + 1, 1, it)
            tail(NPAIR, 0)

        first = lambda i: isinstance(i, int) and i == 0
        ended = lambda i: isinstance(i, int) and i == NPAIR
        least = lambda i, n: not isinstance(i, int) or i >= n

        @block.sync
        def _(sp):
            sp.dma_start(g32[:], gateT.rearrange("(k p) r -> p k r", p=P)).then_inc(k_in, 16)
            sp.dma_start(gb[:], gate_b.partition_broadcast(P)).then_inc(k_in, 16)
            with nc.allow_non_contiguous_dma(reason="a column of biases per output tile, once"):
                sp.dma_start(bcol[:], bias.rearrange("(o p) -> p o", p=P)).then_inc(k_in, 16)
            sp.dma_start(ident[:], ident_d).then_inc(k_in, 16)
            sp.dma_start(aug[:], lora_aug).then_inc(k_in, 16)

            def pair(i, s, u):
                if least(i, 2):
                    n_ready = counted(sp, 16 * u)
                    sp.wait_ge(xsum_ok, 2 * KT * (i - 1))
                    sp.wait_ge(smax_ok, 2 * KT * (i - 1))
                    sp.wait_ge(k_in, 80)
                    sp.wait_ge(x_out[s], n_ready)
                sp.dma_start(xr[s][:], x1[bass.ds(i, 1), :, :, :].rearrange("a p k t -> p (a k) t")).then_inc(x_in[s], 16)
                for o in range(OT):
                    if o >= WR or not first(i):
                        sp.wait_ge(main_mm, OT * i + (o - WR + 1))
                    sp.dma_start(ws[o % WR][:], w_split[o, :, :, :].rearrange("p k (a n) -> p k a n", a=2)).then_inc(w_in[o % WR], 16)
            pairs(sp, pair, lambda i, s: None)

        @block.gpsimd
        def _(pool):
            pool.memset(ones[:], 1.0).then_inc(k_set, 1)
            pool.memset(minus1[:], -1.0).then_inc(k_set, 1)
            pool.memset(eps[:, 0:1], EPS).then_inc(k_set, 1)
            pool.memset(eps[:, 1:2], EPS * W_SCALE ** 2).then_inc(k_set, 1)

            def store_pair(i, s, u):
                n_ready = counted(pool, 2 * KT * i)
                pool.wait_ge(k_set, 4)
                pool.wait_ge(mask_ok, n_ready)
                pool.dma_start(masks[bass.ds(i - 1, 1), :, :, :].rearrange("a p k t -> p (a k) t"), mk[s][:]).then_inc(m_out[s], 16)
                n_ready = counted(pool, 4 * i)
                pool.wait_ge(k_set, 4)
                pool.wait_ge(xn3_ok, n_ready)
                pool.dma_start(xn3[bass.ds(i - 1, 1), :, :, :].rearrange("a p k t -> p (a k) t"), xr[s][:]).then_inc(x_out[s], 16)
                n_ready = counted(pool, i)
                pool.wait_ge(k_set, 4)
                pool.wait_ge(std3, n_ready)
                pool.dma_start(rows3[0:1, bass.ds(i - 1, 1), :].rearrange("r a t -> r (a t)"), mean3[0:1, :]).then_inc(row_out, 16)
                pool.dma_start(rows3[1:2, bass.ds(i - 1, 1), :].rearrange("r a t -> r (a t)"), s3[0:1, :]).then_inc(row_out, 16)

            def pair(i, s, u):
                for n in range(KT):
                    if n == 4 and not first(i):
                        store_pair(i, 1 - s, u)
                    if n >= CR or not first(i):
                        n_ready = counted(pool, 2 * (KT * i + n - CR + 1))
                        pool.wait_ge(k_set, 4)
                        pool.wait_ge(mask_ok, n_ready)
                    pool.dma_start(ct[n % CR][:], ctxT[bass.ds(i, 1), :, n, :].rearrange("a p t -> p (a t)")).then_inc(c_in[n % CR], 16)
            pairs(pool, pair, lambda i, s: store_pair(i, 1, None))
            for s in range(2):
                pool.wait_ge(x_out[s], 16 * (NPAIR // 2))
                pool.wait_ge(m_out[s], 16 * (NPAIR // 2))
            pool.wait_ge(row_out, 32 * NPAIR)

        @block.tensor
        def _(pe):
            pe.wait_ge(k_in, 80)
            pe.wait_ge(k_set, 4)
            pe.wait_ge(g_lo, 1)
            for part, g in enumerate((gh, gl)):
                for k in range(KT):
                    mm = pe.matmul(ps_g[0:1, 0:R + NG], minus1[:], g[:, k, :], start=part == 0 and k == 0, stop=part == 1 and k == KT - 1)
            mm.then_inc(gsum_mm, 1)

            def main(i, o):
                b, n = o % RING, OT * i + o
                pe.wait_ge(w_in[o % WR], 16 * (OT // WR) * i + 16 * (o // WR + 1))
                if o >= RING:
                    pe.wait_ge(ev_ok, OT * i + o - RING + 1)
                elif not first(i):
                    pe.wait_ge(ev_ok, OT * i)
                for k in range(KT):
                    if o == 0 and k % 4 == 0:
                        pe.wait_ge(lo_ok, 4 * i + k // 4 + 1)
                    for a, x in ((0, xh), (1, xh), (0, xl)):
                        mm = pe.matmul(acc[b][:], ws[o % WR][:, k, a, :], x[:, k, :], start=k == 0 and a == 0 and x is xh, stop=False)
                mm.then_inc(main_mm, 1)

            def correct(i, o):
                if o == 0:
                    pe.wait_ge(arhs_ok, i + 1)
                    pe.wait_ge(arow_ok, i + 1)
                pe.matmul(acc[o % RING][:], aug[:, o * P:(o + 1) * P], arhs[:], start=False, stop=True).then_inc(out_mm, 1)

            def stats(sum_red, sq_red, done, i):
                pe.wait_ge(sum_red, i + 1)
                pe.matmul(ps_s[:], ones[:], red[:, 0, :], start=True, stop=True)
                pe.wait_ge(sq_red, 2 * i + 2)
                pe.matmul(ps_q[:], ones[:], red[:, 1, :], start=True, stop=False)
                pe.matmul(ps_q[:], ones[:], red[:, 2, :], start=False, stop=True).then_inc(done, 1)

            def pair(i, s, u):
                main(i, 0)
                main(i, 1)
                if least(i, 2):
                    pe.wait_ge(var3_ok, i - 1)
                    pe.wait_ge(mean3_ok, i - 1)
                elif i == 1:
                    pe.wait_ge(arhs_ok, 1)
                stats(sum2_red, sq2_red, st2_mm, i)
                main(i, 2)
                pe.wait_ge(mean2_ok, i + 1)
                pe.wait_ge(gsum_ok, 1)
                if not first(i):
                    pe.wait_ge(low_ok, 4 * i)
                for q in range(QT):
                    t = slice(q * P, (q + 1) * P)
                    for k in range(KT):
                        for x, g in ((xh, gh), (xh, gl), (xl, gh)):
                            pe.matmul(raw[:, q, :], x[:, k, t], g[:, k, :], start=k == 0 and x is xh and g is gh, stop=False)
                    mm = pe.matmul(raw[:, q, :], mean2[0:1, t], gsum[:], start=False, stop=True)
                mm.then_inc(g_mm, 1)
                pe.wait_ge(r2_ok, i + 1)
                for q in range(QT):
                    mm = pe.matmul(rcol[:, q:q + 1], r2[0:1, q * P:(q + 1) * P], ones[0:1, 0:1], start=True, stop=True)
                mm.then_inc(rcol_mm, 1)
                main(i, 3)
                pe.wait_ge(var2_ok, i + 1)
                n_ready = counted(pe, 4 * (i + 1))
                pe.wait_ge(k_set, 4)
                pe.wait_ge(low_ok, n_ready)
                for q in range(QT):
                    mm = pe.transpose(ps_s[0:R, q * P:(q + 1) * P], low[:, q, :], ident[:])
                mm.then_inc(low_t, 1)
                if not first(i):
                    pe.wait_ge(arhs_ok, i + 1)
                    stats(sum3_red, sq3_red, st3_mm, i - 1)
                for o in range(LAG + 1, OT):
                    correct(i, o - LAG - 1)
                    main(i, o)
                for o in range(OT - LAG - 1, OT):
                    correct(i, o)

            def tail(i, s):
                pe.wait_ge(var3_ok, i - 1)
                stats(sum3_red, sq3_red, st3_mm, i - 1)
            pairs(pe, pair, tail)

        @block.scalar
        def _(act):
            act.wait_ge(k_in, 80)
            act.wait_ge(k_set, 4)
            act.activation(gh[:], g32[:], ACT.Copy, scale=W_SCALE).then_inc(g_hi, 1)
            act.wait_ge(gsum_mm, 1)
            act.activation(gsum[:], ps_g[0:1, 0:R + NG], ACT.Copy).then_inc(gsum_ok, 1)

            def square(i, half, src, done):
                act.activation(sq[:], src[:, half * KT // 2:(half + 1) * KT // 2, :], ACT.Square).then_inc(done, 1)

            def layer3(i, s):
                act.wait_ge(x2_ok, OT * i)
                act.wait_ge(sq2_red, 2 * NPAIR if ended(i) else 2 * i + 2)
                square(i, 0, xr[s], sq3)
                act.wait_ge(sq3_red, 2 * i - 1)
                square(i, 1, xr[s], sq3)
                act.wait_ge(var3_ok, i)
                if least(i, 2):
                    act.wait_ge(row_out, 32 * (i - 1))
                act.activation(s3[:], r3[:], ACT.Sqrt, bias=eps[:, 0:1]).then_inc(std3, 1)

            def sums3(i, s):
                for n in range(2 * KT):
                    act.wait_ge(cmax_ok, 2 * KT * (i - 1) + n + 1)
                    act.activation(junk[:], cf[n % 2][:], ACT.Copy, accum_out=fp[:, 1, n % 2, n // 2:n // 2 + 1]).then_inc(csum_ok, 1)
                    act.wait_ge(csum_ok, 2 * KT * (i - 1) + n + 1)
                    act.activation(junk[:], xr[s][:, n // 2, (n % 2) * L:(n % 2 + 1) * L], ACT.Copy, accum_out=fp[:, 3, n % 2, n // 2:n // 2 + 1]).then_inc(xsum_ok, 1)
                    act.wait_ge(xsum_ok, 2 * KT * (i - 1) + n + 1)
                act.wait_ge(smax_ok, 2 * KT * i)
                act.activation(feat[:, :, bass.ds(2 * (i - 1), 2), :], fp[:], ACT.Copy).then_inc(feat_ok, 1)

            def pair(i, s, u):
                act.wait_ge(x_in[s], 16 * (u + 1))
                if not first(i):
                    act.wait_ge(main_mm, OT * i)
                for c in range(4):
                    k = slice(c * KT // 4, (c + 1) * KT // 4)
                    act.activation(xh[:, k, :], xr[s][:, k, :], ACT.Copy).then_inc(hi_ok, 1)
                if least(i, 2):
                    act.wait_ge(sq3_red, 2 * (i - 1))
                elif i == 1:
                    act.wait_ge(sq2_red, 2)
                square(i, 0, xr[s], sq2)
                act.wait_ge(sq2_red, 2 * i + 1)
                square(i, 1, xr[s], sq2)
                act.wait_ge(var2_ok, i + 1)
                act.activation(msq[:], r2[:], ACT.Sqrt, bias=eps[:, 1:2], scale=W_SCALE ** 2).then_inc(std2, 1)
                act.wait_ge(low_t, i + 1)
                if not first(i):
                    act.wait_ge(out_mm, OT * i)
                act.activation(arhs[0:R, :], ps_s[0:R, :], ACT.Copy).then_inc(arhs_ok, 1)
                if not first(i):
                    layer3(i, 1 - s)
                    sums3(i, 1 - s)

            def tail(i, s):
                layer3(i, 1 - s)
                sums3(i, 1 - s)
                act.wait_ge(feat_ok, NPAIR)
            pairs(act, pair, tail)

        @block.vector
        def _(dve):
            dve.wait_ge(k_in, 80)
            dve.wait_ge(g_hi, 1)
            dve.scalar_tensor_tensor(gl[:], g32[:], W_SCALE, gh[:], ALU.mult, ALU.subtract).then_inc(g_lo, 1)

            def reduce_tiles(out, src):
                return dve.tensor_reduce(out, src.rearrange("p k t -> p t k"), AX.X, ALU.add)

            def variance(mean, var, st, mean_ok, msq_ok, var_ok, i):
                dve.wait_ge(st, i + 1)
                dve.tensor_scalar(mean[:], ps_s[:], 1.0 / D, None, ALU.mult).then_inc(mean_ok, 1)
                dve.wait_ge(mean_ok, i + 1)
                dve.tensor_tensor(msq[:], mean[:], mean[:], ALU.mult).then_inc(msq_ok, 1)
                dve.wait_ge(msq_ok, i + 1)
                dve.scalar_tensor_tensor(var[:], ps_q[:], 1.0 / D, msq[:], ALU.mult, ALU.subtract).then_inc(var_ok, 1)

            def gates(i):
                dve.wait_ge(rcol_mm, i + 1)
                dve.tensor_copy(rc[:], rcol).then_inc(rc_ok, 1)
                dve.wait_ge(rc_ok, i + 1)
                n = SC_STEPS * i
                dve.tensor_tensor(sc[:], raw[:, :, R:R + NG], rc[:].unsqueeze(2).broadcast_to([P, QT, NG]), ALU.mult).then_inc(sc_ok, 1)
                dve.wait_ge(sc_ok, n + 1)
                dve.tensor_tensor(sc[:], sc[:], gb[:].unsqueeze(1).broadcast_to([P, QT, NG]), ALU.add).then_inc(sc_ok, 1)
                dve.wait_ge(sc_ok, n + 2)
                dve.tensor_reduce(mx[:], sc[:], AX.X, ALU.max).then_inc(sc_ok, 1)
                dve.wait_ge(sc_ok, n + 3)
                dve.tensor_tensor(nb[:], sc[:], mx[:].unsqueeze(2).broadcast_to([P, QT, NG]), ALU.is_lt).then_inc(sc_ok, 1)
                dve.wait_ge(sc_ok, n + 4)
                for r in (1, 2):
                    dve.tensor_tensor(nb[:, :, r], nb[:, :, r], nb[:, :, r - 1], ALU.mult).then_inc(sc_ok, 1)
                    dve.wait_ge(sc_ok, n + 4 + r)
                if not first(i):
                    dve.wait_ge(low_t, i)
                dve.tensor_copy(low[:, :, 0:RANKS[0]], raw[:, :, 0:RANKS[0]]).then_inc(low_ok, 1)
                for r in range(3):
                    w = RANKS[r + 1] - RANKS[r]
                    dve.tensor_tensor(low[:, :, RANKS[r]:RANKS[r + 1]], raw[:, :, RANKS[r]:RANKS[r + 1]], nb[:, :, r:r + 1].broadcast_to([P, QT, w]), ALU.mult).then_inc(low_ok, 1)

            def topk(i, n, s):
                for bb in range(2):
                    at = 2 * KT * i + 2 * n + bb
                    t = slice(bb * L, (bb + 1) * L)
                    full, rest = keep // 8, keep % 8
                    rounds = full + (rest > 0)
                    src = ct[n % CR][:, t]
                    for r in range(rounds):
                        dve.max(top[:], src).then_inc(top_ok, 1)
                        n_ready = counted(dve, rounds * at + r + 1)
                        dve.wait_ge(k_in, 80)
                        dve.wait_ge(top_ok, n_ready)
                        if r == full:
                            dve.memset(top[:, rest:8], NEG).then_inc(cut_ok, 1)
                            n_ready = counted(dve, (rounds + 1) * at + r + 1)
                            dve.wait_ge(k_in, 80)
                            dve.wait_ge(cut_ok, n_ready)
                        dve.match_replace(wk[:], top[:], src, NEG).then_inc(cut_ok, 1)
                        n_ready = counted(dve, (rounds + 1) * at + r + 1 + (r == full))
                        dve.wait_ge(k_in, 80)
                        dve.wait_ge(cut_ok, n_ready)
                        src = wk[:]
                    dve.tensor_scalar(mk[s][:, n, t], wk[:], NEG, None, ALU.is_le).then_inc(mask_ok, 1)

            def layer3(i, s):
                j = i - 1
                dve.wait_ge(st2_mm, NPAIR if ended(i) else i + 1)
                dve.wait_ge(x2_ok, OT * i)
                reduce_tiles(red[:, 0, :], xr[s][:]).then_inc(sum3_red, 1)
                for half in range(2):
                    dve.wait_ge(sq3, 2 * j + half + 1)
                    reduce_tiles(red[:, 1 + half, :], sq[:]).then_inc(sq3_red, 1)
                if least(i, 2):
                    dve.wait_ge(row_out, 32 * j)
                dve.wait_ge(std2, NPAIR if ended(i) else i + 1)
                dve.wait_ge(r2_ok, NPAIR if ended(i) else i + 1)
                variance(mean3, r3, st3_mm, mean3_ok, msq3_ok, var3_ok, j)
                dve.wait_ge(std3, i)
                dve.reciprocal(r3[:], s3[:]).then_inc(r3_ok, 1)
                dve.wait_ge(r3_ok, i)
                bc = lambda m: m[:].unsqueeze(1).broadcast_to([P, KT // 4, T])
                for c in range(4):
                    v = xr[s][:, c * KT // 4:(c + 1) * KT // 4, :]
                    dve.tensor_tensor(v, v, bc(mean3), ALU.subtract).then_inc(cent_ok, 1)
                for c in range(4):
                    v = xr[s][:, c * KT // 4:(c + 1) * KT // 4, :]
                    dve.wait_ge(cent_ok, 4 * j + c + 1)
                    dve.tensor_tensor(v, v, bc(r3), ALU.mult).then_inc(xn3_ok, 1)

            def features(i, s, n):
                j = i - 1
                at = 2 * KT * j + n
                n_ready = counted(dve, at - 1)
                n_done = counted(dve, at + 1)
                n_tiles, n_masks, n_pairs = counted(dve, 4 * i), counted(dve, 2 * KT * i), counted(dve, j)
                dve.wait_ge(k_in, 80)
                if n == 0 and least(i, 2):
                    dve.wait_ge(feat_ok, n_pairs)
                if n < 2:
                    dve.wait_ge(xn3_ok, n_tiles)
                    dve.wait_ge(mask_ok, n_masks)
                if n >= 2 or least(i, 2):
                    dve.wait_ge(csum_ok, n_ready)
                    dve.wait_ge(smax_ok, n_ready)
                t = slice((n % 2) * L, (n % 2 + 1) * L)
                c, f = cf[n % 2][:], xr[s][:, n // 2, t]
                dve.tensor_tensor_reduce(out=c, in0=mk[s][:, n // 2, t], in1=f, scale=1.0, scalar=NEG, op0=ALU.mult, op1=ALU.max,
                                         accum_out=fp[:, 0, n % 2, n // 2:n // 2 + 1]).then_inc(cmax_ok, 1)
                dve.wait_ge(k_in, 80)
                dve.wait_ge(cmax_ok, n_done)
                dve.tensor_tensor_reduce(out=sf[n % 2][:], in0=f, in1=c, scale=1.0, scalar=NEG, op0=ALU.subtract, op1=ALU.max,
                                         accum_out=fp[:, 2, n % 2, n // 2:n // 2 + 1]).then_inc(smax_ok, 1)

            def pair(i, s, u):
                for c in range(4):
                    k = slice(c * KT // 4, (c + 1) * KT // 4)
                    dve.wait_ge(hi_ok, 4 * i + c + 1)
                    dve.tensor_tensor(xl[:, k, :], xr[s][:, k, :], xh[:, k, :], ALU.subtract).then_inc(lo_ok, 1)
                if least(i, 2):
                    dve.wait_ge(st3_mm, i - 1)
                elif i == 1:
                    dve.wait_ge(st2_mm, 1)
                reduce_tiles(red[:, 0, :], xr[s][:]).then_inc(sum2_red, 1)
                for half in range(2):
                    dve.wait_ge(sq2, 2 * i + half + 1)
                    reduce_tiles(red[:, 1 + half, :], sq[:]).then_inc(sq2_red, 1)
                if not first(i):
                    dve.wait_ge(g_mm, i)
                    dve.wait_ge(arow_ok, i)
                    dve.wait_ge(ev_ok, OT * i)
                variance(mean2, r2, st2_mm, mean2_ok, msq2_ok, var2_ok, i)
                dve.wait_ge(std2, i + 1)
                dve.reciprocal(r2[:], msq[:]).then_inc(r2_ok, 1)
                if not first(i):
                    dve.wait_ge(out_mm, OT * i)
                dve.tensor_copy(arhs[R:R + 1, :], mean2[R:R + 1, :]).then_inc(arow_ok, 1)
                dve.wait_ge(r2_ok, i + 1)
                gates(i)
                if not first(i):
                    layer3(i, 1 - s)
                for o in range(OT):
                    if not first(i):
                        for n in range(2):
                            features(i, 1 - s, 2 * o + n)
                    at = OT * i + o
                    dve.wait_ge(out_mm, at + 1)
                    if o >= 2 or not first(i):
                        dve.wait_ge(x2_ok, at - 1)
                    dve.tensor_tensor(ev[o % 2][:], acc[o % RING][:], r2[:], ALU.mult).then_inc(ev_ok, 1)
                    dve.wait_ge(ev_ok, at + 1)
                    dve.scalar_tensor_tensor(xr[s][:, o, :], ev[o % 2][:], bcol[:, o:o + 1], xr[s][:, o, :], ALU.add, ALU.add).then_inc(x2_ok, 1)
                    n_ready = counted(dve, 16 * (KT // CR) * i + 16 * (o // CR + 1))
                    n_stored, n_used = counted(dve, 16 * u), counted(dve, 2 * KT * (i - 1))
                    dve.wait_ge(k_in, 80)
                    if o == 0 and least(i, 2):
                        dve.wait_ge(m_out[s], n_stored)
                        dve.wait_ge(smax_ok, n_used)
                    dve.wait_ge(c_in[o % CR], n_ready)
                    topk(i, o, s)

            def tail(i, s):
                layer3(i, 1 - s)
                for n in range(2 * KT):
                    features(i, 1 - s, n)
            pairs(dve, pair, tail)
    nc.clear_and_free_semaphores(sems)
    nc.all_engine_barrier()


def channel_gates_phase(nc, feat, conv_w, gamma, beta, shift_d, ident_d, att, keep, L):
    _, _, NB, J = feat.shape
    G = J // 2
    W = 2 * P
    N = NB * G * W
    TAPS = 7
    PAD = TAPS // 2
    assert NB * G == P
    stack = ExitStack()
    sb = lambda name, shape, dt=FP32: stack.enter_context(nc.sbuf_tensor(name, shape, dt))
    sem = lambda name: stack.enter_context(nc.semaphore(name))
    with stack:
        fy = sb("fy", [P, 4, 2, NB, G])
        y = sb("y_pad", [P, 4, W + 2 * PAD])
        z = sb("z_conv", [P, 2, W])
        zz = sb("z_square", [P, W])
        zs, mu, var, rs = sb("z_sum", [P, 2]), sb("z_mu", [P, 2]), sb("z_var", [P, 2]), sb("z_rs", [P, 2])
        cw, gm, bt = sb("cw", [P, 2 * TAPS]), sb("bn_g", [P, 1]), sb("bn_b", [P, 1])
        shift = sb("shift", [P, 2, P])
        ident, ones, eps = sb("ident_b", [P, P]), sb("ones_b", [P, P]), sb("eps_b", [P, 1])
        yt = stack.enter_context(nc.psum_tensor("yt", [P, 4, W], FP32))
        halo = stack.enter_context(nc.psum_tensor("halo", [P, 2, 4, PAD], FP32))
        tot = stack.enter_context(nc.psum_tensor("tot", [P, 4], FP32))
        back = stack.enter_context(nc.psum_tensor("back", [P, 2, 2, P], FP32))
        (k_in, k_set, fy_ok, y_mm, y_ok, halo_mm, halo_ok, tap_ok, sum_ok, mu_mm, mu_ok, cen_ok, sq_ok, var_mm, std_ok,
         rs_ok, sc_ok, bn_ok, sig_ok, back_mm, a2_ok, att_ok) = map(sem, (
             "kb_in", "kb_set", "fy_ok", "y_mm", "y_ok", "halo_mm", "halo_ok", "tap_ok", "z_sum_ok", "mu_mm", "mu_ok", "cen_ok", "zsq_ok", "zvar_mm", "zstd_ok",
             "zrs_ok", "zsc_ok", "bn_ok", "sig_ok", "back_mm", "a2_ok", "att_ok"))
        block = stack.enter_context(nc.Block())

        @block.sync
        def _(sp):
            sp.dma_start(cw[:], conv_w.rearrange("a c k -> (a c k)").partition_broadcast(P)).then_inc(k_in, 16)
            sp.dma_start(gm[:], gamma.partition_broadcast(P)).then_inc(k_in, 16)
            sp.dma_start(bt[:], beta.partition_broadcast(P)).then_inc(k_in, 16)
            sp.dma_start(shift[:], shift_d).then_inc(k_in, 16)
            sp.dma_start(ident[:], ident_d).then_inc(k_in, 16)

        @block.gpsimd
        def _(pool):
            pool.memset(ones[:], 1.0).then_inc(k_set, 1)
            pool.memset(eps[:], EPS).then_inc(k_set, 1)

        @block.tensor
        def _(pe):
            pe.wait_ge(k_in, 80)
            pe.wait_ge(k_set, 2)
            for q in range(4):
                pe.wait_ge(fy_ok, 5)
                for h in range(2):
                    mm = pe.transpose(yt[:, q, h * P:(h + 1) * P], fy[:, q, h, :, :].rearrange("p b g -> p (b g)"), ident[:])
            mm.then_inc(y_mm, 1)
            pe.wait_ge(y_ok, 1)
            pe.matmul(halo[:, 0, :, :], shift[:, 0, :], y[:, :, W:W + PAD], start=True, stop=True)
            pe.matmul(halo[:, 1, :, :], shift[:, 1, :], y[:, :, PAD:2 * PAD], start=True, stop=True).then_inc(halo_mm, 1)
            pe.wait_ge(sum_ok, 1)
            pe.matmul(tot[:, 0:2], ones[:], zs[:], start=True, stop=True).then_inc(mu_mm, 1)
            pe.wait_ge(sq_ok, 2)
            pe.matmul(tot[:, 2:4], ones[:], var[:], start=True, stop=True).then_inc(var_mm, 1)
            pe.wait_ge(sig_ok, 1)
            for c in range(2):
                for h in range(2):
                    mm = pe.transpose(back[:, c, h, :], z[:, c, h * P:(h + 1) * P], ident[:])
            mm.then_inc(back_mm, 1)

        @block.scalar
        def _(act):
            act.wait_ge(k_set, 2)
            act.wait_ge(y_mm, 1)
            act.activation(y[:, :, PAD:PAD + W], yt[:], ACT.Copy).then_inc(y_ok, 1)
            for c in range(2):
                act.wait_ge(cen_ok, c + 1)
                if c:
                    act.wait_ge(sq_ok, c)
                act.activation(zz[:], z[:, c, :], ACT.Square, accum_out=var[:, c:c + 1]).then_inc(sq_ok, 1)
            act.wait_ge(var_mm, 1)
            act.activation(rs[:], tot[:, 2:4], ACT.Sqrt, bias=eps[:], scale=1.0 / N).then_inc(std_ok, 1)
            act.wait_ge(bn_ok, 4)
            act.activation(z[:], z[:], ACT.Sigmoid).then_inc(sig_ok, 1)

        @block.vector
        def _(dve):
            dve.wait_ge(k_in, 80)
            split = lambda q: feat[:, q, :, :].rearrange("p b (g h) -> p h b g", h=2)
            dve.tensor_copy(fy[:, 0, :, :, :], split(0)).then_inc(fy_ok, 1)
            dve.tensor_scalar(fy[:, 1, :, :, :], split(1), 1.0 / keep, None, ALU.mult).then_inc(fy_ok, 1)
            dve.tensor_copy(fy[:, 2, :, :, :], split(2)).then_inc(fy_ok, 1)
            dve.tensor_tensor(fy[:, 3, :, :, :], split(3), split(1), ALU.subtract).then_inc(fy_ok, 1)
            dve.wait_ge(fy_ok, 4)
            dve.tensor_scalar(fy[:, 3, :, :, :], fy[:, 3, :, :, :], 1.0 / (L - keep), None, ALU.mult).then_inc(fy_ok, 1)
            dve.wait_ge(halo_mm, 1)
            dve.tensor_copy(y[:, :, 0:PAD], halo[:, 0, :, :]).then_inc(halo_ok, 1)
            dve.tensor_copy(y[:, :, PAD + W:], halo[:, 1, :, :]).then_inc(halo_ok, 1)
            dve.wait_ge(halo_ok, 2)
            for tap in range(2 * TAPS):
                ch, k = tap // TAPS, tap % TAPS
                for c in range(2):
                    src, w = y[:, 2 * c + ch, k:k + W], cw[:, tap:tap + 1]
                    if tap == 0:
                        dve.tensor_scalar(z[:, c, :], src, w, None, ALU.mult).then_inc(tap_ok, 1)
                    else:
                        dve.wait_ge(tap_ok, 2 * (tap - 1) + c + 1)
                        dve.scalar_tensor_tensor(z[:, c, :], src, w, z[:, c, :], ALU.mult, ALU.add).then_inc(tap_ok, 1)
            dve.wait_ge(tap_ok, 4 * TAPS)
            dve.tensor_reduce(zs[:], z[:], AX.X, ALU.add).then_inc(sum_ok, 1)
            dve.wait_ge(mu_mm, 1)
            dve.tensor_scalar(mu[:], tot[:, 0:2], 1.0 / N, None, ALU.mult).then_inc(mu_ok, 1)
            dve.wait_ge(mu_ok, 1)
            for c in range(2):
                dve.tensor_scalar(z[:, c, :], z[:, c, :], mu[:, c:c + 1], None, ALU.subtract).then_inc(cen_ok, 1)
            dve.wait_ge(std_ok, 1)
            dve.reciprocal(rs[:], rs[:]).then_inc(rs_ok, 1)
            dve.wait_ge(rs_ok, 1)
            dve.tensor_scalar(rs[:], rs[:], gm[:], None, ALU.mult).then_inc(sc_ok, 1)
            dve.wait_ge(sc_ok, 1)
            dve.wait_ge(sq_ok, 2)
            for c in range(2):
                dve.tensor_scalar(z[:, c, :], z[:, c, :], rs[:, c:c + 1], bt[:], ALU.mult, ALU.add).then_inc(bn_ok, 1)
            for c in range(2):
                dve.wait_ge(bn_ok, c + 1)
                dve.tensor_scalar(z[:, c, :], z[:, c, :], 0.0, None, ALU.max).then_inc(bn_ok, 1)
            dve.wait_ge(back_mm, 1)
            dve.tensor_copy(att[:, 1, :, :, :].rearrange("p h b g -> p h (b g)"), back[:, 1, :, :]).then_inc(a2_ok, 1)
            dve.wait_ge(a2_ok, 1)
            dve.tensor_tensor(att[:, 0, :, :, :].rearrange("p h b g -> p h (b g)"), back[:, 0, :, :], att[:, 1, :, :, :].rearrange("p h b g -> p h (b g)"), ALU.subtract).then_inc(att_ok, 1)
            dve.wait_ge(att_ok, 1)


def experts_phase(nc, xn3, rows3, masks, att, routerT, router_b, expert_b, tail_rows, ident_d, out):
    NPAIR, _, KT, T = xn3.shape
    L = T // 2
    D = KT * P
    QT = T // P
    E = routerT.shape[1]
    A = E + 2
    NCH = 4
    CK = KT // NCH
    TOP = 8
    RING = 4
    STEPS = 14 + 2 * QT

    stack = ExitStack()
    sb = lambda name, shape, dt=FP32: stack.enter_context(nc.sbuf_tensor(name, shape, dt))
    pb = lambda name, shape: stack.enter_context(nc.psum_tensor(name, shape, FP32))
    sem = lambda name: stack.enter_context(nc.semaphore(name))
    with stack:
        xr = [sb(f"x3_{i}", [P, KT, T]) for i in range(2)]
        mk = [sb(f"mk3_{i}", [P, KT, T], UINT8) for i in range(2)]
        m3 = [sb(f"m3_{i}", [P, T]) for i in range(2)]
        s3 = [sb(f"s3_{i}", [P, T]) for i in range(2)]
        gc = [sb(f"gc{i}", [P, CK, T]) for i in range(2)]
        sq = [sb(f"sq3_{i}", [P, CK, T]) for i in range(2)]
        ost = [sb(f"ost{i}", [P, CK, T]) for i in range(2)]
        rt = sb("rt", [P, KT, A])
        rsq = sb("rsq", [P, A])
        eb = sb("eb", [A, D])
        pick = sb("pick", [A, P])
        rb, rsum = sb("rb", [P, E]), sb("rsum", [P, E])
        ident, ones, eps = sb("ident3", [P, P]), sb("ones3", [P, P]), sb("eps3", [P, 1])
        lgs, wds = sb("lgs", [A, T]), sb("wds", [A, T])
        a1 = sb("a1", [P, T])
        mean, msq, r4 = sb("mean4", [P, QT]), sb("msq4", [P, QT]), sb("r4", [P, QT])
        mx, ws, rw = sb("mx4", [P, QT]), sb("ws4", [P, QT]), sb("rw4", [P, QT])
        lt, sc, lm = sb("lt", [P, QT, E]), sb("sc4", [P, QT, E]), sb("lm", [P, QT, E])
        top = sb("top4", [P, QT, TOP])
        wd = sb("wd", [P, QT, A])
        lg, tr, wt, ab = pb("lg", [P, 512]), pb("tr", [P, 512]), pb("wt3", [P, 512]), pb("ab", [P, 512])
        po = [pb(f"po{i}", [P, T]) for i in range(RING)]
        raw = tr[:, 0:QT * A].rearrange("p (q e) -> p q e", q=QT)

        x_in = [[sem(f"x3_in{i}_{c}") for c in range(NCH)] for i in range(2)]
        mk_in, row_in = [sem(f"mk3_in{i}") for i in range(2)], [sem(f"rows_in{i}") for i in range(2)]
        stored = [sem(f"out_stored{i}") for i in range(2)]
        (k_in, k_set, rsum_mm, rsum_ok, g_ok, u_ok, v_ok, x3_ok, sq_ok, x_mm, lg_mm, lg_ok, tr_mm, step_ok, var_ok, std_ok, arg_ok, exp_ok, wd_ok,
         wt_mm, wds_ok, ab_mm, a1_ok, prod_ok, bias_mm, out_ok) = map(sem, (
             "k3_in", "k3_set", "rsum_mm", "rsum_ok", "g3_ok", "u3_ok", "v3_ok", "x3_ok", "sq3_ok", "x3_mm", "lg_mm", "lg_ok", "tr_mm", "step_ok", "var4_ok", "std4_ok", "arg_ok", "exp_ok", "wd_ok",
             "wt3_mm", "wds_ok", "ab_mm", "a1_ok", "prod_ok", "bias_mm", "out_ok"))
        block = stack.enter_context(nc.Block())

        def pairs(eng, pair, tail):
            pair(0, 0, 0)
            pair(1, 1, 0)
            if NPAIR > 2:
                with eng.Fori(1, NPAIR // 2) as it:
                    pair(2 * it, 0, it)
                    pair(2 * it + 1, 1, it)
            tail()

        least = lambda i, n: not isinstance(i, int) or i >= n

        @block.sync
        def _(sp):
            sp.dma_start(rt[:, :, 0:E], routerT.rearrange("(k p) e -> p k e", p=P)).then_inc(k_in, 16)
            sp.dma_start(rb[:], router_b.partition_broadcast(P)).then_inc(k_in, 16)
            sp.dma_start(eb[0:E, :], expert_b).then_inc(k_in, 16)
            sp.dma_start(eb[E:A, :], tail_rows[:, 0:D]).then_inc(k_in, 16)
            sp.dma_start(pick[E:A, :], tail_rows[:, D:D + P]).then_inc(k_in, 16)
            sp.dma_start(ident[:], ident_d).then_inc(k_in, 16)

            def store(i, u, c):
                sp.dma_start(out[bass.ds(i, 1), :, c * CK:(c + 1) * CK, :].rearrange("a p k t -> p (a k) t"), ost[c % 2][:]).then_inc(stored[c % 2], 16)

            def pair(i, s, u):
                if least(i, 2):
                    n_ready = counted(sp, NCH * (i - 1))
                    sp.wait_ge(k_in, 96)
                    sp.wait_ge(x3_ok, n_ready)
                sp.dma_start(mk[s][:], masks[bass.ds(i, 1), :, :, :].rearrange("a p k t -> p (a k) t")).then_inc(mk_in[s], 16)
                sp.dma_start(s3[s][:], rows3[1:2, bass.ds(i, 1), :].rearrange("r a t -> (r a t)").partition_broadcast(P)).then_inc(row_in[s], 16)
                sp.dma_start(m3[s][:], rows3[0:1, bass.ds(i, 1), :].rearrange("r a t -> (r a t)").partition_broadcast(P)).then_inc(row_in[s], 16)
                for c in range(NCH):
                    k = slice(c * CK, (c + 1) * CK)
                    if least(i, 2):
                        n_ready = counted(sp, KT * (i - 2) + CK * (c + 1))
                        sp.wait_ge(k_in, 96)
                        sp.wait_ge(out_ok, n_ready)
                    sp.dma_start(xr[s][:, k, :], xn3[bass.ds(i, 1), :, k, :].rearrange("a p k t -> p (a k) t")).then_inc(x_in[s][c], 16)
                    if least(i, 2):
                        store(i - 2, u, c)

            def tail():
                for i in (NPAIR - 2, NPAIR - 1):
                    for c in range(NCH):
                        sp.wait_ge(out_ok, KT * i + CK * (c + 1))
                        store(i, None, c)
                for s in range(2):
                    sp.wait_ge(stored[s], 16 * NPAIR * NCH // 2)
            pairs(sp, pair, tail)

        @block.gpsimd
        def _(pool):
            pool.memset(ones[:], 1.0).then_inc(k_set, 1)
            pool.memset(eps[:], EPS).then_inc(k_set, 1)
            pool.memset(rt[:, :, E:E + 1], 1.0).then_inc(k_set, 1)
            pool.memset(rt[:, :, E + 1:A], 0.0).then_inc(k_set, 1)
            pool.memset(rsq[:, 0:E + 1], 0.0).then_inc(k_set, 1)
            pool.memset(rsq[:, E + 1:A], 1.0).then_inc(k_set, 1)
            pool.memset(pick[0:E, :], 0.0).then_inc(k_set, 1)

            def products(i, s):
                pool.wait_ge(a1_ok, i)
                for k in range(KT):
                    pool.tensor_tensor(xr[s][:, k, :], xr[s][:, k, :], a1[:], ALU.mult).then_inc(prod_ok, 1)

            def pair(i, s, u):
                pool.wait_ge(row_in[s], 32 * (u + 1))
                for c in range(NCH):
                    pool.wait_ge(g_ok, NCH * i + c + 1)
                    pool.tensor_tensor(gc[c % 2][:], gc[c % 2][:], s3[s][:].unsqueeze(1).broadcast_to([P, CK, T]), ALU.add).then_inc(u_ok, 1)
                if least(i, 1):
                    products(i, 1 - s)
            pairs(pool, pair, lambda: products(NPAIR, 1))

        @block.tensor
        def _(pe):
            pe.wait_ge(k_in, 96)
            pe.wait_ge(k_set, 7)
            for k in range(KT):
                mm = pe.matmul(tr[:, 0:E], ones[:], rt[:, k, 0:E], start=k == 0, stop=k == KT - 1)
            mm.then_inc(rsum_mm, 1)

            def biases(i):
                for k in range(KT):
                    if k < RING and least(i, 2):
                        pe.wait_ge(out_ok, KT * (i - 1) + k - RING + 1)
                    elif k >= RING:
                        pe.wait_ge(out_ok, KT * (i - 1) + k - RING + 1)
                    if k == 0:
                        pe.wait_ge(wds_ok, i)
                    pe.matmul(po[k % RING][:], eb[:, k * P:(k + 1) * P], wds[:], start=True, stop=True).then_inc(bias_mm, 1)

            def pair(i, s, u):
                if least(i, 1):
                    pe.wait_ge(lg_ok, i)
                for c in range(NCH + 1):
                    if c < NCH:
                        pe.wait_ge(x3_ok, NCH * i + c + 1)
                        for k in range(c * CK, (c + 1) * CK):
                            pe.matmul(lg[0:A, :], rt[:, k, :], xr[s][:, k, :], start=k == 0, stop=False)
                    if c >= 1:
                        pe.wait_ge(sq_ok, NCH * i + c)
                        for k in range(CK):
                            mm = pe.matmul(lg[0:A, :], rsq[:], sq[(c - 1) % 2][:, k, :], start=False, stop=c == NCH and k == CK - 1)
                        if c < NCH:
                            mm.then_inc(x_mm, 1)
                mm.then_inc(lg_mm, 1)
                if least(i, 1):
                    biases(i)
                pe.wait_ge(lg_ok, i + 1)
                if least(i, 1):
                    pe.wait_ge(wd_ok, i)
                else:
                    pe.wait_ge(rsum_ok, 1)
                for q in range(QT):
                    mm = pe.transpose(raw[:, q, :], lgs[:, q * P:(q + 1) * P], ident[0:A, 0:A])
                mm.then_inc(tr_mm, 1)
                pe.wait_ge(wd_ok, i + 1)
                if least(i, 1):
                    pe.wait_ge(wds_ok, i)
                for q in range(QT):
                    mm = pe.transpose(wt[0:A, q * P:(q + 1) * P], wd[:, q, :], ident[:])
                mm.then_inc(wt_mm, 1)
                pe.wait_ge(wds_ok, i + 1)
                if least(i, 1):
                    pe.wait_ge(a1_ok, i)
                pe.matmul(ab[:], pick[:], wds[:], start=True, stop=True).then_inc(ab_mm, 1)
            pairs(pe, pair, lambda: biases(NPAIR))

        @block.scalar
        def _(act):
            act.wait_ge(k_set, 7)
            act.wait_ge(rsum_mm, 1)
            act.activation(rsum[:], tr[:, 0:E], ACT.Copy).then_inc(rsum_ok, 1)

            def gates(i, s, c):
                if c >= 2:
                    act.wait_ge(x3_ok, NCH * i + c - 1)
                elif least(i, 1):
                    act.wait_ge(x3_ok, NCH * i + c - 1)
                for k in range(c * CK, (c + 1) * CK):
                    for bb in range(2):
                        b = 2 * i + bb
                        t = slice(bb * L, (bb + 1) * L)
                        g = act.activation(gc[c % 2][:, k - c * CK, t], mk[s][:, k, t], ACT.Identity, bias=att[:, 1, k % 2, bass.ds(b, 1), k // 2], scale=att[:, 0, k % 2, bass.ds(b, 1), k // 2])
                g.then_inc(g_ok, 1)

            def squares(i, s, c):
                act.wait_ge(x3_ok, NCH * i + c + 1)
                if c >= 2:
                    act.wait_ge(x_mm, (NCH - 1) * i + c - 1)
                elif least(i, 1):
                    act.wait_ge(lg_mm, i)
                act.activation(sq[c % 2][:], xr[s][:, c * CK:(c + 1) * CK, :], ACT.Square).then_inc(sq_ok, 1)

            def pair(i, s, u):
                act.wait_ge(mk_in[s], 16 * (u + 1))
                gates(i, s, 0)
                gates(i, s, 1)
                for c in range(NCH):
                    squares(i, s, c)
                    if c + 2 < NCH:
                        gates(i, s, c + 2)
                act.wait_ge(lg_mm, i + 1)
                if least(i, 1):
                    act.wait_ge(tr_mm, i)
                act.activation(lgs[:], lg[0:A, :], ACT.Copy).then_inc(lg_ok, 1)
                act.wait_ge(var_ok, i + 1)
                act.activation(r4[:], r4[:], ACT.Sqrt, bias=eps[:]).then_inc(std_ok, 1)
                act.wait_ge(arg_ok, i + 1)
                act.activation(sc[:], lt[:], ACT.Exp).then_inc(exp_ok, 1)
                act.wait_ge(wt_mm, i + 1)
                if least(i, 1):
                    act.wait_ge(bias_mm, KT * i)
                act.activation(wds[:], wt[0:A, :], ACT.Copy).then_inc(wds_ok, 1)
                act.wait_ge(ab_mm, i + 1)
                if least(i, 1):
                    act.wait_ge(prod_ok, KT * i)
                act.activation(a1[:], ab[:], ACT.Identity, bias=ones[:, 0:1]).then_inc(a1_ok, 1)
            pairs(act, pair, lambda: None)

        @block.vector
        def _(dve):
            dve.wait_ge(k_in, 96)

            def x3(i, s, u):
                for c in range(NCH):
                    v = xr[s][:, c * CK:(c + 1) * CK, :]
                    dve.wait_ge(u_ok, NCH * i + c + 1)
                    dve.wait_ge(x_in[s][c], 16 * (u + 1))
                    dve.tensor_tensor(gc[c % 2][:], gc[c % 2][:], v, ALU.mult).then_inc(v_ok, 1)
                    dve.wait_ge(v_ok, NCH * i + c + 1)
                    if c == 0:
                        dve.wait_ge(row_in[s], 32 * (u + 1))
                    dve.tensor_tensor(v, gc[c % 2][:], m3[s][:].unsqueeze(1).broadcast_to([P, CK, T]), ALU.add).then_inc(x3_ok, 1)

            def outputs(i, s):
                for k in range(KT):
                    n = KT * (i - 1) + k
                    c = k // CK
                    dve.wait_ge(bias_mm, n + 1)
                    dve.wait_ge(prod_ok, n + 1)
                    if k % CK == 0 and (c >= 2 or least(i, 2)):
                        dve.wait_ge(stored[c % 2], 16 * (NCH // 2 * (i - 1) + c // 2))
                    dve.tensor_tensor(ost[c % 2][:, k % CK, :], xr[s][:, k, :], po[k % RING][:], ALU.add).then_inc(out_ok, 1)

            def routing(i):
                bc = lambda m: m[:].unsqueeze(2).broadcast_to([P, QT, E])
                row = lambda m: m[:].unsqueeze(1).broadcast_to([P, QT, E])
                dve.wait_ge(tr_mm, i + 1)
                n = STEPS * i
                if least(i, 1):
                    dve.wait_ge(wt_mm, i)
                dve.tensor_scalar(mean[:], raw[:, :, E], 1.0 / D, None, ALU.mult).then_inc(step_ok, 1)
                dve.wait_ge(step_ok, n + 1)
                dve.tensor_tensor(msq[:], mean[:], mean[:], ALU.mult).then_inc(step_ok, 1)
                dve.wait_ge(step_ok, n + 2)
                dve.scalar_tensor_tensor(r4[:], raw[:, :, E + 1], 1.0 / D, msq[:], ALU.mult, ALU.subtract).then_inc(var_ok, 1)
                dve.tensor_tensor(lm[:], bc(mean), row(rsum), ALU.mult).then_inc(step_ok, 1)
                dve.wait_ge(step_ok, n + 3)
                dve.tensor_tensor(lt[:], raw[:, :, 0:E], lm[:], ALU.subtract).then_inc(step_ok, 1)
                dve.wait_ge(step_ok, n + 4)
                dve.wait_ge(std_ok, i + 1)
                dve.reciprocal(r4[:], r4[:]).then_inc(step_ok, 1)
                dve.wait_ge(step_ok, n + 5)
                dve.tensor_tensor(lt[:], lt[:], bc(r4), ALU.mult).then_inc(step_ok, 1)
                dve.wait_ge(step_ok, n + 6)
                dve.tensor_tensor(lt[:], lt[:], row(rb), ALU.add).then_inc(step_ok, 1)
                dve.wait_ge(step_ok, n + 7)
                dve.tensor_reduce(mx[:], lt[:], AX.X, ALU.max).then_inc(step_ok, 1)
                dve.wait_ge(step_ok, n + 8)
                dve.tensor_tensor(lt[:], lt[:], bc(mx), ALU.subtract).then_inc(arg_ok, 1)
                dve.wait_ge(exp_ok, i + 1)
                dve.tensor_reduce(mx[:], sc[:], AX.X, ALU.add).then_inc(step_ok, 1)
                dve.wait_ge(step_ok, n + 9)
                dve.reciprocal(mx[:], mx[:]).then_inc(step_ok, 1)
                dve.wait_ge(step_ok, n + 10)
                dve.tensor_tensor(sc[:], sc[:], bc(mx), ALU.mult).then_inc(step_ok, 1)
                n_ready = counted(dve, n + 11)
                dve.wait_ge(k_in, 96)
                dve.wait_ge(step_ok, n_ready)
                for q in range(QT):
                    dve.max(top[:, q, :], sc[:, q, :]).then_inc(step_ok, 1)
                    n_ready = counted(dve, n + 11 + q + 1)
                    dve.wait_ge(k_in, 96)
                    dve.wait_ge(step_ok, n_ready)
                for q in range(QT):
                    dve.scalar_tensor_tensor(wd[:, q, 0:E], sc[:, q, :], top[:, q, TOP - 1:TOP], sc[:, q, :], ALU.is_ge, ALU.mult).then_inc(step_ok, 1)
                    dve.wait_ge(step_ok, n + 11 + QT + q + 1)
                dve.tensor_reduce(ws[:], top[:], AX.X, ALU.add).then_inc(step_ok, 1)
                dve.wait_ge(step_ok, n + 12 + 2 * QT)
                dve.tensor_tensor(rw[:], r4[:], ws[:], ALU.mult).then_inc(step_ok, 1)
                dve.wait_ge(step_ok, n + 13 + 2 * QT)
                dve.tensor_copy(wd[:, :, E + 1], rw[:]).then_inc(step_ok, 1)
                dve.wait_ge(step_ok, n + 14 + 2 * QT)
                dve.scalar_tensor_tensor(wd[:, :, E], mean[:], -1.0, rw[:], ALU.mult, ALU.mult).then_inc(wd_ok, 1)

            def pair(i, s, u):
                x3(i, s, u)
                if least(i, 1):
                    outputs(i, 1 - s)
                routing(i)
            pairs(dve, pair, lambda: outputs(NPAIR, 1))


def autocorrelation_lora_ffn_channel_attention_experts(nc, t):
    NB, L, D = t["x"].shape
    KEEP = int(np.floor(0.6 * L))
    KEEP += KEEP % 2
    R = t["loraT"].shape[0]
    pairs_shape = (NB // 2, P, D // P, 2 * L)
    scratch = lambda name, shape, dt=FP32: nc.dram_tensor(name, shape, dt, kind="Internal").ap()
    x1, xn3 = scratch("x1_pairs", pairs_shape), scratch("xn3_pairs", pairs_shape)
    masks = scratch("mask_pairs", pairs_shape, UINT8)
    rows3 = scratch("rows3", (2, NB // 2, 2 * L))
    w_split = scratch("w_split", (D // P, P, D // P, 2 * P), FP16)
    lora_aug = scratch("lora_aug", (R + 1, D))
    dft = [t[n] for n in ("dft_q", "dft_k", "dft_we", "dft_vo", "dft_wo", "dft_ic", "dft_iz", "identity")]
    split_weights_phase(nc, t["wT"], t["loraT"], w_split, lora_aug)
    attention_phase(nc, t["x"], t["ctx"], t["xT"], dft, x1)
    with nc.sbuf_tensor("feat", [P, 4, NB, D // P], FP32) as feat:
        ffn_phase(nc, x1, w_split, lora_aug, t["ffn_b"], t["gateT"], t["gate_b"], t["ctx_pairs"], t["identity"], xn3, rows3, masks, feat, KEEP)
        with nc.sbuf_tensor("att", [P, 2, 2, NB, D // P // 2], FP32) as att:
            channel_gates_phase(nc, feat, t["conv_w"], t["bn_gamma"], t["bn_beta"], t["neighbours"], t["identity"], att, KEEP, L)
            experts_phase(nc, xn3, rows3, masks, att, t["routerT"], t["router_b"], t["expert_b"], t["tail_rows"], t["identity"], t["out_pairs"])


def layouts(x, ctx_4096, L0_ffn_W, L0_ffn_b, L0_ffn_A, L0_ffn_B, L0_ffn_gate_w, L0_ffn_gate_b, L1_xattn_conv_w, L1_xattn_bn_gamma,
            L1_xattn_bn_beta, L1_ffn_router_weight, L1_ffn_router_bias, L1_ffn_expert_bias):
    NB, L, D = x.shape
    q, k, we, vo, wo, ic, ie, io = [m.astype(np.float32) for m in dft_constants(L)]
    segments = D // (2 * P)
    neighbours = np.zeros((P, 2, P), np.float32)
    for row in range(P):
        if row % segments:
            neighbours[row - 1, 0, row] = 1.0
        if row % segments != segments - 1:
            neighbours[row + 1, 1, row] = 1.0
    tail_rows = np.zeros((2, D + P), np.float32)
    tail_rows[0, :D] = 1.0
    tail_rows[1, D:] = 1.0
    return dict(
        x=x, ctx=ctx_4096, xT=x.transpose(0, 2, 1),
        ctx_pairs=ctx_4096.reshape(NB // 2, 2, L, D // P, P).transpose(0, 4, 3, 1, 2).reshape(NB // 2, P, D // P, 2 * L),
        wT=L0_ffn_W.T, loraT=L0_ffn_B.T, ffn_b=L0_ffn_b, gateT=np.concatenate([L0_ffn_A, L0_ffn_gate_w]).T, gate_b=L0_ffn_gate_b,
        conv_w=L1_xattn_conv_w, bn_gamma=L1_xattn_bn_gamma, bn_beta=L1_xattn_bn_beta,
        routerT=L1_ffn_router_weight.T, router_b=L1_ffn_router_bias, expert_b=L1_ffn_expert_bias,
        dft_q=q, dft_k=k, dft_we=we, dft_vo=vo, dft_wo=wo, dft_ic=ic, dft_iz=np.concatenate([ie, io]),
        identity=np.eye(P, dtype=np.float32), neighbours=neighbours, tail_rows=tail_rows)


def kernel(**inputs):
    import concourse.bacc as bacc
    from concourse.bass_utils import run_bass_kernel_spmd

    nc = bacc.Bacc("TRN2", target_bir_lowering=False, num_devices=1)
    arrays = {n: np.ascontiguousarray(a) for n, a in layouts(**{n: np.asarray(a) for n, a in inputs.items()}).items()}
    t = {n: nc.dram_tensor(n, a.shape, FP32, kind="ExternalInput").ap() for n, a in arrays.items()}
    NB, L, D = arrays["x"].shape
    t["out_pairs"] = nc.dram_tensor("out_pairs", (NB // 2, P, D // P, 2 * L), FP32, kind="ExternalOutput").ap()
    autocorrelation_lora_ffn_channel_attention_experts(nc, t)
    r = run_bass_kernel_spmd(nc, [arrays], core_ids=[0])
    out = r.results[0]["out_pairs"].reshape(NB // 2, P, D // P, 2, L)
    return np.ascontiguousarray(out.transpose(0, 3, 4, 2, 1).reshape(NB, L, D))
```

```python
import math
import numpy as np
import concourse.bass as bass
from concourse import mybir
from concourse.alu_op_type import AluOpType as ALU
from contextlib import ExitStack

FP32 = mybir.dt.float32
FP32R = mybir.dt.float32r
FP16 = mybir.dt.float16
BF16 = mybir.dt.bfloat16
UINT8 = mybir.dt.uint8
ACT = mybir.ActivationFunctionType
AX = mybir.AxisListType
P = 128
EPS = 1e-5
DFT_SCALE = 64.0
W_SCALE = 64.0


def dft_constants(L):
    F = L // 2
    t = np.arange(L)[:, None].astype(np.float64)
    f = np.arange(F)[None, :].astype(np.float64)
    alt = (-1.0) ** np.arange(L)
    cos_e, sin_e = np.cos(2 * np.pi * t * f / L), np.sin(2 * np.pi * t * f / L)
    cos_e[:, 0] = alt
    q = np.concatenate([cos_e, sin_e], 1)
    q[:, F] = 0.0
    k = q.copy()
    k[:, F] = 1.0
    k[L - 1, F] = 1.0 + L
    we = q.copy()
    we[:, F] = 1.0
    wo_ = np.pi * t * (2 * f + 1) / L
    wo = np.concatenate([np.cos(wo_), np.sin(wo_)], 1)
    vo = wo.copy()
    vo[L - 1] -= wo.sum(0)
    p = np.arange(L)[None, :].astype(np.float64)
    fc = np.arange(F)[:, None].astype(np.float64)
    ce, se = np.cos(2 * np.pi * fc * p / L), np.sin(2 * np.pi * fc * p / L)
    ic = np.concatenate([2 * ce, -2 * se], 0) / L
    ic[0] = alt / L
    ic[F] = 0.0
    ie = np.concatenate([2 * ce, 2 * se], 0) / (2 * L)
    ie[0] = alt / (2 * L)
    ie[F] = -1.0 / (2 * L)
    a = np.pi * (2 * fc + 1) * p / L
    io = np.concatenate([2 * np.cos(a), 2 * np.sin(a)], 0) / (2 * L)
    return q, k, we, vo, wo, ic, ie, io


def counted(eng, n):
    return n if isinstance(n, int) else eng.snap(eng.to_reg(n))


def attention_phase(nc, x, ctx, xT, dft, x1):
    NB, L, D = x.shape
    TT = L // P
    CW = 512
    CH = D // CW
    CT = CW // P
    TOPK = int(2 * np.log(L))
    STEPS = 2 * CH
    ITS = NB // 2
    LAST = NB * CH
    NEG = -3.0e38
    AFTER_LN, AFTER_S, AFTER_F, AFTER_C, AFTER_T, AFTER_I = 1, 2, 3, 4, 5, 6

    stack = ExitStack()
    sb = lambda name, shape, dt=FP32: stack.enter_context(nc.sbuf_tensor(name, shape, dt))
    pb = lambda name, shape: stack.enter_context(nc.psum_tensor(name, shape, FP32))
    sems = []

    def sem(name):
        sems.append(nc.alloc_semaphore(name))
        return sems[-1]
    with stack:
        m_q, m_k, m_we, m_vo, m_wo = (sb("m_" + n, [P, 2, TT, L], FP16) for n in ("q", "k", "we", "vo", "wo"))
        m_ic = sb("m_ic", [P, TT, L])
        m_iz = sb("m_iz", [P, 2 * TT, L])
        ident = sb("ident", [P, P])
        not_slot0 = sb("not_slot0", [P, 1])
        eps = sb("eps", [P, 1])
        xn = [sb(f"xn{i}", [P, TT, D]) for i in range(2)]
        cx = [sb(f"cx{i}", [P, TT, CW]) for i in range(2)]
        xs = [sb(f"xs{i}", [P, 2, TT, CW], FP16) for i in range(2)]
        cs = [sb(f"cs{i}", [P, 2, TT, CW], FP16) for i in range(2)]
        xt = [sb(f"xt{i}", [P, CT, L]) for i in range(2)]
        qf = [sb(f"qf{i}", [P, 2, CW]) for i in range(2)]
        kf = [sb(f"kf{i}", [P, 3, CW]) for i in range(4)]
        vf = [sb(f"vf{i}", [P, 3, CW]) for i in range(4)]
        pr = sb("pr", [P, 4, CW])
        pf = [sb(f"pf{i}", [P, 2, CW]) for i in range(2)]
        co = [sb(f"co{i}", [P, CT, L]) for i in range(2)]
        wk = [sb(f"wk{i}", [P, CT, L]) for i in range(2)]
        top = [sb(f"top{i}", [P, CT, 16]) for i in range(2)]
        nmax = [sb(f"nmax{i}", [P, CT]) for i in range(2)]
        wsum = [sb(f"wsum{i}", [P, CT]) for i in range(2)]
        wrec = [sb(f"wrec{i}", [P, CT]) for i in range(2)]
        ws = sb("wts", [P, 2, TT, CW], FP16)
        zf = [sb(f"zf{i}", [P, 4, CW]) for i in range(2)]
        xo = [sb(f"xo{i}", [P, CT, L]) for i in range(2)]
        st = sb("st", [P, TT, D // 512, 6])
        mv = sb("mv", [P, TT, 2])
        std = sb("std", [P, TT])
        rstd = sb("rstd", [P, TT])
        nmr = sb("nmr", [P, TT])
        bx, by, bz, bu = (pb(n, [P, 2, 512]) for n in ("bx", "by", "bz", "bu"))

        consts_in = sem("consts_in")
        x_in = [sem(f"x_in{i}") for i in range(2)]
        cx_in = [sem(f"cx_in{i}") for i in range(2)]
        xt_in = [sem(f"xt_in{i}") for i in range(2)]
        x1_out = [sem(f"x1_out{i}") for i in range(2)]
        const_set, ln_bn, ln_mv, ln_std, ln_rstd, ln_scale, x_normed = map(sem, (
            "const_set", "ln_bn", "ln_mv", "ln_std", "ln_rstd", "ln_scale", "x_normed"))
        q_mm, k_mm, v_mm, c_mm, t_mm, we_mm, wo_mm, i_mm = map(sem, (
            "q_mm", "k_mm", "v_mm", "c_mm", "t_mm", "we_mm", "wo_mm", "i_mm"))
        q_sb, k_part, k_sb, v_sb, c_sb, wt_sb, e_sb, w_sb = map(sem, (
            "q_sb", "k_part", "k_sb", "v_sb", "c_sb", "wt_sb", "e_sb", "w_sb"))
        p_mul, p_sum, top_a, top_cut, top_b, nmax_ok, w_cut, w_rec, ze_mul, ze_sum, zo_mul, zo_sum, x1_sum = map(sem, (
            "p_mul", "p_sum", "top_a", "top_cut", "top_b", "nmax_ok", "w_cut", "w_rec", "ze_mul", "ze_sum", "zo_mul", "zo_sum", "x1_sum"))
        xh_ok, xl_ok, ch_ok, cl_ok, wl_ok, mats_ok = map(sem, ("xh1_ok", "xl1_ok", "ch_ok", "cl_ok", "wl_ok", "mats_ok"))
        N_CONST = 8
        parts = (m_q, m_k, m_we, m_vo, m_wo)
        staged = [t.rearrange("p b (a n) -> p b a n", n=L) for t in (
            zf[0][:, 0:2, :], zf[0][:, 2:4, :], zf[1][:, 0:2, :], zf[1][:, 2:4, :], pr[:, 0:2, :])]
        block = stack.enter_context(nc.Block())

        def steps(eng, step, drain):
            for k in range(STEPS):
                step(0, k)
            if ITS > 1:
                with eng.Fori(1, ITS) as it:
                    for k in range(STEPS):
                        step(it, k)
            for k in range(drain):
                step(ITS, k)

        def chunk(it, k, lag):
            h = STEPS * it + (k - lag)
            return None if isinstance(h, int) and not 0 <= h < LAST else h

        def batch(it, k):
            b = 2 * it + k // CH
            return None if k % CH or (isinstance(b, int) and b >= NB) else b

        def dram_batch(ap, it, k, lag):
            return ap[bass.ds(2 * it + (k - lag) // CH, 1), :, :].rearrange("a p n -> p (a n)")

        @block.sync
        def _(sp):
            for tile, m in zip(staged, dft[:5]):
                sp.dma_start(tile, m.rearrange("b (a p) n -> p b a n", p=P)).then_inc(consts_in, 16)
            for tile, m in zip((m_ic, m_iz), dft[5:7]):
                sp.dma_start(tile[:], m.rearrange("(a p) n -> p a n", p=P)).then_inc(consts_in, 16)
            sp.dma_start(ident[:], dft[7]).then_inc(consts_in, 16)

            def step(it, k):
                b = batch(it, k)
                if b is not None:
                    if not isinstance(b, int) or b >= 2:
                        sp.wait_ge(xl_ok, CH * (b - 1))
                    sp.dma_start(xn[(k // CH) % 2][:], x[bass.ds(b, 1), :, :].rearrange("a (t p) n -> p (a t) n", p=P)).then_inc(x_in[(k // CH) % 2], 16)
                h = chunk(it, k, 1)
                if h is not None:
                    s = (k - 1) % 2
                    if not isinstance(h, int) or h >= 2:
                        sp.wait_ge(cl_ok, h - 1)
                    c = (k - 1) % CH
                    sp.dma_start(cx[s][:], ctx[bass.ds(2 * it + (k - 1) // CH, 1), :, c * CW:(c + 1) * CW].rearrange("a (t p) n -> p (a t) n", p=P)).then_inc(cx_in[s], 16)
                h = chunk(it, k, AFTER_T)
                if h is not None:
                    s, b = (k - AFTER_T) % 2, counted(sp, 2 * it + (k - AFTER_T) // CH)
                    if not isinstance(h, int) or h >= 2:
                        sp.wait_ge(x1_sum, h - 1)
                    c = (k - AFTER_T) % CH
                    sp.dma_start(xt[s][:], xT[bass.ds(b, 1), c * CW:(c + 1) * CW, :].rearrange("a (j p) t -> p (a j) t", p=P)).then_inc(xt_in[s], 16)
            steps(sp, step, AFTER_T)

        @block.gpsimd
        def _(pool):
            pool.memset(not_slot0[:], 1.0 / DFT_SCALE).then_inc(const_set, 1)
            pool.memset(eps[:], EPS).then_inc(const_set, 1)
            pool.wait_ge(const_set, 2)
            pool.memset(not_slot0[0:1, :], 0.0).then_inc(const_set, 1)

            def step(it, k):
                h = chunk(it, k, AFTER_S)
                if h is not None:
                    kk = k - AFTER_S
                    s, c = kk % 2, kk % CH
                    if not isinstance(h, int) or h >= 2:
                        pool.wait_ge(v_mm, h - 1)
                    pool.wait_ge(xh_ok, h + 1)
                    pool.tensor_tensor(xs[s][:, 1, :, :], xn[(kk // CH) % 2][:, :, c * CW:(c + 1) * CW], xs[s][:, 0, :, :], ALU.subtract).then_inc(xl_ok, 1)
                    pool.wait_ge(ch_ok, h + 1)
                    pool.tensor_tensor(cs[s][:, 1, :, :], cx[s][:], cs[s][:, 0, :, :], ALU.subtract).then_inc(cl_ok, 1)
                h = chunk(it, k, AFTER_I)
                if h is None:
                    return
                s, c = (k - AFTER_I) % 2, (k - AFTER_I) % CH
                n_ready = counted(pool, h + 1)
                pool.wait_ge(const_set, 3)
                pool.wait_ge(x1_sum, n_ready)
                bb = (k - AFTER_I) // CH
                pool.dma_start(x1[bass.ds(it + bb // 2, 1), :, c * CT:(c + 1) * CT, bb % 2 * L:(bb % 2 + 1) * L].rearrange("a p j t -> p (a j) t"), xo[s][:]).then_inc(x1_out[s], 16)
            steps(pool, step, AFTER_I)
            for s in range(2):
                pool.wait_ge(x1_out[s], 16 * (LAST // 2))

        @block.tensor
        def _(pe):
            pe.wait_ge(consts_in, 16 * N_CONST)

            pe.wait_ge(mats_ok, len(parts))

            def transform(out, mats, src, done):
                for m in range(2):
                    for a in range(TT):
                        for hm, hx in ((0, 0), (0, 1), (1, 0)):
                            mm = pe.matmul(out[:, m, :], mats[:, hm, a, m * P:(m + 1) * P], src[:, hx, a, :], start=a + hm + hx == 0, stop=a == TT - 1 and hm == 1)
                mm.then_inc(done, 1)

            def step(it, k):
                h = chunk(it, k, AFTER_F)
                if h is not None:
                    kk = k - AFTER_F
                    pe.wait_ge(xl_ok, h + 1)
                    if not isinstance(h, int) or h >= 2:
                        pe.wait_ge(c_sb, h - 1)
                    elif h == 1:
                        pe.wait_ge(q_sb, 1)
                    transform(bx, m_q, xs[kk % 2], q_mm)
                    pe.wait_ge(cl_ok, h + 1)
                    if not isinstance(h, int) or h >= 3:
                        pe.wait_ge(ze_mul, 2 * (h - 2))
                    elif h >= 1:
                        pe.wait_ge(k_sb, h)
                    transform(by, m_k, cs[kk % 2], k_mm)
                    if not isinstance(h, int) or h >= 3:
                        pe.wait_ge(zo_mul, 2 * (h - 2))
                    elif h >= 1:
                        pe.wait_ge(v_sb, h)
                    transform(bz, m_vo, cs[kk % 2], v_mm)
                h = chunk(it, k, AFTER_T)
                if h is not None:
                    s = (k - AFTER_T) % 2
                    pe.wait_ge(w_sb, CT * (h + 1))
                    if not isinstance(h, int) or h >= 2:
                        pe.wait_ge(x1_sum, h - 1)
                    elif h == 1:
                        pe.wait_ge(wl_ok, 1)
                    for a in range(TT):
                        for j in range(CT):
                            mm = pe.transpose(bu[:, a, j * P:(j + 1) * P], wk[s][:, j, a * P:(a + 1) * P], ident[:])
                    mm.then_inc(t_mm, 1)
                h = chunk(it, k, AFTER_C)
                if h is not None:
                    s = (k - AFTER_C) % 2
                    pe.wait_ge(p_sum, 2 * (h + 1))
                    g = chunk(it, k, AFTER_F)
                    if g is not None:
                        pe.wait_ge(q_sb, g + 1)
                    else:
                        pe.wait_ge(q_sb, LAST)
                        pe.wait_ge(c_sb, h)
                    for j in range(CT):
                        for a in range(TT):
                            mm = pe.matmul(bx[:, j // 2, (j % 2) * L:(j % 2 + 1) * L], pf[s][:, a, j * P:(j + 1) * P], m_ic[:, a, :], start=a == 0, stop=a == TT - 1)
                    mm.then_inc(c_mm, 1)
                h = chunk(it, k, AFTER_T)
                if h is not None:
                    g = chunk(it, k, AFTER_F)
                    n = LAST if g is None else g + 1
                    pe.wait_ge(wl_ok, h + 1)
                    if g is None:
                        pe.wait_ge(zo_mul, 2 * h)
                        pe.wait_ge(ze_mul, 2 * h)
                    pe.wait_ge(k_sb, n)
                    transform(by, m_we, ws, we_mm)
                    pe.wait_ge(v_sb, n)
                    transform(bz, m_wo, ws, wo_mm)
                h = chunk(it, k, AFTER_I)
                if h is not None:
                    s = (k - AFTER_I) % 2
                    pe.wait_ge(ze_sum, 2 * (h + 1))
                    pe.wait_ge(zo_sum, 2 * (h + 1))
                    g = chunk(it, k, AFTER_T)
                    pe.wait_ge(wl_ok, LAST if g is None else g + 1)
                    if g is None:
                        pe.wait_ge(x1_sum, h)
                    for j in range(CT):
                        for a in range(2 * TT):
                            mm = pe.matmul(bu[:, j // 2, (j % 2) * L:(j % 2 + 1) * L], zf[s][:, a, j * P:(j + 1) * P], m_iz[:, a, :], start=a == 0, stop=a == 2 * TT - 1)
                    mm.then_inc(i_mm, 1)
            steps(pe, step, AFTER_I)

        @block.scalar
        def _(act):
            act.wait_ge(const_set, 3)
            act.wait_ge(consts_in, 16 * N_CONST)
            for tile, whole in zip(parts, staged):
                act.activation(tile[:], whole, ACT.Copy).then_inc(mats_ok, 1)

            def step(it, k):
                b = batch(it, k - AFTER_LN) if k >= AFTER_LN else None
                if b is not None:
                    act.wait_ge(ln_scale, b + 1)
                    for a in range(TT):
                        tile = xn[((k - AFTER_LN) // CH) % 2][:, a, :]
                        act.activation(tile, tile, ACT.Identity, bias=nmr[:, a:a + 1], scale=rstd[:, a:a + 1]).then_inc(x_normed, 1)
                h = chunk(it, k, AFTER_S)
                if h is not None:
                    kk = k - AFTER_S
                    s, c = kk % 2, kk % CH
                    if not isinstance(h, int) or h >= 2:
                        act.wait_ge(v_mm, h - 1)
                    bb = 2 * it + kk // CH
                    act.wait_ge(x_normed, TT * (bb + 1))
                    act.activation(xs[s][:, 0, :, :], xn[(kk // CH) % 2][:, :, c * CW:(c + 1) * CW], ACT.Copy).then_inc(xh_ok, 1)
                    act.wait_ge(cx_in[s], 16 * (4 * it + kk // 2 + 1))
                    act.activation(cs[s][:, 0, :, :], cx[s][:], ACT.Copy).then_inc(ch_ok, 1)
                h = chunk(it, k, AFTER_F)
                if h is not None:
                    kk = k - AFTER_F
                    s, s4 = kk % 2, kk % 4
                    act.wait_ge(q_mm, h + 1)
                    if not isinstance(h, int) or h >= 2:
                        act.wait_ge(p_mul, 2 * (h - 1))
                    act.activation(qf[s][:], bx[:], ACT.Copy, scale=1.0 / DFT_SCALE).then_inc(q_sb, 1)
                    act.wait_ge(k_mm, h + 1)
                    if not isinstance(h, int) or h >= 4:
                        act.wait_ge(ze_mul, 2 * (h - 3))
                    act.activation(kf[s4][:, 0, :], by[:, 0, :], ACT.Copy, scale=1.0 / DFT_SCALE).then_inc(k_part, 1)
                    act.activation(kf[s4][:, 2, :], by[:, 0, :], ACT.Copy, scale=1.0 / DFT_SCALE).then_inc(k_part, 1)
                    act.activation(kf[s4][:, 1, :], by[:, 1, :], ACT.Copy, scale=not_slot0[:]).then_inc(k_part, 1)
                    act.wait_ge(k_part, 3 * h + 3)
                    act.activation(kf[s4][0:1, 2, :], by[0:1, 1, :], ACT.Copy, scale=1.0 / DFT_SCALE).then_inc(k_sb, 1)
                    act.wait_ge(v_mm, h + 1)
                    if not isinstance(h, int) or h >= 4:
                        act.wait_ge(zo_mul, 2 * (h - 3))
                    act.activation(vf[s4][:, 0:2, :], bz[:], ACT.Copy, scale=1.0 / DFT_SCALE)
                    act.activation(vf[s4][:, 2, :], bz[:, 0, :], ACT.Copy, scale=1.0 / DFT_SCALE).then_inc(v_sb, 1)
                h = chunk(it, k, AFTER_T)
                if h is not None:
                    act.wait_ge(t_mm, h + 1)
                    if not isinstance(h, int) or h >= 1:
                        act.wait_ge(wo_mm, h)
                    act.activation(ws[:, 0, :, :], bu[:], ACT.Copy).then_inc(wt_sb, 1)
                h = chunk(it, k, AFTER_C)
                if h is not None:
                    s = (k - AFTER_C) % 2
                    act.wait_ge(c_mm, h + 1)
                    if not isinstance(h, int) or h >= 2:
                        act.wait_ge(w_cut, CT * (h - 1))
                    act.activation(co[s][:].rearrange("p (a j) t -> p a (j t)", a=2), bx[:], ACT.Copy).then_inc(c_sb, 1)
                    act.wait_ge(c_sb, h + 1)
                    act.wait_ge(nmax_ok, h + 1)
                    for j in range(CT):
                        act.activation(wk[s][:, j, :], co[s][:, j, :], ACT.Exp, bias=nmax[s][:, j:j + 1]).then_inc(e_sb, 1)
                    act.wait_ge(w_rec, h + 1)
                    for j in range(CT):
                        act.activation(wk[s][:, j, :], wk[s][:, j, :], ACT.Copy, scale=wrec[s][:, j:j + 1]).then_inc(w_sb, 1)
                b = batch(it, k)
                if b is not None:
                    act.wait_ge(ln_mv, TT * (b + 1))
                    act.activation(std[:], mv[:, :, 1], ACT.Sqrt, bias=eps[:]).then_inc(ln_std, 1)
            steps(act, step, AFTER_I)

        @block.vector
        def _(dve):
            def products(src, spectrum, scratch, out, mul, added, h):
                dve.tensor_tensor(scratch[:, 0:2, :], src, spectrum[:, 0:2, :], ALU.mult).then_inc(mul, 1)
                dve.tensor_tensor(scratch[:, 2:4, :], src, spectrum[:, 1:3, :], ALU.mult).then_inc(mul, 1)
                dve.wait_ge(mul, 2 * h + 1)
                dve.tensor_tensor(out[:, 0, :], scratch[:, 0, :], scratch[:, 1, :], ALU.add).then_inc(added, 1)
                dve.wait_ge(mul, 2 * h + 2)
                dve.tensor_tensor(out[:, 1, :], scratch[:, 2, :], scratch[:, 3, :], ALU.subtract).then_inc(added, 1)

            def step(it, k):
                b = batch(it, k)
                if b is not None:
                    slot = (k // CH) % 2
                    dve.wait_ge(x_in[slot], 16 * (it + 1))
                    for a in range(TT):
                        for n in range(D // 512):
                            dve.bn_stats(st[:, a, n, :], xn[slot][:, a, n * 512:(n + 1) * 512]).then_inc(ln_bn, 1)
                    n_ready = counted(dve, TT * (D // 512) * (b + 1))
                    dve.wait_ge(consts_in, 16 * N_CONST)
                    dve.wait_ge(ln_bn, n_ready)
                    for a in range(TT):
                        dve.bn_aggr(mv[:, a, :], st[:, a, :, :]).then_inc(ln_mv, 1)
                b = batch(it, k - AFTER_LN) if k >= AFTER_LN else None
                if b is not None:
                    dve.wait_ge(ln_std, b + 1)
                    if not isinstance(b, int) or b >= 1:
                        dve.wait_ge(x_normed, TT * b)
                    dve.reciprocal(rstd[:], std[:]).then_inc(ln_rstd, 1)
                    dve.wait_ge(ln_rstd, b + 1)
                    dve.scalar_tensor_tensor(nmr[:], mv[:, :, 0], -1.0, rstd[:], ALU.mult, ALU.mult).then_inc(ln_scale, 1)
                h = chunk(it, k, AFTER_F)
                if h is not None:
                    kk = k - AFTER_F
                    dve.wait_ge(q_sb, h + 1)
                    dve.wait_ge(k_sb, h + 1)
                    if not isinstance(h, int) or h >= 3:
                        dve.wait_ge(zo_sum, 2 * (h - 2))
                    elif h >= 1:
                        dve.wait_ge(p_sum, 2 * h)
                    if not isinstance(h, int) or h >= 2:
                        dve.wait_ge(c_mm, h - 1)
                    products(qf[kk % 2][:], kf[kk % 4], pr, pf[kk % 2], p_mul, p_sum, h)
                h = chunk(it, k, AFTER_T)
                if h is not None:
                    dve.wait_ge(wt_sb, h + 1)
                    dve.tensor_tensor(ws[:, 1, :, :], bu[:], ws[:, 0, :, :], ALU.subtract).then_inc(wl_ok, 1)
                h = chunk(it, k, AFTER_C)
                if h is not None:
                    s = (k - AFTER_C) % 2
                    n_ready, n_used = counted(dve, h + 1), counted(dve, h - 1)
                    dve.wait_ge(consts_in, 16 * N_CONST)
                    if not isinstance(h, int) or h >= 2:
                        dve.wait_ge(t_mm, n_used)
                    dve.wait_ge(c_sb, n_ready)
                    for j in range(CT):
                        dve.max(top[s][:, j, 0:8], co[s][:, j, :]).then_inc(top_a, 1)
                    for j in range(CT):
                        n_ready = counted(dve, CT * h + j + 1)
                        dve.wait_ge(consts_in, 16 * N_CONST)
                        dve.wait_ge(top_a, n_ready)
                        dve.match_replace(wk[s][:, j, :], top[s][:, j, 0:8], co[s][:, j, :], NEG).then_inc(top_cut, 1)
                    for j in range(CT):
                        n_ready = counted(dve, CT * h + j + 1)
                        dve.wait_ge(consts_in, 16 * N_CONST)
                        dve.wait_ge(top_cut, n_ready)
                        dve.max(top[s][:, j, 8:16], wk[s][:, j, :]).then_inc(top_b, 1)
                    dve.wait_ge(top_b, CT * (h + 1))
                    dve.tensor_scalar(nmax[s][:], top[s][:, :, 0], -1.0, None, ALU.mult).then_inc(nmax_ok, 1)
                h = chunk(it, k, AFTER_T)
                if h is not None:
                    s4, s = (k - AFTER_T) % 4, (k - AFTER_T) % 2
                    g = chunk(it, k, AFTER_F)
                    dve.wait_ge(p_sum, 2 * LAST if g is None else 2 * (g + 1))
                    if not isinstance(h, int) or h >= 2:
                        dve.wait_ge(i_mm, h - 1)
                    dve.wait_ge(we_mm, h + 1)
                    products(by[:], kf[s4], pr, zf[s][:, 0:2, :], ze_mul, ze_sum, h)
                    dve.wait_ge(ze_sum, 2 * (h + 1))
                    dve.wait_ge(wo_mm, h + 1)
                    products(bz[:], vf[s4], pr, zf[s][:, 2:4, :], zo_mul, zo_sum, h)
                h = chunk(it, k, AFTER_C)
                if h is not None:
                    s = (k - AFTER_C) % 2
                    for j in range(CT):
                        dve.wait_ge(e_sb, CT * h + j + 1)
                        dve.scalar_tensor_tensor(wk[s][:, j, :], co[s][:, j, :], top[s][:, j, TOPK - 1:TOPK], wk[s][:, j, :], ALU.is_ge, ALU.mult, accum_out=wsum[s][:, j:j + 1]).then_inc(w_cut, 1)
                    dve.wait_ge(w_cut, CT * (h + 1))
                    dve.reciprocal(wrec[s][:], wsum[s][:]).then_inc(w_rec, 1)
                h = chunk(it, k, AFTER_I)
                if h is not None:
                    s = (k - AFTER_I) % 2
                    dve.wait_ge(i_mm, h + 1)
                    dve.wait_ge(xt_in[s], 16 * (4 * it + (k - AFTER_I) // 2 + 1))
                    if not isinstance(h, int) or h >= 2:
                        dve.wait_ge(x1_out[s], 16 * (4 * it + (k - AFTER_I) // 2))
                    dve.tensor_tensor(xo[s][:].rearrange("p (a j) t -> p a (j t)", a=2), bu[:], xt[s][:].rearrange("p (a j) t -> p a (j t)", a=2), ALU.add).then_inc(x1_sum, 1)
            steps(dve, step, AFTER_I)
    nc.clear_and_free_semaphores(sems)
    nc.all_engine_barrier()


def split_weights_phase(nc, wT, loraT, w_split, lora_aug):
    D, O = wT.shape
    R = loraT.shape[0]
    KT, OT, NC = D // P, O // P, O // 512
    stack = ExitStack()
    sb = lambda name, shape, dt=FP32: stack.enter_context(nc.sbuf_tensor(name, shape, dt))
    sems = []

    def sem(name):
        sems.append(nc.alloc_semaphore(name))
        return sems[-1]
    with stack:
        w = [sb(f"w_f32_{i}", [P, OT, P]) for i in range(2)]
        hl = [sb(f"w_hl_{i}", [P, OT, 2, P], FP16) for i in range(2)]
        minus = sb("minus", [P, R + 1], FP16)
        aug = sb("aug_row", [R + 1, O])
        sums = stack.enter_context(nc.psum_tensor("w_sums", [R + 1, NC, 512], FP32))
        w_in = [sem(f"w0_in{i}") for i in range(2)]
        w_out = [sem(f"w0_out{i}") for i in range(2)]
        hi_ok, lo_ok, sums_mm, minus_set, b_in, row_ok, row_out = map(sem, (
            "w0_hi", "w0_lo", "w0_sums", "w0_minus", "w0_b_in", "w0_row", "w0_row_out"))
        block = stack.enter_context(nc.Block())

        def tiles(eng, step):
            step(0, 0, 0)
            step(1, 1, 0)
            with eng.Fori(1, KT // 2 - 1) as it:
                step(2 * it, 0, it)
                step(2 * it + 1, 1, it)
            step(KT - 2, 0, KT // 2 - 1)
            step(KT - 1, 1, KT // 2 - 1)

        @block.sync
        def _(sp):
            sp.dma_start(aug[0:R, :], loraT).then_inc(b_in, 16)

            def step(k, s, it):
                if not isinstance(k, int) or k >= 2:
                    sp.wait_ge(lo_ok, k - 1)
                sp.dma_start(w[s][:], wT[bass.ds(k * P, P), :].rearrange("p (o n) -> p o n", n=P)).then_inc(w_in[s], 16)
            tiles(sp, step)
            sp.wait_ge(row_ok, NC)
            sp.wait_ge(b_in, 16)
            sp.dma_start(lora_aug, aug[:]).then_inc(row_out, 16)
            sp.wait_ge(row_out, 16)

        @block.gpsimd
        def _(pool):
            pool.memset(minus[:], 0.0).then_inc(minus_set, 1)
            pool.wait_ge(minus_set, 1)
            pool.memset(minus[:, R:R + 1], -1.0).then_inc(minus_set, 1)

            def step(k, s, it):
                pool.wait_ge(lo_ok, k + 1)
                pool.dma_start(w_split[:, :, bass.ds(k, 1), :].rearrange("o p a n -> p o (a n)"), hl[s][:].rearrange("p o a n -> p o (a n)")).then_inc(w_out[s], 16)
            tiles(pool, step)
            for s in range(2):
                pool.wait_ge(w_out[s], 16 * (KT // 2))

        @block.scalar
        def _(act):
            def step(k, s, it):
                act.wait_ge(w_in[s], 16 * (it + 1))
                if not isinstance(k, int) or k >= 2:
                    act.wait_ge(w_out[s], 16 * it)
                    act.wait_ge(sums_mm, k - 1)
                act.activation(hl[s][:, :, 0, :], w[s][:], ACT.Copy, scale=W_SCALE).then_inc(hi_ok, 1)
            tiles(act, step)

        @block.vector
        def _(dve):
            def step(k, s, it):
                dve.wait_ge(hi_ok, k + 1)
                for o in range(0, OT, 8):
                    i = dve.scalar_tensor_tensor(hl[s][:, o:o + 8, 1, :], w[s][:, o:o + 8, :], W_SCALE, hl[s][:, o:o + 8, 0, :], ALU.mult, ALU.subtract)
                i.then_inc(lo_ok, 1)
            tiles(dve, step)
            for c in range(NC):
                dve.wait_ge(sums_mm, KT)
                dve.tensor_copy(aug[R:R + 1, c * 512:(c + 1) * 512], sums[R:R + 1, c, :]).then_inc(row_ok, 1)

        @block.tensor
        def _(pe):
            pe.wait_ge(minus_set, 2)

            def step(k, s, it):
                pe.wait_ge(lo_ok, k + 1)
                first, last = isinstance(k, int) and k == 0, isinstance(k, int) and k == KT - 1
                for c in range(NC):
                    for part in range(2):
                        mm = pe.matmul(sums[:, c, :], minus[:], hl[s][:, 4 * c:4 * c + 4, part, :], start=first and part == 0, stop=last and part == 1)
                mm.then_inc(sums_mm, 1)
            tiles(pe, step)
    nc.clear_and_free_semaphores(sems)
    nc.all_engine_barrier()


def ffn_phase(nc, x1, w_split, lora_aug, bias, gateT, gate_b, ctxT, ident_d, xn3, rows3, masks, feat, keep, bad):
    NPAIR, _, KT, T = x1.shape
    L = T // 2
    D = KT * P
    OT = KT
    R = lora_aug.shape[0] - 1
    NG = gateT.shape[1] - R
    RANKS = (8, 16, 32, 64)
    QT = T // P
    LAG, RING = 2, 4
    WR = 2
    CR = 8
    NCH, CK = 4, KT // 4
    GT, GU = 4, 8
    NGRP = KT // GT
    MOVES = (1.0, 0.8, 0.6, 0.5, 0.4)
    COUNTS = len(MOVES) + 1
    WINDOW = 16
    FRAC = keep / L
    lo, hi = -9.0, 9.0
    for _ in range(60):
        z = (lo + hi) / 2
        lo, hi = (z, hi) if 0.5 * math.erfc(z / math.sqrt(2)) > FRAC else (lo, z)
    TOKENS_PER_STD = L * math.exp(-z * z / 2) / math.sqrt(2 * math.pi)
    AIM = 2.0 * (keep - WINDOW // 2) - L
    NEG = -3.0e38
    CHUNK_UNITS = 2 * CK
    UNITS = 2 * KT

    stack = ExitStack()
    sb = lambda name, shape, dt=FP32: stack.enter_context(nc.sbuf_tensor(name, shape, dt))
    sems = []

    def sem(name):
        sems.append(nc.alloc_semaphore(name))
        return sems[-1]
    with stack:
        xr = [sb(f"xr{i}", [P, KT, T]) for i in range(2)]
        xh, xl = sb("xh", [P, KT, T], FP16), sb("xl", [P, KT, T], FP16)
        sq = sb("sq", [P, CK, T])
        g32 = sq[:].rearrange("p k t -> p (k t)")[:, 0:KT * (R + NG)].rearrange("p (k r) -> p k r", k=KT)
        ws = [sb(f"ws{i}", [P, KT, 2, P], FP16) for i in range(WR)]
        mk = [sb(f"mk{i}", [P, KT, T], UINT8) for i in range(2)]
        ct = [sb(f"ct{i}", [P, T]) for i in range(CR)]
        cut = [sb(f"cut{i}", [P, 2, L]) for i in range(2)]
        top = sb("top2", [P, 2, WINDOW])
        rank, pick, vk = sb("rank", [P, WINDOW]), sb("pick_k", [P, 2, WINDOW]), sb("vk", [P, 2])
        st6, mv = sb("st6", [P, GU, 6]), sb("mv2", [P, GU, 2])
        std, guess = sb("std_c", [P, GU]), [sb(f"minus_guess{i}", [P, GU]) for i in range(2)]
        slope, off = [sb(f"slope{i}", [P, GU]) for i in range(2)], sb("off", [P, GU])
        above = [sb(f"above{i}", [P, GU]) for i in range(2)]
        limit, kth = [sb(f"limit{i}", [P, GU]) for i in range(2)], [sb(f"kth{i}", [P, GU]) for i in range(2)]
        kept, wrong = sb("kept", [P, UNITS]), sb("wrong", [P, 1])
        signs = [sb(f"signs{i}", [P, L], BF16) for i in range(4)]
        aug = sb("aug", [R + 1, OT * P])
        gh, gl = sb("gh", [P, KT, R + NG], FP16), sb("gl", [P, KT, R + NG], FP16)
        gsum = sb("gsum", [1, R + NG])
        gb = sb("gb", [P, NG])
        bcol = sb("bcol", [P, OT])
        ident = sb("ident2", [P, P])
        ones = sb("ones", [P, P])
        minus1 = sb("minus1", [P, 1], FP16)
        eps = sb("eps2", [P, 2])
        red2, red3 = sb("red2", [P, 2, T]), sb("red3", [P, 2, T])
        mean2, r2, msq = sb("mean2", [P, T]), [sb(f"r2_{i}", [P, T]) for i in range(2)], sb("msq", [P, T])
        part = msq
        mean3, s3, r3 = sb("mean3", [P, T]), sb("s3", [P, T]), sb("r3", [P, T])
        ev = sb("ev", [P, T])
        low = sb("low", [P, QT, R])
        rc, mx = sb("rc", [P, QT]), sb("mx", [P, QT])
        sc, nb = sb("sc", [P, QT, NG]), sb("nb", [P, QT, NG])
        arhs = sb("arhs", [R + 1, T])
        cf = [sb(f"cf{i}", [P, L]) for i in range(2)]
        sf = sb("sf", [P, L])
        fp = sb("feat_pair", [P, 4, 2, KT])
        acc = [stack.enter_context(nc.psum_tensor(f"acc{i}", [P, T], FP32)) for i in range(RING)]
        ps_s, ps_q, ps_g, ps_a = (stack.enter_context(nc.psum_tensor(n, [P, 512], FP32)) for n in ("ps_s", "ps_q", "ps_g", "ps_a"))
        unread = ps_a[:].rearrange("p (h l) -> p h l", h=2)
        raw = ps_g[:, 0:QT * (R + NG)].rearrange("p (q r) -> p q r", q=QT)
        rcol = ps_g[:, QT * (R + NG):QT * (R + NG) + QT]

        x_in = [[sem(f"x1_in{i}_{c}") for c in range(NCH)] for i in range(2)]
        w_in = [sem(f"w_in{i}") for i in range(WR)]
        c_in = [sem(f"c_in{i}") for i in range(CR)]
        x_out = [sem(f"xn3_out{i}") for i in range(2)]
        m_out = [sem(f"mask_out{i}") for i in range(2)]
        (k_in, k_set, g_hi, g_lo, gsum_mm, gsum_ok, hi_ok, lo_ok, sq_ok, part_ok, sum_ok, st2_mm, mean2_ok, msq_ok, var2_ok,
         std2, r2_ok, g_mm, rcol_mm, rc_ok, sc_ok, low_ok, low_t, arhs_ok, arow_ok, main_mm, out_mm, ev_ok, x2_ok,
         st3_mm, mean3_ok, var3_ok, std3, r3_ok, cent_ok, xn3_ok, cmax_ok, smax_ok, csum_ok, xsum_ok,
         feat_ok, red_ok, row_out, bn_ok, mv_ok, std_ok, init_ok, guess_ok, off_ok, sign_ok, fin_ok, ind_ok, cut_ok, top_ok, kth_ok, mask_ok, bad_ok) = map(sem, (
             "k2_in", "k2_set", "g_hi", "g_lo", "gsum_mm", "gsum_ok", "x_hi", "x_lo", "sq_ok", "part_ok", "sum_ok", "st2_mm", "mean2_ok", "msq_ok", "var2_ok",
             "std2", "r2_ok", "g_mm", "rcol_mm", "rc_ok", "sc_ok", "low_ok", "low_t", "arhs_ok", "arow_ok", "main_mm", "out_mm", "ev_ok", "x2_ok",
             "st3_mm", "mean3_ok", "var3_ok", "std3", "r3_ok", "cent_ok", "xn3_ok", "cmax_ok", "smax_ok", "csum_ok", "xsum_ok",
             "feat_ok", "red_ok", "row_out", "bn_ok", "mv_ok", "std_ok", "init_ok", "guess_ok", "off_ok", "sign_ok", "fin_ok", "ind_ok", "cut_ok", "top_ok", "kth_ok", "mask_ok", "bad_ok"))
        block = stack.enter_context(nc.Block())
        SC_STEPS = 6

        def pairs(eng, pair, tail):
            pair(0, 0, 0)
            pair(1, 1, 0)
            if NPAIR > 4:
                with eng.Fori(1, NPAIR // 2 - 1) as it:
                    pair(2 * it, 0, it)
                    pair(2 * it + 1, 1, it)
            if NPAIR > 2:
                pair(NPAIR - 2, 0, NPAIR // 2 - 1)
                pair(NPAIR - 1, 1, NPAIR // 2 - 1)
            tail(NPAIR, 0, NPAIR // 2)

        least = lambda i, n: not isinstance(i, int) or i >= n
        first = lambda i: not least(i, 1)
        is_last = lambda i: isinstance(i, int) and i == NPAIR - 1
        ended = lambda i: isinstance(i, int) and i == NPAIR

        def square_at(i, n):
            at = 2 * NCH * i + NCH - 1 + n
            return at - (NCH if ended(i) else 2 if is_last(i) and n == 5 else 0)

        @block.sync
        def _(sp):
            sp.dma_start(g32, gateT.rearrange("(k p) r -> p k r", p=P)).then_inc(k_in, 16)
            sp.dma_start(gb[:], gate_b.partition_broadcast(P)).then_inc(k_in, 16)
            with nc.allow_non_contiguous_dma(reason="a column of biases per output tile, once"):
                sp.dma_start(bcol[:], bias.rearrange("(o p) -> p o", p=P)).then_inc(k_in, 16)
            sp.dma_start(ident[:], ident_d).then_inc(k_in, 16)
            sp.dma_start(aug[:], lora_aug).then_inc(k_in, 16)

            for c in range(NCH):
                k = slice(c * CK, (c + 1) * CK)
                sp.dma_start(xr[0][:, k, :], x1[0, :, k, :]).then_inc(x_in[0][c], 16)

            def pair(i, s, u):
                for o in range(OT):
                    if o >= WR or not first(i):
                        sp.wait_ge(main_mm, OT * i + (o - WR + 1))
                    sp.dma_start(ws[o % WR][:], w_split[o, :, :, :].rearrange("p k (a n) -> p k a n", a=2)).then_inc(w_in[o % WR], 16)
            pairs(sp, pair, lambda i, s, u: None)

        @block.gpsimd
        def _(pool):
            pool.memset(ones[:], 1.0).then_inc(k_set, 1)
            pool.memset(minus1[:], -1.0).then_inc(k_set, 1)
            pool.memset(eps[:, 0:1], EPS).then_inc(k_set, 1)
            pool.memset(eps[:, 1:2], EPS * W_SCALE ** 2).then_inc(k_set, 1)
            pool.memset(bad[:], 0.0).then_inc(k_set, 1)
            for w in range(WINDOW):
                pool.memset(rank[:, w:w + 1], w + 1.0).then_inc(k_set, 1)

            def load_ctx(i, n):
                pool.dma_start(ct[n % CR][:], ctxT[bass.ds(i, 1), :, n, :].rearrange("a p t -> p (a t)")).then_inc(c_in[n % CR], 16)
            for n in range(CR):
                load_ctx(0, n)

            def centre(i, s, c):
                n_mean = counted(pool, i)
                pool.wait_ge(k_set, 5 + WINDOW)
                pool.wait_ge(mean3_ok, n_mean)
                v = xr[s][:, c * CK:(c + 1) * CK, :]
                pool.tensor_tensor(v, v, mean3[:].unsqueeze(1).broadcast_to([P, CK, T]), ALU.subtract).then_inc(cent_ok, 1)

            def cut_tile(i, o):
                g, n = (o // GT - 1) % 2, (o - GT) % KT
                at = KT * i + o - GT
                n_fin, n_top, n_ind = counted(pool, 2 * (NGRP * i + o // GT)), counted(pool, 6 * (at - 1)), counted(pool, 2 * at + 2)
                pool.wait_ge(k_set, 5 + WINDOW)
                pool.wait_ge(fin_ok, n_fin)
                if o >= GT + 2 or not first(i):
                    pool.wait_ge(top_ok, n_top)
                for bb in range(2):
                    u = 2 * (n % GT) + bb
                    pool.tensor_scalar(cut[n % 2][:, bb, :], ct[n % CR][:, bb * L:(bb + 1) * L], limit[g][:, u:u + 1], NEG, ALU.is_gt, ALU.mult).then_inc(ind_ok, 1)
                pool.wait_ge(k_set, 5 + WINDOW)
                pool.wait_ge(ind_ok, n_ind)
                c = cut[n % 2][:].rearrange("p b t -> p (b t)")
                pool.tensor_tensor(c, c, ct[n % CR][:], ALU.add).then_inc(cut_ok, 1)

            def step(i, s, o):
                if not first(i) and 1 <= o <= NCH:
                    centre(i, 1 - s, o - 1)
                if (o >= GT or not first(i)) and not (ended(i) and o >= GT):
                    cut_tile(i, o)
                    n = (o + GT) % KT
                    if not (o + GT >= KT and is_last(i)) and not ended(i):
                        n_mask = counted(pool, 2 * (KT * i + o - GT + 1))
                        pool.wait_ge(k_set, 5 + WINDOW)
                        pool.wait_ge(mask_ok, n_mask)
                        load_ctx(i + (o + GT) // KT, n)

            def pair(i, s, u):
                for o in range(OT):
                    step(i, s, o)

            def tail(i, s, u):
                for o in range(NCH + 1):
                    step(i, s, o)
            pairs(pool, pair, tail)

        @block.tensor
        def _(pe):
            pe.wait_ge(k_in, 80)
            pe.wait_ge(k_set, 4)
            pe.wait_ge(g_lo, 1)
            for part_, g in enumerate((gh, gl)):
                for k in range(KT):
                    mm = pe.matmul(ps_g[0:1, 0:R + NG], minus1[:], g[:, k, :], start=part_ == 0 and k == 0, stop=part_ == 1 and k == KT - 1)
            mm.then_inc(gsum_mm, 1)

            def main(i, o):
                b = o % RING
                pe.wait_ge(w_in[o % WR], 16 * (OT // WR) * i + 16 * (o // WR + 1))
                if o >= RING or not first(i):
                    pe.wait_ge(ev_ok, OT * i + o - RING + 1)
                for k in range(KT):
                    if o == 0 and k % CK == 0:
                        pe.wait_ge(lo_ok, NCH * i + k // CK + 1)
                    for a, x in ((0, xh), (1, xh), (0, xl)):
                        mm = pe.matmul(acc[b][:], ws[o % WR][:, k, a, :], x[:, k, :], start=k == 0 and a == 0 and x is xh, stop=False)
                mm.then_inc(main_mm, 1)

            def correct(i, s, o):
                if o == 0:
                    pe.wait_ge(arhs_ok, i + 1)
                    pe.wait_ge(arow_ok, i + 1)
                pe.matmul(acc[o % RING][:], aug[:, o * P:(o + 1) * P], arhs[:], start=False, stop=True).then_inc(out_mm, 1)

            def stats(red, done):
                pe.matmul(ps_s[:], ones[:], red[:, 0, :], start=True, stop=True)
                pe.matmul(ps_q[:], ones[:], red[:, 1, :], start=True, stop=True).then_inc(done, 1)

            def stats2(i):
                if not first(i):
                    pe.wait_ge(arhs_ok, i)
                if least(i, 2):
                    pe.wait_ge(var3_ok, i - 1)
                    pe.wait_ge(mean3_ok, i - 1)
                pe.wait_ge(sum_ok, 2 * NCH if first(i) else 2 * (square_at(i - 1, 7) + 1))
                stats(red2, st2_mm)

            def stats3(i):
                pe.wait_ge(arhs_ok, NPAIR if ended(i) else i + 1)
                pe.wait_ge(sum_ok, 2 * (square_at(i, 0) + 1))
                stats(red3, st3_mm)

            def gates(i, s):
                pe.wait_ge(mean2_ok, i + 1)
                pe.wait_ge(gsum_ok, 1)
                if not first(i):
                    pe.wait_ge(low_ok, 4 * i)
                for q in range(QT):
                    t = slice(q * P, (q + 1) * P)
                    for k in range(KT):
                        for x, g in ((xh, gh), (xh, gl), (xl, gh)):
                            pe.matmul(raw[:, q, :], x[:, k, t], g[:, k, :], start=k == 0 and x is xh and g is gh, stop=False)
                    mm = pe.matmul(raw[:, q, :], mean2[0:1, t], gsum[:], start=False, stop=True)
                mm.then_inc(g_mm, 1)
                pe.wait_ge(r2_ok, i + 1)
                for q in range(QT):
                    mm = pe.matmul(rcol[:, q:q + 1], r2[s][0:1, q * P:(q + 1) * P], ones[0:1, 0:1], start=True, stop=True)
                mm.then_inc(rcol_mm, 1)

            def pair(i, s, u):
                for o in range(OT):
                    if o > LAG:
                        correct(i, s, o - LAG - 1)
                    main(i, o)
                    if o == 0 and not first(i):
                        stats2(i)
                    if o == 1:
                        gates(i, s)
                    if o == LAG:
                        n_low, n_var = counted(pe, 4 * (i + 1)), counted(pe, i + 1)
                        pe.wait_ge(k_set, 4)
                        pe.wait_ge(var2_ok, n_var)
                        pe.wait_ge(low_ok, n_low)
                        for q in range(QT):
                            mm = pe.transpose(ps_s[0:R, q * P:(q + 1) * P], low[:, q, :], ident[:])
                        mm.then_inc(low_t, 1)
                    if o == LAG + 1 and not first(i):
                        stats3(i)
                for o in range(OT - LAG - 1, OT):
                    correct(i, s, o)
            stats2(0)
            pairs(pe, pair, lambda i, s, u: stats3(i))

        @block.scalar
        def _(act):
            act.wait_ge(k_in, 80)
            act.wait_ge(k_set, 4)
            act.activation(gh[:], g32, ACT.Copy, scale=W_SCALE).then_inc(g_hi, 1)

            def square(at, src, c):
                if isinstance(at, int) and at == 0:
                    act.wait_ge(g_lo, 1)
                else:
                    act.wait_ge(part_ok, at)
                act.activation(sq[:], src[:, c * CK:(c + 1) * CK, :], ACT.Square).then_inc(sq_ok, 1)

            def high(i, s, n_in):
                if not first(i):
                    act.wait_ge(main_mm, OT * i)
                    act.wait_ge(g_mm, i)
                for c in range(NCH):
                    k = slice(c * CK, (c + 1) * CK)
                    act.wait_ge(x_in[s][c], n_in)
                    act.activation(xh[:, k, :], xr[s][:, k, :], ACT.Copy).then_inc(hi_ok, 1)

            def deviation2(i, s):
                act.wait_ge(var2_ok, i + 1)
                act.activation(msq[:], r2[s][:], ACT.Sqrt, bias=eps[:, 1:2], scale=W_SCALE ** 2).then_inc(std2, 1)

            def lora(i, s):
                act.wait_ge(low_t, i + 1)
                if not first(i):
                    act.wait_ge(out_mm, OT * i)
                act.activation(arhs[0:R, :], ps_s[0:R, :], ACT.Copy).then_inc(arhs_ok, 1)

            def deviation3(i):
                act.wait_ge(var3_ok, i)
                if least(i, 2):
                    act.wait_ge(row_out, 32 * (i - 1))
                act.activation(s3[:], r3[:], ACT.Sqrt, bias=eps[:, 0:1]).then_inc(std3, 1)

            def sums(i, s, o):
                for n in range(4 * o, 4 * o + 4):
                    at = UNITS * (i - 1) + n
                    act.wait_ge(cmax_ok, at + 1)
                    if n or least(i, 2):
                        act.wait_ge(csum_ok, at)
                        act.wait_ge(xsum_ok, at)
                    act.activation(unread[:, 0, :], cf[n % 2][:], ACT.Copy, accum_out=fp[:, 1, n % 2, n // 2:n // 2 + 1]).then_inc(csum_ok, 1)
                    act.activation(unread[:, 1, :], xr[s][:, n // 2, (n % 2) * L:(n % 2 + 1) * L], ACT.Copy, accum_out=fp[:, 3, n % 2, n // 2:n // 2 + 1]).then_inc(xsum_ok, 1)
                if o == KT // 2 - 1:
                    act.wait_ge(xsum_ok, UNITS * i)
                    act.wait_ge(smax_ok, UNITS * i)
                    act.activation(feat[:, :, bass.ds(2 * (i - 1), 2), :], fp[:], ACT.Copy).then_inc(feat_ok, 1)

            def count(i, q, n):
                g = NGRP * i + q
                act.wait_ge(guess_ok, COUNTS * g + n + 1)
                for u in range(GU):
                    at = GU * COUNTS * g + GU * n + u
                    if not isinstance(at, int) or at >= 4:
                        act.wait_ge(sign_ok, at - 3)
                    k = GT * q + u // 2
                    act.activation(signs[u % 4][:], ct[k % CR][:, (u % 2) * L:(u % 2 + 1) * L], ACT.Sign, bias=guess[q % 2][:, u:u + 1], accum_out=above[q % 2][:, u:u + 1]).then_inc(sign_ok, 1)

            def stores(i, s):
                act.wait_ge(mask_ok, 2 * KT * i)
                act.wait_ge(xn3_ok, NCH * i)
                act.wait_ge(std3, i)
                act.dma_start(xn3[bass.ds(i - 1, 1), :, :, :].rearrange("a p k t -> p (a k) t"), xr[s][:]).then_inc(x_out[s], 16)
                act.dma_start(masks[bass.ds(i - 1, 1), :, :, :].rearrange("a p k t -> p (a k) t"), mk[s][:]).then_inc(m_out[s], 16)
                act.dma_start(rows3[0:1, bass.ds(i - 1, 1), :].rearrange("r a t -> r (a t)"), mean3[0:1, :]).then_inc(row_out, 16)
                act.dma_start(rows3[1:2, bass.ds(i - 1, 1), :].rearrange("r a t -> r (a t)"), s3[0:1, :]).then_inc(row_out, 16)

            def load_x1(i, s, u, c):
                if not first(i):
                    act.wait_ge(x_out[1 - s], 16 * (u + s))
                    act.wait_ge(xsum_ok, UNITS * (i - 1) + CHUNK_UNITS * (c + 1))
                    act.wait_ge(smax_ok, UNITS * (i - 1) + CHUNK_UNITS * (c + 1))
                k = slice(c * CK, (c + 1) * CK)
                act.dma_start(xr[1 - s][:, k, :], x1[bass.ds(i + 1, 1), :, k, :].rearrange("a p k t -> p (a k) t")).then_inc(x_in[1 - s][c], 16)

            def trail(i, s, o):
                if o == 0:
                    act.wait_ge(x2_ok, OT * i)
                    square(square_at(i, 0), xr[s], NCH - 1)
                if o == 1:
                    deviation3(i)

            def step(i, s, u, o):
                q, r = o // GT, o % GT
                if not first(i):
                    trail(i, 1 - s, o)
                if not is_last(i) and o == 12:
                    high(i + 1, 1 - s, 16 * (u + s + 1))
                if r == 0:
                    act.wait_ge(mv_ok, GU * (NGRP * i + q + 1))
                    act.activation(std[:], mv[:, :, 1], ACT.Sqrt).then_inc(std_ok, 1)
                if r:
                    count(i, q, 2 * r - 1)
                if not first(i) and 2 <= o < 2 + KT // 2:
                    sums(i, 1 - s, o - 2)
                if r < 3:
                    count(i, q, 2 * r)
                if o == 6 and not first(i):
                    stores(i, 1 - s)
                if o in (4, 8, 12):
                    act.wait_ge(x2_ok, OT * i + o)
                    square(square_at(i, {4: 1, 8: 2, 12: 5}[o]), xr[s], o // CK - 1)
                if not is_last(i):
                    if o in (9, 10):
                        for c in (2 * (o - 9), 2 * (o - 9) + 1):
                            load_x1(i, s, u, c)
                    if o in (11, 12):
                        for c in (2 * (o - 11), 2 * (o - 11) + 1):
                            act.wait_ge(x_in[1 - s][c], 16 * (u + s + 1))
                            square(square_at(i, (3, 4, 6, 7)[c]), xr[1 - s], c)
                    if o == 14:
                        deviation2(i + 1, 1 - s)
                    if o == 15:
                        lora(i + 1, 1 - s)

            def pair(i, s, u):
                for o in range(OT):
                    step(i, s, u, o)

            def tail(i, s, u):
                for o in range(2 + KT // 2):
                    trail(i, 1 - s, o)
                    if o >= 2:
                        sums(i, 1 - s, o - 2)
                stores(i, 1 - s)
                act.wait_ge(feat_ok, NPAIR)
                for p in range(2):
                    act.wait_ge(x_out[p], 16 * (NPAIR // 2))
                    act.wait_ge(m_out[p], 16 * (NPAIR // 2))
                act.wait_ge(row_out, 32 * NPAIR)
            for c in range(NCH):
                act.wait_ge(x_in[0][c], 16)
                square(c, xr[0], c)
            high(0, 0, 16)
            act.wait_ge(gsum_mm, 1)
            act.activation(gsum[:], ps_g[0:1, 0:R + NG], ACT.Copy).then_inc(gsum_ok, 1)
            deviation2(0, 0)
            lora(0, 0)
            pairs(act, pair, tail)

        @block.vector
        def _(dve):
            dve.wait_ge(k_in, 80)
            dve.wait_ge(g_hi, 1)
            dve.scalar_tensor_tensor(gl[:], g32, W_SCALE, gh[:], ALU.mult, ALU.subtract).then_inc(g_lo, 1)

            def chunk_sums(at, src, c, red):
                if not isinstance(at, int) or at >= 1:
                    dve.wait_ge(sum_ok, 2 * at)
                dve.tensor_reduce(part[:], src[:, c * CK:(c + 1) * CK, :].rearrange("p k t -> p t k"), AX.X, ALU.add).then_inc(red_ok, 1)
                for which in range(2):
                    if which:
                        dve.wait_ge(sq_ok, at + 1)
                        dve.wait_ge(sum_ok, 2 * at + 1)
                        dve.tensor_reduce(part[:], sq[:].rearrange("p k t -> p t k"), AX.X, ALU.add).then_inc(part_ok, 1)
                        dve.wait_ge(part_ok, at + 1)
                    else:
                        dve.wait_ge(red_ok, at + 1)
                    if c:
                        dve.tensor_tensor(red[:, which, :], red[:, which, :], part[:], ALU.add).then_inc(sum_ok, 1)
                    else:
                        dve.tensor_copy(red[:, which, :], part[:]).then_inc(sum_ok, 1)

            def variance(mean, var, st, mean_ok, m_sq, var_ok, i, n):
                dve.wait_ge(st, i + 1)
                dve.tensor_scalar(mean[:], ps_s[:], 1.0 / D, None, ALU.mult).then_inc(mean_ok, 1)
                dve.wait_ge(mean_ok, i + 1)
                dve.tensor_tensor(msq[:], mean[:], mean[:], ALU.mult).then_inc(m_sq, 1)
                dve.wait_ge(m_sq, n + 1)
                dve.scalar_tensor_tensor(var[:], ps_q[:], 1.0 / D, msq[:], ALU.mult, ALU.subtract).then_inc(var_ok, 1)

            def low_parts(i, s):
                for c in range(NCH):
                    k = slice(c * CK, (c + 1) * CK)
                    dve.wait_ge(hi_ok, NCH * i + c + 1)
                    dve.tensor_tensor(xl[:, k, :], xr[s][:, k, :], xh[:, k, :], ALU.subtract).then_inc(lo_ok, 1)

            def norm2(i, s):
                if not first(i):
                    dve.wait_ge(g_mm, i)
                    dve.wait_ge(arow_ok, i)
                variance(mean2, r2[s], st2_mm, mean2_ok, msq_ok, var2_ok, i, 0 if first(i) else 2 * i - 1)
                dve.wait_ge(std2, i + 1)
                dve.reciprocal(r2[s][:], msq[:]).then_inc(r2_ok, 1)
                if not first(i):
                    dve.wait_ge(out_mm, OT * i)
                dve.tensor_copy(arhs[R:R + 1, :], mean2[R:R + 1, :]).then_inc(arow_ok, 1)

            def gates(i):
                dve.wait_ge(rcol_mm, i + 1)
                dve.tensor_copy(rc[:], rcol).then_inc(rc_ok, 1)
                dve.wait_ge(rc_ok, i + 1)
                n = SC_STEPS * i
                dve.tensor_tensor(sc[:], raw[:, :, R:R + NG], rc[:].unsqueeze(2).broadcast_to([P, QT, NG]), ALU.mult).then_inc(sc_ok, 1)
                dve.wait_ge(sc_ok, n + 1)
                dve.tensor_tensor(sc[:], sc[:], gb[:].unsqueeze(1).broadcast_to([P, QT, NG]), ALU.add).then_inc(sc_ok, 1)
                dve.wait_ge(sc_ok, n + 2)
                dve.tensor_reduce(mx[:], sc[:], AX.X, ALU.max).then_inc(sc_ok, 1)
                dve.wait_ge(sc_ok, n + 3)
                dve.tensor_tensor(nb[:], sc[:], mx[:].unsqueeze(2).broadcast_to([P, QT, NG]), ALU.is_lt).then_inc(sc_ok, 1)
                dve.wait_ge(sc_ok, n + 4)
                for r in (1, 2):
                    dve.tensor_tensor(nb[:, :, r], nb[:, :, r], nb[:, :, r - 1], ALU.mult).then_inc(sc_ok, 1)
                    dve.wait_ge(sc_ok, n + 4 + r)
                if not first(i):
                    dve.wait_ge(low_t, i)
                dve.tensor_copy(low[:, :, 0:RANKS[0]], raw[:, :, 0:RANKS[0]]).then_inc(low_ok, 1)
                for r in range(3):
                    w = RANKS[r + 1] - RANKS[r]
                    dve.tensor_tensor(low[:, :, RANKS[r]:RANKS[r + 1]], raw[:, :, RANKS[r]:RANKS[r + 1]], nb[:, :, r:r + 1].broadcast_to([P, QT, w]), ALU.mult).then_inc(low_ok, 1)

            def moments(i, q):
                g = NGRP * i + q
                ctx = lambda c: ct[(GT * q + c // 2) % CR][:, (c % 2) * L:(c % 2 + 1) * L]
                n_bn = counted(dve, GU * (g + 1))
                for c in range(GU):
                    n = GT * q + c // 2
                    dve.wait_ge(c_in[n % CR], 16 * (KT // CR) * i + 16 * (n // CR + 1))
                    dve.bn_stats(st6[:, c, :], ctx(c)).then_inc(bn_ok, 1)
                dve.wait_ge(k_in, 80)
                dve.wait_ge(bn_ok, n_bn)
                for c in range(GU):
                    dve.bn_aggr(mv[:, c, :], st6[:, c, :]).then_inc(mv_ok, 1)

            def first_guess(i, q):
                g = NGRP * i + q
                dve.wait_ge(std_ok, g + 1)
                dve.tensor_scalar(slope[q % 2][:], std[:], 0.5 / TOKENS_PER_STD, None, ALU.mult).then_inc(init_ok, 1)
                dve.scalar_tensor_tensor(guess[q % 2][:], std[:], -z, mv[:, :, 0], ALU.mult, ALU.subtract).then_inc(guess_ok, 1)

            def move_guess(i, q, n):
                g = NGRP * i + q
                dve.wait_ge(sign_ok, GU * COUNTS * g + GU * (n + 1))
                if n == 0:
                    dve.wait_ge(init_ok, g + 1)
                dve.scalar_tensor_tensor(off[:], above[q % 2][:], AIM, slope[q % 2][:], ALU.subtract, ALU.mult).then_inc(off_ok, 1)
                dve.wait_ge(off_ok, len(MOVES) * g + n + 1)
                dve.wait_ge(guess_ok, COUNTS * g + n + 1)
                dve.scalar_tensor_tensor(guess[q % 2][:], off[:], -MOVES[n], guess[q % 2][:], ALU.mult, ALU.add).then_inc(guess_ok, 1)

            def end_guess(i, q):
                g = NGRP * i + q
                dve.wait_ge(sign_ok, GU * COUNTS * (g + 1))
                if not isinstance(g, int) or g >= 2:
                    dve.wait_ge(cut_ok, GT * (g - 1))
                dve.tensor_scalar(limit[q % 2][:], guess[q % 2][:], -1.0, None, ALU.mult).then_inc(fin_ok, 1)
                dve.tensor_scalar(kth[q % 2][:], above[q % 2][:], -0.5, keep - 0.5 * L, ALU.mult, ALU.add).then_inc(fin_ok, 1)

            def mask_tile(i, s, u, o):
                at = KT * i + o - GT
                n, g = (o - GT) % KT, (o // GT - 1) % 2
                m = mk[s if o >= GT else 1 - s]
                n_cut, n_top = counted(dve, at + 1), counted(dve, 6 * at + 2)
                n_rep, n_all = counted(dve, 6 * at + 4), counted(dve, 6 * at + 6)
                dve.wait_ge(k_in, 80)
                dve.wait_ge(cut_ok, n_cut)
                for b in range(2):
                    dve.max(top[:, b, 0:8], cut[n % 2][:, b, :]).then_inc(top_ok, 1)
                dve.wait_ge(k_in, 80)
                dve.wait_ge(top_ok, n_top)
                for b in range(2):
                    dve.match_replace(cut[n % 2][:, b, :], top[:, b, 0:8], cut[n % 2][:, b, :], NEG).then_inc(top_ok, 1)
                k2 = kth[g][:, 2 * (n % GT):2 * (n % GT) + 2].unsqueeze(2).broadcast_to([P, 2, WINDOW])
                dve.wait_ge(fin_ok, 2 * (NGRP * i + o // GT))
                dve.tensor_tensor(pick[:], rank[:].unsqueeze(1).broadcast_to([P, 2, WINDOW]), k2, ALU.is_equal).then_inc(kth_ok, 1)
                dve.wait_ge(k_in, 80)
                dve.wait_ge(top_ok, n_rep)
                for b in range(2):
                    dve.max(top[:, b, 8:16], cut[n % 2][:, b, :]).then_inc(top_ok, 1)
                dve.wait_ge(top_ok, n_all)
                dve.wait_ge(kth_ok, 3 * at + 1)
                dve.tensor_tensor(pick[:], pick[:], top[:], ALU.mult).then_inc(kth_ok, 1)
                dve.wait_ge(kth_ok, 3 * at + 2)
                dve.tensor_reduce(vk[:], pick[:], AX.X, ALU.add).then_inc(kth_ok, 1)
                dve.wait_ge(kth_ok, 3 * at + 3)
                if o == GT and least(i, 2):
                    dve.wait_ge(m_out[s], 16 * u)
                for b in range(2):
                    dve.tensor_scalar(m[:, n, b * L:(b + 1) * L], ct[n % CR][:, b * L:(b + 1) * L], vk[:, b:b + 1], 0.0, ALU.is_ge, ALU.add, accum_out=kept[:, 2 * n + b:2 * n + b + 1]).then_inc(mask_ok, 1)

            def check_masks(i):
                dve.wait_ge(mask_ok, UNITS * i)
                dve.tensor_scalar(kept[:], kept[:], float(keep), None, ALU.not_equal).then_inc(bad_ok, 1)
                dve.wait_ge(bad_ok, 3 * i - 2)
                dve.tensor_reduce(wrong[:], kept[:], AX.X, ALU.max).then_inc(bad_ok, 1)
                dve.wait_ge(bad_ok, 3 * i - 1)
                dve.tensor_tensor(bad[:], bad[:], wrong[:], ALU.max).then_inc(bad_ok, 1)
                dve.wait_ge(bad_ok, 3 * i)

            def norm3(i):
                if least(i, 2):
                    dve.wait_ge(row_out, 32 * (i - 1))
                    dve.wait_ge(cent_ok, NCH * (i - 1))
                variance(mean3, r3, st3_mm, mean3_ok, msq_ok, var3_ok, i - 1, 2 * i - (1 if ended(i) else 0))
                dve.wait_ge(std3, i)
                dve.reciprocal(r3[:], s3[:]).then_inc(r3_ok, 1)

            def scale3(i, s, c):
                v = xr[s][:, c * CK:(c + 1) * CK, :]
                dve.wait_ge(r3_ok, i)
                dve.wait_ge(cent_ok, NCH * (i - 1) + c + 1)
                dve.tensor_tensor(v, v, r3[:].unsqueeze(1).broadcast_to([P, CK, T]), ALU.mult).then_inc(xn3_ok, 1)

            def features(i, s, n):
                at = UNITS * (i - 1) + n
                n_before, n_now, n_tile = counted(dve, at - 1), counted(dve, at + 1), counted(dve, NCH * (i - 1) + n // CHUNK_UNITS + 1)
                n_pairs, n_at = counted(dve, i - 1), counted(dve, at)
                dve.wait_ge(k_in, 80)
                if n == 0 and least(i, 2):
                    dve.wait_ge(feat_ok, n_pairs)
                dve.wait_ge(xn3_ok, n_tile)
                dve.wait_ge(mask_ok, n_now)
                if n >= 2 or least(i, 2):
                    dve.wait_ge(csum_ok, n_before)
                t = slice((n % 2) * L, (n % 2 + 1) * L)
                c, f = cf[n % 2][:], xr[s][:, n // 2, t]
                dve.tensor_tensor_reduce(out=c, in0=mk[s][:, n // 2, t], in1=f, scale=1.0, scalar=NEG, op0=ALU.mult, op1=ALU.max,
                                         accum_out=fp[:, 0, n % 2, n // 2:n // 2 + 1]).then_inc(cmax_ok, 1)
                dve.wait_ge(k_in, 80)
                dve.wait_ge(cmax_ok, n_now)
                if n or least(i, 2):
                    dve.wait_ge(smax_ok, n_at)
                dve.tensor_tensor_reduce(out=sf[:], in0=f, in1=c, scale=1.0, scalar=NEG, op0=ALU.subtract, op1=ALU.max,
                                         accum_out=fp[:, 2, n % 2, n // 2:n // 2 + 1]).then_inc(smax_ok, 1)

            def trail(i, s, u, o):
                if o == 0:
                    dve.wait_ge(x2_ok, OT * i)
                    chunk_sums(square_at(i, 0), xr[s], NCH - 1, red3)
                if o == 1:
                    norm3(i)
                if 2 <= o < 2 + NCH:
                    scale3(i, s, o - 2)
                if 2 <= o < 2 + KT // 2:
                    for n in range(4 * (o - 2), 4 * (o - 2) + 4):
                        features(i, s, n)

            def step(i, s, u, o):
                q, r = o // GT, o % GT
                if r == 0:
                    moments(i, q)
                if not is_last(i) and o == 12:
                    low_parts(i + 1, 1 - s)
                if not first(i):
                    trail(i, 1 - s, u, o)
                if r in (1, 2):
                    move_guess(i, q, 2 * r - 1)
                at = OT * i + o
                dve.wait_ge(out_mm, at + 1)
                if o >= 1 or not first(i):
                    dve.wait_ge(x2_ok, at)
                dve.tensor_tensor(ev[:], acc[o % RING][:], r2[s][:], ALU.mult).then_inc(ev_ok, 1)
                dve.wait_ge(ev_ok, at + 1)
                dve.scalar_tensor_tensor(xr[s][:, o, :], ev[:], bcol[:, o:o + 1], xr[s][:, o, :], ALU.add, ALU.add).then_inc(x2_ok, 1)
                if r == 0:
                    first_guess(i, q)
                if o >= GT or not first(i):
                    mask_tile(i, s, u, o)
                if o == GT - 1 and not first(i):
                    check_masks(i)
                if o in (4, 8, 12):
                    if o == 4 and not first(i):
                        dve.wait_ge(st3_mm, i)
                    dve.wait_ge(x2_ok, OT * i + o)
                    chunk_sums(square_at(i, {4: 1, 8: 2, 12: 5}[o]), xr[s], o // CK - 1, red3)
                if not is_last(i) and o in (11, 12):
                    for c in (2 * (o - 11), 2 * (o - 11) + 1):
                        if c == 0:
                            dve.wait_ge(st2_mm, i + 1)
                        dve.wait_ge(x_in[1 - s][c], 16 * (u + s + 1))
                        chunk_sums(square_at(i, (3, 4, 6, 7)[c]), xr[1 - s], c, red2)
                if not is_last(i) and o == 14:
                    norm2(i + 1, 1 - s)
                if r < 3:
                    move_guess(i, q, 2 * r)
                else:
                    end_guess(i, q)
                if not is_last(i) and o == 15:
                    gates(i + 1)

            def pair(i, s, u):
                for o in range(OT):
                    step(i, s, u, o)

            def tail(i, s, u):
                for o in range(2 + KT // 2):
                    trail(i, 1 - s, u, o)
                    if o < GT:
                        mask_tile(i, s, u, o)
                check_masks(i)
            for c in range(NCH):
                dve.wait_ge(x_in[0][c], 16)
                chunk_sums(c, xr[0], c, red2)
            low_parts(0, 0)
            norm2(0, 0)
            gates(0)
            pairs(dve, pair, tail)
    nc.clear_and_free_semaphores(sems)
    nc.all_engine_barrier()


def exact_masks_phase(nc, ctxT, xn3, masks, feat, bad, keep):
    NPAIR, _, KT, T = ctxT.shape
    L = T // 2
    NEG = -3.0e38
    FULL, REST = keep // 8, keep % 8
    ROUNDS = FULL + (REST > 0)
    TAKES = 2 * (2 * ROUNDS + (REST > 0))
    FEATURES = 6

    stack = ExitStack()
    sb = lambda name, shape, dt=FP32: stack.enter_context(nc.sbuf_tensor(name, shape, dt))
    sems = []

    def sem(name):
        sems.append(nc.alloc_semaphore(name))
        return sems[-1]
    with stack:
        ones = sb("ones_e", [P, 1])
        flag = sb("flag", [1, 1], mybir.dt.int32)
        c, x = sb("ctx_e", [P, T]), sb("xn3_e", [P, T])
        left = sb("left", [P, T])
        m = sb("mask_e", [P, T], UINT8)
        top = sb("top_e", [P, 8])
        kept, other = sb("kept_e", [P, 2, L]), sb("other_e", [P, 2, L])
        four = sb("four_e", [P, 4, 2])
        any_bad = stack.enter_context(nc.psum_tensor("any_bad", [1, 1], FP32))
        ones_set, flag_mm, flag_ok, c_in, x_in, take_ok, mask_ok, stored, feat_ok, tile_ok = map(sem, (
            "ones_e_set", "flag_mm", "flag_ok", "ctx_e_in", "xn3_e_in", "take_e_ok", "mask_e_ok", "mask_e_out", "feat_e_ok", "tile_e_ok"))
        block = stack.enter_context(nc.Block())

        @block.gpsimd
        def _(pool):
            pool.memset(ones[:], 1.0).then_inc(ones_set, 1)

        @block.tensor
        def _(pe):
            pe.wait_ge(ones_set, 1)
            pe.matmul(any_bad[:], ones[:], bad[:], start=True, stop=True).then_inc(flag_mm, 1)

        @block.sync
        def _(sp):
            sp.wait_ge(flag_ok, 1)
            again = sp.value_load(flag[0:1, 0:1], min_val=0, max_val=P)
            with sp.If(again > 0):
                with sp.Fori(0, NPAIR) as i, sp.Fori(0, KT) as n:
                    tile = lambda ap: ap[bass.ds(i, 1), :, bass.ds(n, 1), :].rearrange("a p k t -> p (a k t)")
                    n_before, n_masks = counted(sp, KT * i + n), counted(sp, 2 * (KT * i + n) + 2)
                    sp.wait_ge(ones_set, 1)
                    sp.wait_ge(tile_ok, n_before)
                    sp.dma_start(c[:], tile(ctxT)).then_inc(c_in, 16)
                    sp.dma_start(x[:], tile(xn3)).then_inc(x_in, 16)
                    sp.wait_ge(ones_set, 1)
                    sp.wait_ge(mask_ok, n_masks)
                    sp.dma_start(tile(masks), m[:]).then_inc(stored, 16)
                sp.wait_ge(stored, 16 * NPAIR * KT)

        @block.vector
        def _(dve):
            dve.wait_ge(flag_mm, 1)
            dve.tensor_copy(flag[:], any_bad[:]).then_inc(flag_ok, 1)
            dve.wait_ge(flag_ok, 1)
            again = dve.value_load(flag[0:1, 0:1], min_val=0, max_val=P)
            with dve.If(again > 0):
                with dve.Fori(0, NPAIR) as i, dve.Fori(0, KT) as n:
                    at = KT * i + n
                    done = TAKES * at
                    n_in = counted(dve, 16 * at + 16)
                    dve.wait_ge(ones_set, 1)
                    dve.wait_ge(c_in, n_in)
                    for b in range(2):
                        t = slice(b * L, (b + 1) * L)
                        src = c[:, t]
                        for r in range(ROUNDS):
                            n_max = counted(dve, done + 1)
                            dve.max(top[:], src).then_inc(take_ok, 1)
                            dve.wait_ge(ones_set, 1)
                            dve.wait_ge(take_ok, n_max)
                            done = done + 1
                            if r == FULL:
                                n_cut = counted(dve, done + 1)
                                dve.memset(top[:, REST:8], NEG).then_inc(take_ok, 1)
                                dve.wait_ge(ones_set, 1)
                                dve.wait_ge(take_ok, n_cut)
                                done = done + 1
                            n_out = counted(dve, done + 1)
                            dve.match_replace(left[:, t], top[:], src, NEG).then_inc(take_ok, 1)
                            dve.wait_ge(ones_set, 1)
                            dve.wait_ge(take_ok, n_out)
                            done = done + 1
                            src = left[:, t]
                    dve.wait_ge(stored, 16 * at)
                    for b in range(2):
                        t = slice(b * L, (b + 1) * L)
                        dve.tensor_scalar(m[:, t], left[:, t], NEG, None, ALU.is_le).then_inc(mask_ok, 1)
                    x2 = x[:].rearrange("p (b t) -> p b t", b=2)
                    dve.wait_ge(mask_ok, 2 * at + 2)
                    dve.wait_ge(x_in, 16 * at + 16)
                    dve.tensor_tensor(kept[:], m[:].rearrange("p (b t) -> p b t", b=2), x2, ALU.mult).then_inc(feat_ok, 1)
                    dve.wait_ge(feat_ok, FEATURES * at + 1)
                    dve.tensor_tensor(other[:], x2, kept[:], ALU.subtract).then_inc(feat_ok, 1)
                    dve.tensor_reduce(four[:, 0, :], kept[:], AX.X, ALU.max).then_inc(feat_ok, 1)
                    dve.tensor_reduce(four[:, 1, :], kept[:], AX.X, ALU.add).then_inc(feat_ok, 1)
                    dve.wait_ge(feat_ok, FEATURES * at + 2)
                    dve.tensor_reduce(four[:, 2, :], other[:], AX.X, ALU.max).then_inc(feat_ok, 1)
                    dve.tensor_reduce(four[:, 3, :], x2, AX.X, ALU.add).then_inc(feat_ok, 1)
                    dve.wait_ge(feat_ok, FEATURES * at + 6)
                    dve.tensor_copy(feat[:, :, bass.ds(2 * i, 2), bass.ds(n, 1)].rearrange("p q b k -> p q (b k)"), four[:]).then_inc(tile_ok, 1)
                    dve.wait_ge(tile_ok, at + 1)
    nc.clear_and_free_semaphores(sems)
    nc.all_engine_barrier()


def channel_gates_phase(nc, feat, conv_w, gamma, beta, shift_d, ident_d, att, keep, L):
    _, _, NB, J = feat.shape
    G = J // 2
    W = 2 * P
    N = NB * G * W
    TAPS = 7
    PAD = TAPS // 2
    assert NB * G == P
    stack = ExitStack()
    sb = lambda name, shape, dt=FP32: stack.enter_context(nc.sbuf_tensor(name, shape, dt))
    sem = lambda name: stack.enter_context(nc.semaphore(name))
    with stack:
        fy = sb("fy", [P, 4, 2, NB, G])
        y = sb("y_pad", [P, 4, W + 2 * PAD])
        z = sb("z_conv", [P, 2, W])
        zz = sb("z_square", [P, W])
        zs, mu, var, rs = sb("z_sum", [P, 2]), sb("z_mu", [P, 2]), sb("z_var", [P, 2]), sb("z_rs", [P, 2])
        cw, gm, bt = sb("cw", [P, 2 * TAPS]), sb("bn_g", [P, 1]), sb("bn_b", [P, 1])
        shift = sb("shift", [P, 2, P])
        ident, ones, eps = sb("ident_b", [P, P]), sb("ones_b", [P, P]), sb("eps_b", [P, 1])
        yt = stack.enter_context(nc.psum_tensor("yt", [P, 4, W], FP32))
        halo = stack.enter_context(nc.psum_tensor("halo", [P, 2, 4, PAD], FP32))
        tot = stack.enter_context(nc.psum_tensor("tot", [P, 4], FP32))
        back = stack.enter_context(nc.psum_tensor("back", [P, 2, 2, P], FP32))
        (k_in, k_set, fy_ok, y_mm, y_ok, halo_mm, halo_ok, tap_ok, sum_ok, mu_mm, mu_ok, cen_ok, sq_ok, var_mm, std_ok,
         rs_ok, sc_ok, bn_ok, sig_ok, back_mm, a2_ok, att_ok) = map(sem, (
             "kb_in", "kb_set", "fy_ok", "y_mm", "y_ok", "halo_mm", "halo_ok", "tap_ok", "z_sum_ok", "mu_mm", "mu_ok", "cen_ok", "zsq_ok", "zvar_mm", "zstd_ok",
             "zrs_ok", "zsc_ok", "zbn_ok", "sig_ok", "back_mm", "a2_ok", "att_ok"))
        block = stack.enter_context(nc.Block())

        @block.sync
        def _(sp):
            sp.dma_start(cw[:], conv_w.rearrange("a c k -> (a c k)").partition_broadcast(P)).then_inc(k_in, 16)
            sp.dma_start(gm[:], gamma.partition_broadcast(P)).then_inc(k_in, 16)
            sp.dma_start(bt[:], beta.partition_broadcast(P)).then_inc(k_in, 16)
            sp.dma_start(shift[:], shift_d).then_inc(k_in, 16)
            sp.dma_start(ident[:], ident_d).then_inc(k_in, 16)

        @block.gpsimd
        def _(pool):
            pool.memset(ones[:], 1.0).then_inc(k_set, 1)
            pool.memset(eps[:], EPS).then_inc(k_set, 1)

        @block.tensor
        def _(pe):
            pe.wait_ge(k_in, 80)
            pe.wait_ge(k_set, 2)
            for q in range(4):
                pe.wait_ge(fy_ok, 5)
                for h in range(2):
                    mm = pe.transpose(yt[:, q, h * P:(h + 1) * P], fy[:, q, h, :, :].rearrange("p b g -> p (b g)"), ident[:])
            mm.then_inc(y_mm, 1)
            pe.wait_ge(y_ok, 1)
            pe.matmul(halo[:, 0, :, :], shift[:, 0, :], y[:, :, W:W + PAD], start=True, stop=True)
            pe.matmul(halo[:, 1, :, :], shift[:, 1, :], y[:, :, PAD:2 * PAD], start=True, stop=True).then_inc(halo_mm, 1)
            pe.wait_ge(sum_ok, 1)
            pe.matmul(tot[:, 0:2], ones[:], zs[:], start=True, stop=True).then_inc(mu_mm, 1)
            pe.wait_ge(sq_ok, 2)
            pe.matmul(tot[:, 2:4], ones[:], var[:], start=True, stop=True).then_inc(var_mm, 1)
            pe.wait_ge(sig_ok, 1)
            for c in range(2):
                for h in range(2):
                    mm = pe.transpose(back[:, c, h, :], z[:, c, h * P:(h + 1) * P], ident[:])
            mm.then_inc(back_mm, 1)

        @block.scalar
        def _(act):
            act.wait_ge(k_set, 2)
            act.wait_ge(y_mm, 1)
            act.activation(y[:, :, PAD:PAD + W], yt[:], ACT.Copy).then_inc(y_ok, 1)
            for c in range(2):
                act.wait_ge(cen_ok, c + 1)
                if c:
                    act.wait_ge(sq_ok, c)
                act.activation(zz[:], z[:, c, :], ACT.Square, accum_out=var[:, c:c + 1]).then_inc(sq_ok, 1)
            act.wait_ge(var_mm, 1)
            act.activation(rs[:], tot[:, 2:4], ACT.Sqrt, bias=eps[:], scale=1.0 / N).then_inc(std_ok, 1)
            act.wait_ge(bn_ok, 4)
            act.activation(z[:], z[:], ACT.Sigmoid).then_inc(sig_ok, 1)

        @block.vector
        def _(dve):
            dve.wait_ge(k_in, 80)
            split = lambda q: feat[:, q, :, :].rearrange("p b (g h) -> p h b g", h=2)
            dve.tensor_copy(fy[:, 0, :, :, :], split(0)).then_inc(fy_ok, 1)
            dve.tensor_scalar(fy[:, 1, :, :, :], split(1), 1.0 / keep, None, ALU.mult).then_inc(fy_ok, 1)
            dve.tensor_copy(fy[:, 2, :, :, :], split(2)).then_inc(fy_ok, 1)
            dve.tensor_tensor(fy[:, 3, :, :, :], split(3), split(1), ALU.subtract).then_inc(fy_ok, 1)
            dve.wait_ge(fy_ok, 4)
            dve.tensor_scalar(fy[:, 3, :, :, :], fy[:, 3, :, :, :], 1.0 / (L - keep), None, ALU.mult).then_inc(fy_ok, 1)
            dve.wait_ge(halo_mm, 1)
            dve.tensor_copy(y[:, :, 0:PAD], halo[:, 0, :, :]).then_inc(halo_ok, 1)
            dve.tensor_copy(y[:, :, PAD + W:], halo[:, 1, :, :]).then_inc(halo_ok, 1)
            dve.wait_ge(halo_ok, 2)
            for tap in range(2 * TAPS):
                ch, k = tap // TAPS, tap % TAPS
                for c in range(2):
                    src, w = y[:, 2 * c + ch, k:k + W], cw[:, tap:tap + 1]
                    if tap == 0:
                        dve.tensor_scalar(z[:, c, :], src, w, None, ALU.mult).then_inc(tap_ok, 1)
                    else:
                        dve.wait_ge(tap_ok, 2 * (tap - 1) + c + 1)
                        dve.scalar_tensor_tensor(z[:, c, :], src, w, z[:, c, :], ALU.mult, ALU.add).then_inc(tap_ok, 1)
            dve.wait_ge(tap_ok, 4 * TAPS)
            dve.tensor_reduce(zs[:], z[:], AX.X, ALU.add).then_inc(sum_ok, 1)
            dve.wait_ge(mu_mm, 1)
            dve.tensor_scalar(mu[:], tot[:, 0:2], 1.0 / N, None, ALU.mult).then_inc(mu_ok, 1)
            dve.wait_ge(mu_ok, 1)
            for c in range(2):
                dve.tensor_scalar(z[:, c, :], z[:, c, :], mu[:, c:c + 1], None, ALU.subtract).then_inc(cen_ok, 1)
            dve.wait_ge(std_ok, 1)
            dve.reciprocal(rs[:], rs[:]).then_inc(rs_ok, 1)
            dve.wait_ge(rs_ok, 1)
            dve.tensor_scalar(rs[:], rs[:], gm[:], None, ALU.mult).then_inc(sc_ok, 1)
            dve.wait_ge(sc_ok, 1)
            dve.wait_ge(sq_ok, 2)
            for c in range(2):
                dve.tensor_scalar(z[:, c, :], z[:, c, :], rs[:, c:c + 1], bt[:], ALU.mult, ALU.add).then_inc(bn_ok, 1)
            for c in range(2):
                dve.wait_ge(bn_ok, c + 1)
                dve.tensor_scalar(z[:, c, :], z[:, c, :], 0.0, None, ALU.max).then_inc(bn_ok, 1)
            dve.wait_ge(back_mm, 1)
            dve.tensor_copy(att[:, 1, :, :, :].rearrange("p h b g -> p h (b g)"), back[:, 1, :, :]).then_inc(a2_ok, 1)
            dve.wait_ge(a2_ok, 1)
            dve.tensor_tensor(att[:, 0, :, :, :].rearrange("p h b g -> p h (b g)"), back[:, 0, :, :], att[:, 1, :, :, :].rearrange("p h b g -> p h (b g)"), ALU.subtract).then_inc(att_ok, 1)
            dve.wait_ge(att_ok, 1)


def experts_phase(nc, xn3, rows3, masks, att, routerT, router_b, expert_b, tail_rows, ident_d, out):
    NPAIR, _, KT, T = xn3.shape
    L = T // 2
    D = KT * P
    QT = T // P
    E = routerT.shape[1]
    A = E + 2
    NCH = 4
    CK = KT // NCH
    TOP = 8
    RING = 4
    STEPS = 14 + 2 * QT

    stack = ExitStack()
    sb = lambda name, shape, dt=FP32: stack.enter_context(nc.sbuf_tensor(name, shape, dt))
    pb = lambda name, shape: stack.enter_context(nc.psum_tensor(name, shape, FP32))
    sem = lambda name: stack.enter_context(nc.semaphore(name))
    with stack:
        xr = [sb(f"x3_{i}", [P, KT, T]) for i in range(2)]
        mk = [sb(f"mk3_{i}", [P, KT, T], UINT8) for i in range(2)]
        m3 = [sb(f"m3_{i}", [P, T]) for i in range(2)]
        s3 = [sb(f"s3_{i}", [P, T]) for i in range(2)]
        gc = [sb(f"gc{i}", [P, CK, T]) for i in range(NCH)]
        sq = [sb(f"sq3_{i}", [P, CK, T]) for i in range(2)]
        ost = [sb(f"ost{i}", [P, CK, T]) for i in range(NCH)]
        rt = sb("rt", [P, KT, A])
        rsq = sb("rsq", [P, A])
        eb = sb("eb", [A, D])
        pick = sb("pick", [A, P])
        rb, rsum = sb("rb", [P, E]), sb("rsum", [P, E])
        ident, ones, eps = sb("ident3", [P, P]), sb("ones3", [P, P]), sb("eps3", [P, 1])
        lgs, wds = sb("lgs", [A, T]), [sb(f"wds{i}", [A, T]) for i in range(2)]
        a1 = [sb(f"a1_{i}", [P, T]) for i in range(2)]
        mean, msq, r4 = sb("mean4", [P, QT]), sb("msq4", [P, QT]), sb("r4", [P, QT])
        mx, ws, rw = sb("mx4", [P, QT]), sb("ws4", [P, QT]), sb("rw4", [P, QT])
        lt, sc, lm = sb("lt", [P, QT, E]), sb("sc4", [P, QT, E]), sb("lm", [P, QT, E])
        top = sb("top4", [P, QT, TOP])
        wd = sb("wd", [P, QT, A])
        lg, tr, wt, ab = pb("lg", [P, 512]), pb("tr", [P, 512]), pb("wt3", [P, 512]), pb("ab", [P, 512])
        po = [pb(f"po{i}", [P, T]) for i in range(RING)]
        raw = tr[:, 0:QT * A].rearrange("p (q e) -> p q e", q=QT)

        x_in = [[sem(f"x3_in{i}_{c}") for c in range(NCH)] for i in range(2)]
        mk_in, row_in = [sem(f"mk3_in{i}") for i in range(2)], [sem(f"rows_in{i}") for i in range(2)]
        stored = [sem(f"out_stored{i}") for i in range(NCH)]
        (k_in, k_set, rsum_mm, rsum_ok, g_ok, u_ok, v_ok, x3_ok, sq_ok, x_mm, lg_mm, lg_ok, tr_mm, step_ok, var_ok, std_ok, arg_ok, exp_ok, wd_ok,
         wt_mm, wds_ok, ab_mm, a1_ok, prod_ok, bias_mm, out_ok) = map(sem, (
             "k3_in", "k3_set", "rsum_mm", "rsum_ok", "g3_ok", "u3_ok", "v3_ok", "x3_ok", "sq3_ok", "x3_mm", "lg_mm", "lg_ok", "tr_mm", "step_ok", "var4_ok", "std4_ok", "arg_ok", "exp_ok", "wd_ok",
             "wt3_mm", "wds_ok", "ab_mm", "a1_ok", "prod_ok", "bias_mm", "out_ok"))
        block = stack.enter_context(nc.Block())

        def pairs(eng, pair, tail):
            pair(0, 0, 0)
            pair(1, 1, 0)
            if NPAIR > 4:
                with eng.Fori(1, NPAIR // 2 - 1) as it:
                    pair(2 * it, 0, it)
                    pair(2 * it + 1, 1, it)
            if NPAIR > 2:
                pair(NPAIR - 2, 0, NPAIR // 2 - 1)
                pair(NPAIR - 1, 1, NPAIR // 2 - 1)
            tail()

        is_last = lambda i: isinstance(i, int) and i == NPAIR - 1
        least = lambda i, n: not isinstance(i, int) or i >= n

        @block.sync
        def _(sp):
            sp.dma_start(rt[:, :, 0:E], routerT.rearrange("(k p) e -> p k e", p=P)).then_inc(k_in, 16)
            sp.dma_start(rb[:], router_b.partition_broadcast(P)).then_inc(k_in, 16)
            sp.dma_start(eb[0:E, :], expert_b).then_inc(k_in, 16)
            sp.dma_start(eb[E:A, :], tail_rows[:, 0:D]).then_inc(k_in, 16)
            sp.dma_start(pick[E:A, :], tail_rows[:, D:D + P]).then_inc(k_in, 16)
            sp.dma_start(ident[:], ident_d).then_inc(k_in, 16)

            def store(i, c):
                sp.dma_start(out[bass.ds(i, 1), :, c * CK:(c + 1) * CK, :].rearrange("a p k t -> p (a k) t"), ost[c][:]).then_inc(stored[c], 16)

            def load_masks(i, s):
                sp.dma_start(mk[s][:], masks[bass.ds(i, 1), :, :, :].rearrange("a p k t -> p (a k) t")).then_inc(mk_in[s], 16)
                sp.dma_start(s3[s][:], rows3[1:2, bass.ds(i, 1), :].rearrange("r a t -> (r a t)").partition_broadcast(P)).then_inc(row_in[s], 16)
                sp.dma_start(m3[s][:], rows3[0:1, bass.ds(i, 1), :].rearrange("r a t -> (r a t)").partition_broadcast(P)).then_inc(row_in[s], 16)
            load_masks(0, 0)

            def pair(i, s, u):
                for c in range(NCH):
                    k = slice(c * CK, (c + 1) * CK)
                    if least(i, 2):
                        n_used = counted(sp, KT * (i - 2) + CK * (c + 1))
                        sp.wait_ge(k_in, 96)
                        sp.wait_ge(prod_ok, n_used)
                    sp.dma_start(xr[s][:, k, :], xn3[bass.ds(i, 1), :, k, :].rearrange("a p k t -> p (a k) t")).then_inc(x_in[s][c], 16)
                for c in range(NCH):
                    if least(i, 2):
                        n_out = counted(sp, KT * (i - 2) + CK * (c + 1))
                        sp.wait_ge(k_in, 96)
                        sp.wait_ge(out_ok, n_out)
                        store(i - 2, c)
                if not is_last(i):
                    if least(i, 1):
                        n_x3 = counted(sp, NCH * i)
                        sp.wait_ge(k_in, 96)
                        sp.wait_ge(x3_ok, n_x3)
                    load_masks(i + 1, 1 - s)

            def tail():
                for i in (NPAIR - 2, NPAIR - 1):
                    for c in range(NCH):
                        sp.wait_ge(out_ok, KT * i + CK * (c + 1))
                        store(i, c)
                for c in range(NCH):
                    sp.wait_ge(stored[c], 16 * NPAIR)
            pairs(sp, pair, tail)

        @block.gpsimd
        def _(pool):
            pool.memset(ones[:], 1.0).then_inc(k_set, 1)
            pool.memset(eps[:], EPS).then_inc(k_set, 1)
            pool.memset(rt[:, :, E:E + 1], 1.0).then_inc(k_set, 1)
            pool.memset(rt[:, :, E + 1:A], 0.0).then_inc(k_set, 1)
            pool.memset(rsq[:, 0:E + 1], 0.0).then_inc(k_set, 1)
            pool.memset(rsq[:, E + 1:A], 1.0).then_inc(k_set, 1)
            pool.memset(pick[0:E, :], 0.0).then_inc(k_set, 1)

            def products(i, s, c):
                pool.wait_ge(a1_ok, i)
                if least(i, 2):
                    pool.wait_ge(stored[c], 16 * (i - 1))
                for k in range(c * CK, (c + 1) * CK):
                    pool.tensor_tensor(ost[c][:, k - c * CK, :], xr[s][:, k, :], a1[s][:], ALU.mult).then_inc(prod_ok, 1)

            def add_deviation(i, s, c):
                pool.wait_ge(g_ok, NCH * i + c + 1)
                pool.tensor_tensor(gc[c][:], gc[c][:], s3[s][:].unsqueeze(1).broadcast_to([P, CK, T]), ALU.add).then_inc(u_ok, 1)
            pool.wait_ge(row_in[0], 32)
            for c in range(NCH):
                add_deviation(0, 0, c)

            def pair(i, s, u):
                for c in range(NCH):
                    if least(i, 1):
                        products(i, 1 - s, c)
                    if not is_last(i):
                        if c == 0:
                            pool.wait_ge(row_in[1 - s], 32 * (u + s + 1))
                        add_deviation(i + 1, 1 - s, c)

            def tail():
                for c in range(NCH):
                    products(NPAIR, 1, c)
            pairs(pool, pair, tail)

        @block.tensor
        def _(pe):
            pe.wait_ge(k_in, 96)
            pe.wait_ge(k_set, 7)
            for k in range(KT):
                mm = pe.matmul(tr[:, 0:E], ones[:], rt[:, k, 0:E], start=k == 0, stop=k == KT - 1)
            mm.then_inc(rsum_mm, 1)

            def biases(i, s, c):
                for k in range(c * CK, (c + 1) * CK):
                    if k < RING and least(i, 2):
                        pe.wait_ge(out_ok, KT * (i - 1) + k - RING + 1)
                    elif k >= RING:
                        pe.wait_ge(out_ok, KT * (i - 1) + k - RING + 1)
                    if k == 0:
                        pe.wait_ge(wds_ok, i)
                    pe.matmul(po[k % RING][:], eb[:, k * P:(k + 1) * P], wds[s][:], start=True, stop=True).then_inc(bias_mm, 1)

            def logits(i, s, c):
                pe.wait_ge(x3_ok, NCH * i + c + 1)
                for k in range(c * CK, (c + 1) * CK):
                    pe.matmul(lg[0:A, :], rt[:, k, :], xr[s][:, k, :], start=k == 0, stop=False)

            def squares(i, c):
                pe.wait_ge(sq_ok, NCH * i + c + 1)
                for k in range(CK):
                    mm = pe.matmul(lg[0:A, :], rsq[:], sq[c % 2][:, k, :], start=False, stop=c == NCH - 1 and k == CK - 1)
                mm.then_inc(lg_mm if c == NCH - 1 else x_mm, 1)

            def weights(i, s):
                pe.wait_ge(wd_ok, i + 1)
                if least(i, 1):
                    pe.wait_ge(wds_ok, i)
                for q in range(QT):
                    mm = pe.transpose(wt[0:A, q * P:(q + 1) * P], wd[:, q, :], ident[:])
                mm.then_inc(wt_mm, 1)
                pe.wait_ge(wds_ok, i + 1)
                if least(i, 1):
                    pe.wait_ge(a1_ok, i)
                pe.matmul(ab[:], pick[:], wds[s][:], start=True, stop=True).then_inc(ab_mm, 1)

            def pair(i, s, u):
                if least(i, 1):
                    biases(i, 1 - s, 0)
                    pe.wait_ge(lg_ok, i)
                logits(i, s, 0)
                for c in range(1, NCH):
                    logits(i, s, c)
                    squares(i, c - 1)
                squares(i, NCH - 1)
                if least(i, 1):
                    biases(i, 1 - s, 1)
                pe.wait_ge(lg_ok, i + 1)
                if least(i, 1):
                    pe.wait_ge(wd_ok, i)
                else:
                    pe.wait_ge(rsum_ok, 1)
                for q in range(QT):
                    mm = pe.transpose(raw[:, q, :], lgs[:, q * P:(q + 1) * P], ident[0:A, 0:A])
                mm.then_inc(tr_mm, 1)
                if least(i, 1):
                    biases(i, 1 - s, 2)
                    biases(i, 1 - s, 3)
                weights(i, s)

            def tail():
                for c in range(NCH):
                    biases(NPAIR, 1, c)
            pairs(pe, pair, tail)

        @block.scalar
        def _(act):
            act.wait_ge(k_set, 7)
            act.wait_ge(rsum_mm, 1)
            act.activation(rsum[:], tr[:, 0:E], ACT.Copy).then_inc(rsum_ok, 1)

            def gates(i, s, c):
                if least(i, 1):
                    act.wait_ge(x3_ok, NCH * (i - 1) + c + 1)
                for k in range(c * CK, (c + 1) * CK):
                    for bb in range(2):
                        b = 2 * i + bb
                        t = slice(bb * L, (bb + 1) * L)
                        g = act.activation(gc[c][:, k - c * CK, t], mk[s][:, k, t], ACT.Identity, bias=att[:, 1, k % 2, bass.ds(b, 1), k // 2], scale=att[:, 0, k % 2, bass.ds(b, 1), k // 2])
                g.then_inc(g_ok, 1)

            def squares(i, s, c):
                act.wait_ge(x3_ok, NCH * i + c + 1)
                if c >= 2:
                    act.wait_ge(x_mm, (NCH - 1) * i + c - 1)
                elif least(i, 1):
                    act.wait_ge(lg_mm, i)
                act.activation(sq[c % 2][:], xr[s][:, c * CK:(c + 1) * CK, :], ACT.Square).then_inc(sq_ok, 1)

            def weights(i, s):
                act.wait_ge(var_ok, i + 1)
                act.activation(r4[:], r4[:], ACT.Sqrt, bias=eps[:]).then_inc(std_ok, 1)
                act.wait_ge(arg_ok, i + 1)
                act.activation(sc[:], lt[:], ACT.Exp).then_inc(exp_ok, 1)
                act.wait_ge(wt_mm, i + 1)
                if least(i, 2):
                    act.wait_ge(bias_mm, KT * (i - 1))
                act.activation(wds[s][:], wt[0:A, :], ACT.Copy).then_inc(wds_ok, 1)
                act.wait_ge(ab_mm, i + 1)
                if least(i, 2):
                    act.wait_ge(prod_ok, KT * (i - 1))
                act.activation(a1[s][:], ab[:], ACT.Identity, bias=ones[:, 0:1]).then_inc(a1_ok, 1)

            def pair(i, s, u):
                for c in range(NCH):
                    squares(i, s, c)
                    if not is_last(i):
                        if c == 0:
                            act.wait_ge(mk_in[1 - s], 16 * (u + s + 1))
                        gates(i + 1, 1 - s, c)
                act.wait_ge(lg_mm, i + 1)
                if least(i, 1):
                    act.wait_ge(tr_mm, i)
                act.activation(lgs[:], lg[0:A, :], ACT.Copy).then_inc(lg_ok, 1)
                weights(i, s)
            act.wait_ge(mk_in[0], 16)
            for c in range(NCH):
                gates(0, 0, c)
            pairs(act, pair, lambda: None)

        @block.vector
        def _(dve):
            dve.wait_ge(k_in, 96)

            def x3(i, s, u, c):
                v = xr[s][:, c * CK:(c + 1) * CK, :]
                dve.wait_ge(u_ok, NCH * i + c + 1)
                dve.wait_ge(x_in[s][c], 16 * (u + 1))
                dve.tensor_tensor(gc[c][:], gc[c][:], v, ALU.mult).then_inc(v_ok, 1)
                dve.wait_ge(v_ok, NCH * i + c + 1)
                if c == 0:
                    dve.wait_ge(row_in[s], 32 * (u + 1))
                dve.tensor_tensor(v, gc[c][:], m3[s][:].unsqueeze(1).broadcast_to([P, CK, T]), ALU.add).then_inc(x3_ok, 1)

            def outputs(i, s, c):
                for k in range(c * CK, (c + 1) * CK):
                    n = KT * (i - 1) + k
                    dve.wait_ge(bias_mm, n + 1)
                    dve.wait_ge(prod_ok, n + 1)
                    o = ost[c][:, k - c * CK, :]
                    dve.tensor_tensor(o, o, po[k % RING][:], ALU.add).then_inc(out_ok, 1)

            def routing(i):
                bc = lambda m: m[:].unsqueeze(2).broadcast_to([P, QT, E])
                row = lambda m: m[:].unsqueeze(1).broadcast_to([P, QT, E])
                dve.wait_ge(tr_mm, i + 1)
                n = STEPS * i
                if least(i, 1):
                    dve.wait_ge(wt_mm, i)
                dve.tensor_scalar(mean[:], raw[:, :, E], 1.0 / D, None, ALU.mult).then_inc(step_ok, 1)
                dve.wait_ge(step_ok, n + 1)
                dve.tensor_tensor(msq[:], mean[:], mean[:], ALU.mult).then_inc(step_ok, 1)
                dve.wait_ge(step_ok, n + 2)
                dve.scalar_tensor_tensor(r4[:], raw[:, :, E + 1], 1.0 / D, msq[:], ALU.mult, ALU.subtract).then_inc(var_ok, 1)
                dve.tensor_tensor(lm[:], bc(mean), row(rsum), ALU.mult).then_inc(step_ok, 1)
                dve.wait_ge(step_ok, n + 3)
                dve.tensor_tensor(lt[:], raw[:, :, 0:E], lm[:], ALU.subtract).then_inc(step_ok, 1)
                dve.wait_ge(step_ok, n + 4)
                dve.wait_ge(std_ok, i + 1)
                dve.reciprocal(r4[:], r4[:]).then_inc(step_ok, 1)
                dve.wait_ge(step_ok, n + 5)
                dve.tensor_tensor(lt[:], lt[:], bc(r4), ALU.mult).then_inc(step_ok, 1)
                dve.wait_ge(step_ok, n + 6)
                dve.tensor_tensor(lt[:], lt[:], row(rb), ALU.add).then_inc(step_ok, 1)
                dve.wait_ge(step_ok, n + 7)
                dve.tensor_reduce(mx[:], lt[:], AX.X, ALU.max).then_inc(step_ok, 1)
                dve.wait_ge(step_ok, n + 8)
                dve.tensor_tensor(lt[:], lt[:], bc(mx), ALU.subtract).then_inc(arg_ok, 1)
                dve.wait_ge(exp_ok, i + 1)
                dve.tensor_reduce(mx[:], sc[:], AX.X, ALU.add).then_inc(step_ok, 1)
                dve.wait_ge(step_ok, n + 9)
                dve.reciprocal(mx[:], mx[:]).then_inc(step_ok, 1)
                dve.wait_ge(step_ok, n + 10)
                dve.tensor_tensor(sc[:], sc[:], bc(mx), ALU.mult).then_inc(step_ok, 1)
                n_ready = counted(dve, n + 11)
                dve.wait_ge(k_in, 96)
                dve.wait_ge(step_ok, n_ready)
                for q in range(QT):
                    dve.max(top[:, q, :], sc[:, q, :]).then_inc(step_ok, 1)
                    n_ready = counted(dve, n + 11 + q + 1)
                    dve.wait_ge(k_in, 96)
                    dve.wait_ge(step_ok, n_ready)
                for q in range(QT):
                    dve.scalar_tensor_tensor(wd[:, q, 0:E], sc[:, q, :], top[:, q, TOP - 1:TOP], sc[:, q, :], ALU.is_ge, ALU.mult).then_inc(step_ok, 1)
                    dve.wait_ge(step_ok, n + 11 + QT + q + 1)
                dve.tensor_reduce(ws[:], top[:], AX.X, ALU.add).then_inc(step_ok, 1)
                dve.wait_ge(step_ok, n + 12 + 2 * QT)
                dve.tensor_tensor(rw[:], r4[:], ws[:], ALU.mult).then_inc(step_ok, 1)
                dve.wait_ge(step_ok, n + 13 + 2 * QT)
                dve.tensor_copy(wd[:, :, E + 1], rw[:]).then_inc(step_ok, 1)
                dve.wait_ge(step_ok, n + 14 + 2 * QT)
                dve.scalar_tensor_tensor(wd[:, :, E], mean[:], -1.0, rw[:], ALU.mult, ALU.mult).then_inc(wd_ok, 1)

            def pair(i, s, u):
                for c in range(NCH):
                    x3(i, s, u, c)
                if least(i, 1):
                    for c in range(NCH - 1):
                        outputs(i, 1 - s, c)
                routing(i)
                if least(i, 1):
                    outputs(i, 1 - s, NCH - 1)

            def tail():
                for c in range(NCH):
                    outputs(NPAIR, 1, c)
            pairs(dve, pair, tail)


def autocorrelation_lora_ffn_channel_attention_experts(nc, t):
    NB, L, D = t["x"].shape
    KEEP = int(np.floor(0.6 * L))
    KEEP += KEEP % 2
    R = t["loraT"].shape[0]
    pairs_shape = (NB // 2, P, D // P, 2 * L)
    scratch = lambda name, shape, dt=FP32: nc.dram_tensor(name, shape, dt, kind="Internal").ap()
    x1, xn3 = scratch("x1_pairs", pairs_shape), scratch("xn3_pairs", pairs_shape)
    masks = scratch("mask_pairs", pairs_shape, UINT8)
    rows3 = scratch("rows3", (2, NB // 2, 2 * L))
    w_split = scratch("w_split", (D // P, P, D // P, 2 * P), FP16)
    lora_aug = scratch("lora_aug", (R + 1, D))
    dft = [t[n] for n in ("dft_q", "dft_k", "dft_we", "dft_vo", "dft_wo", "dft_ic", "dft_iz", "identity")]
    split_weights_phase(nc, t["wT"], t["loraT"], w_split, lora_aug)
    attention_phase(nc, t["x"], t["ctx"], t["xT"], dft, x1)
    with nc.sbuf_tensor("feat", [P, 4, NB, D // P], FP32) as feat, nc.sbuf_tensor("bad", [P, 1], FP32) as bad:
        ffn_phase(nc, x1, w_split, lora_aug, t["ffn_b"], t["gateT"], t["gate_b"], t["ctx_pairs"], t["identity"], xn3, rows3, masks, feat, KEEP, bad)
        exact_masks_phase(nc, t["ctx_pairs"], xn3, masks, feat, bad, KEEP)
        with nc.sbuf_tensor("att", [P, 2, 2, NB, D // P // 2], FP32) as att:
            channel_gates_phase(nc, feat, t["conv_w"], t["bn_gamma"], t["bn_beta"], t["neighbours"], t["identity"], att, KEEP, L)
            experts_phase(nc, xn3, rows3, masks, att, t["routerT"], t["router_b"], t["expert_b"], t["tail_rows"], t["identity"], t["out_pairs"])


def two_parts(m):
    high = m.astype(np.float16).astype(np.float64)
    return np.stack([high, (m - high).astype(np.float16)]).astype(np.float32)


def layouts(x, ctx_4096, L0_ffn_W, L0_ffn_b, L0_ffn_A, L0_ffn_B, L0_ffn_gate_w, L0_ffn_gate_b, L1_xattn_conv_w, L1_xattn_bn_gamma,
            L1_xattn_bn_beta, L1_ffn_router_weight, L1_ffn_router_bias, L1_ffn_expert_bias):
    NB, L, D = x.shape
    q, k, we, vo, wo, ic, ie, io = dft_constants(L)
    q, k, we, vo, wo = [two_parts(DFT_SCALE * m) for m in (q, k, we, vo, wo)]
    ic, iz = ic.astype(np.float32), (np.concatenate([ie, io]) / DFT_SCALE).astype(np.float32)
    segments = D // (2 * P)
    neighbours = np.zeros((P, 2, P), np.float32)
    for row in range(P):
        if row % segments:
            neighbours[row - 1, 0, row] = 1.0
        if row % segments != segments - 1:
            neighbours[row + 1, 1, row] = 1.0
    tail_rows = np.zeros((2, D + P), np.float32)
    tail_rows[0, :D] = 1.0
    tail_rows[1, D:] = 1.0
    return dict(
        x=x, ctx=ctx_4096, xT=x.transpose(0, 2, 1),
        ctx_pairs=ctx_4096.reshape(NB // 2, 2, L, D // P, P).transpose(0, 4, 3, 1, 2).reshape(NB // 2, P, D // P, 2 * L),
        wT=L0_ffn_W.T, loraT=L0_ffn_B.T, ffn_b=L0_ffn_b, gateT=np.concatenate([L0_ffn_A, L0_ffn_gate_w]).T, gate_b=L0_ffn_gate_b,
        conv_w=L1_xattn_conv_w, bn_gamma=L1_xattn_bn_gamma, bn_beta=L1_xattn_bn_beta,
        routerT=L1_ffn_router_weight.T, router_b=L1_ffn_router_bias, expert_b=L1_ffn_expert_bias,
        dft_q=q, dft_k=k, dft_we=we, dft_vo=vo, dft_wo=wo, dft_ic=ic, dft_iz=iz,
        identity=np.eye(P, dtype=np.float32), neighbours=neighbours, tail_rows=tail_rows)


def kernel(**inputs):
    import concourse.bacc as bacc
    from concourse.bass_utils import run_bass_kernel_spmd

    nc = bacc.Bacc("TRN2", target_bir_lowering=False, num_devices=1)
    arrays = {n: np.ascontiguousarray(a) for n, a in layouts(**{n: np.asarray(a) for n, a in inputs.items()}).items()}
    t = {n: nc.dram_tensor(n, a.shape, FP32, kind="ExternalInput").ap() for n, a in arrays.items()}
    NB, L, D = arrays["x"].shape
    t["out_pairs"] = nc.dram_tensor("out_pairs", (NB // 2, P, D // P, 2 * L), FP32, kind="ExternalOutput").ap()
    autocorrelation_lora_ffn_channel_attention_experts(nc, t)
    r = run_bass_kernel_spmd(nc, [arrays], core_ids=[0])
    out = r.results[0]["out_pairs"].reshape(NB // 2, P, D // P, 2, L)
    return np.ascontiguousarray(out.transpose(0, 3, 4, 2, 1).reshape(NB, L, D))
```

```python
import math
import numpy as np
import concourse.bass as bass
from concourse import mybir
from concourse.alu_op_type import AluOpType as ALU
from contextlib import ExitStack

FP32 = mybir.dt.float32
FP16 = mybir.dt.float16
BF16 = mybir.dt.bfloat16
UINT8 = mybir.dt.uint8
ACT = mybir.ActivationFunctionType
AX = mybir.AxisListType
P = 128
EPS = 1e-5
DFT_SCALE = 64.0
W_SCALE = 64.0


def dft_constants(L):
    F = L // 2
    t = np.arange(L)[:, None].astype(np.float64)
    f = np.arange(F)[None, :].astype(np.float64)
    alt = (-1.0) ** np.arange(L)
    cos_e, sin_e = np.cos(2 * np.pi * t * f / L), np.sin(2 * np.pi * t * f / L)
    cos_e[:, 0] = alt
    q = np.concatenate([cos_e, sin_e], 1)
    q[:, F] = 0.0
    k = q.copy()
    k[:, F] = 1.0
    k[L - 1, F] = 1.0 + L
    we = q.copy()
    we[:, F] = 1.0
    wo_ = np.pi * t * (2 * f + 1) / L
    wo = np.concatenate([np.cos(wo_), np.sin(wo_)], 1)
    vo = wo.copy()
    vo[L - 1] -= wo.sum(0)
    p = np.arange(L)[None, :].astype(np.float64)
    fc = np.arange(F)[:, None].astype(np.float64)
    ce, se = np.cos(2 * np.pi * fc * p / L), np.sin(2 * np.pi * fc * p / L)
    ic = np.concatenate([2 * ce, -2 * se], 0) / L
    ic[0] = alt / L
    ic[F] = 0.0
    ie = np.concatenate([2 * ce, 2 * se], 0) / (2 * L)
    ie[0] = alt / (2 * L)
    ie[F] = -1.0 / (2 * L)
    a = np.pi * (2 * fc + 1) * p / L
    io = np.concatenate([2 * np.cos(a), 2 * np.sin(a)], 0) / (2 * L)
    return q, k, we, vo, wo, ic, ie, io


def counted(eng, n):
    return n if isinstance(n, int) else eng.snap(eng.to_reg(n))


def attention_phase(nc, x, ctx, xT, dft, x1, x1_sums, wT, w_split, w_sums):
    NB, L, D = x.shape
    TT = L // P
    CW = 512
    CH = D // CW
    CT = CW // P
    TOPK = int(2 * np.log(L))
    STEPS = 2 * CH
    ITS = NB // 2
    LAST = NB * CH
    NEG = -3.0e38
    BW = wT.shape[1] * (wT.shape[0] // P) // LAST
    GB = STEPS // 2
    assert wT.shape[1] == GB * BW
    AFTER_LN, AFTER_S, AFTER_F, AFTER_C, AFTER_T, AFTER_I, AFTER_Q = 1, 2, 3, 4, 5, 6, 7

    stack = ExitStack()
    sb = lambda name, shape, dt=FP32: stack.enter_context(nc.sbuf_tensor(name, shape, dt))
    pb = lambda name, shape: stack.enter_context(nc.psum_tensor(name, shape, FP32))
    sems = []

    def sem(name):
        sems.append(nc.alloc_semaphore(name))
        return sems[-1]
    with stack:
        m_q, m_k, m_we, m_vo, m_wo = (sb("m_" + n, [P, 2, TT, L], FP16) for n in ("q", "k", "we", "vo", "wo"))
        m_ic = sb("m_ic", [P, TT, L])
        m_iz = sb("m_iz", [P, 2 * TT, L])
        ident = sb("ident", [P, P])
        not_slot0 = sb("not_slot0", [P, 1])
        eps = sb("eps", [P, 1])
        xn = [sb(f"xn{i}", [P, TT, D]) for i in range(2)]
        cx = [sb(f"cx{i}", [P, TT, CW]) for i in range(2)]
        xs = [sb(f"xs{i}", [P, 2, TT, CW], FP16) for i in range(2)]
        cs = [sb(f"cs{i}", [P, 2, TT, CW], FP16) for i in range(2)]
        xt = [sb(f"xt{i}", [P, CT, L]) for i in range(2)]
        qf = [sb(f"qf{i}", [P, 2, CW]) for i in range(2)]
        kf = [sb(f"kf{i}", [P, 3, CW]) for i in range(4)]
        vf = [sb(f"vf{i}", [P, 2, CW]) for i in range(4)]
        pr = sb("pr", [P, 4, CW])
        pf = [sb(f"pf{i}", [P, 2, CW]) for i in range(2)]
        co = [sb(f"co{i}", [P, CT, L]) for i in range(2)]
        wk = [sb(f"wk{i}", [P, CT, L]) for i in range(2)]
        top = [sb(f"top{i}", [P, CT, 16]) for i in range(2)]
        nmax = [sb(f"nmax{i}", [P, CT]) for i in range(2)]
        wsum = [sb(f"wsum{i}", [P, CT]) for i in range(2)]
        wrec = [sb(f"wrec{i}", [P, CT]) for i in range(2)]
        ws = sb("wts", [P, 2, TT, CW], FP16)
        zf = [sb(f"zf{i}", [P, 4, CW]) for i in range(2)]
        xo = [sb(f"xo{i}", [P, CT, L]) for i in range(2)]
        sums = [sb(f"x1_sums{i}", [P, 2, L]) for i in range(2)]
        wf = [sb(f"w_f32_{i}", [P, BW]) for i in range(2)]
        wp = sb("w_parts", [P, BW // P, 2, P], FP16)
        wa = sb("w_acc", [P, GB, BW])
        st = sb("st", [P, TT, D // 512, 6])
        mv = sb("mv", [P, TT, 2])
        std = sb("std", [P, TT])
        rstd = sb("rstd", [P, TT])
        nmr = sb("nmr", [P, TT])
        bx, by, bz, bu = (pb(n, [P, 2, 512]) for n in ("bx", "by", "bz", "bu"))

        consts_in = sem("consts_in")
        x_in = [sem(f"x_in{i}") for i in range(2)]
        cx_in = [sem(f"cx_in{i}") for i in range(2)]
        xt_in = [sem(f"xt_in{i}") for i in range(2)]
        x1_out = [sem(f"x1_out{i}") for i in range(2)]
        sums_out = [sem(f"sums_out{i}") for i in range(2)]
        const_set, ln_bn, ln_mv, ln_std, ln_rstd, ln_scale, x_normed = map(sem, (
            "const_set", "ln_bn", "ln_mv", "ln_std", "ln_rstd", "ln_scale", "x_normed"))
        q_mm, k_mm, v_mm, c_mm, t_mm, we_mm, wo_mm, i_mm = map(sem, (
            "q_mm", "k_mm", "v_mm", "c_mm", "t_mm", "we_mm", "wo_mm", "i_mm"))
        q_sb, k_part, k_sb, v_sb, c_sb, wt_sb, e_sb, w_sb = map(sem, (
            "q_sb", "k_part", "k_sb", "v_sb", "c_sb", "wt_sb", "e_sb", "w_sb"))
        p_mul, p_sum, top_a, top_cut, top_b, nmax_ok, w_cut, w_rec, ze_mul, ze_sum, zo_mul, zo_sum, x1_sum = map(sem, (
            "p_mul", "p_sum", "top_a", "top_cut", "top_b", "nmax_ok", "w_cut", "w_rec", "ze_mul", "ze_sum", "zo_mul", "zo_sum", "x1_sum"))
        xh_ok, xl_ok, ch_ok, cl_ok, wl_ok, mats_ok = map(sem, ("xh1_ok", "xl1_ok", "ch_ok", "cl_ok", "wl_ok", "mats_ok"))
        w_in = [sem(f"w0_in{i}") for i in range(2)]
        w_scaled, w_hi, w_lo, w_added, w_out, w_sums_out = map(sem, ("w0_scaled", "w0_hi", "w0_lo", "w0_added", "w0_out", "w0_sums_out"))
        sq1_ok, halves_ok, chunk_ok, added_ok = map(sem, ("sq1_ok", "halves_ok", "chunk_ok", "added_ok"))
        N_CONST = 8
        parts = (m_q, m_k, m_we, m_vo, m_wo)
        staged = [t.rearrange("p b (a n) -> p b a n", n=L) for t in (
            zf[0][:, 0:2, :], zf[0][:, 2:4, :], zf[1][:, 0:2, :], zf[1][:, 2:4, :], pr[:, 0:2, :])]
        block = stack.enter_context(nc.Block())

        def steps(eng, step, drain):
            for k in range(STEPS):
                step(0, k)
            if ITS > 1:
                with eng.Fori(1, ITS) as it:
                    for k in range(STEPS):
                        step(it, k)
            for k in range(drain):
                step(ITS, k)

        def chunk(it, k, lag):
            h = STEPS * it + (k - lag)
            return None if isinstance(h, int) and not 0 <= h < LAST else h

        def batch(it, k):
            b = 2 * it + k // CH
            return None if k % CH or (isinstance(b, int) and b >= NB) else b

        def block_of(it, k, lag):
            at = (k - lag) % STEPS
            return at // 2, 2 * (it + (k - lag) // STEPS) + at % 2

        @block.sync
        def _(sp):
            for tile, m in zip(staged, dft[:5]):
                sp.dma_start(tile, m.rearrange("b (a p) n -> p b a n", p=P)).then_inc(consts_in, 16)
            for tile, m in zip((m_ic, m_iz), dft[5:7]):
                sp.dma_start(tile[:], m.rearrange("(a p) n -> p a n", p=P)).then_inc(consts_in, 16)
            sp.dma_start(ident[:], dft[7]).then_inc(consts_in, 16)

            def split_step(it, k):
                h = chunk(it, k, 0)
                if h is not None:
                    c, r = block_of(it, k, 0)
                    row = counted(sp, r * P)
                    if not isinstance(h, int) or h >= 2:
                        sp.wait_ge(w_added, h - 1)
                    sp.dma_start(wf[k % 2][:], wT[bass.ds(row, P), c * BW:(c + 1) * BW]).then_inc(w_in[k % 2], 16)
                h = chunk(it, k, 2)
                if h is not None:
                    c, r = block_of(it, k, 2)
                    tile = counted(sp, r)
                    sp.wait_ge(w_lo, h + 1)
                    sp.dma_start(w_split[c, bass.ds(tile, 1), :, :, :, :].rearrange("k p j a n -> p (k j a n)"), wp[:].rearrange("p j a n -> p (j a n)")).then_inc(w_out, 16)

            def step(it, k):
                b = batch(it, k)
                if b is not None:
                    if not isinstance(b, int) or b >= 2:
                        sp.wait_ge(xl_ok, CH * (b - 1))
                    sp.dma_start(xn[(k // CH) % 2][:], x[bass.ds(b, 1), :, :].rearrange("a (t p) n -> p (a t) n", p=P)).then_inc(x_in[(k // CH) % 2], 16)
                h = chunk(it, k, 1)
                if h is not None:
                    s = (k - 1) % 2
                    if not isinstance(h, int) or h >= 2:
                        sp.wait_ge(cl_ok, h - 1)
                    c = (k - 1) % CH
                    sp.dma_start(cx[s][:], ctx[bass.ds(2 * it + (k - 1) // CH, 1), :, c * CW:(c + 1) * CW].rearrange("a (t p) n -> p (a t) n", p=P)).then_inc(cx_in[s], 16)
                h = chunk(it, k, AFTER_I)
                if h is not None:
                    s, b = (k - AFTER_I) % 2, counted(sp, 2 * it + (k - AFTER_I) // CH)
                    if not isinstance(h, int) or h >= 2:
                        sp.wait_ge(added_ok, h - 1)
                    c = (k - AFTER_I) % CH
                    sp.dma_start(xt[s][:], xT[bass.ds(b, 1), c * CW:(c + 1) * CW, :].rearrange("a (j p) t -> p (a j) t", p=P)).then_inc(xt_in[s], 16)

            def both_steps(it, k):
                step(it, k)
                split_step(it, k)
            steps(sp, both_steps, AFTER_I)
            sp.wait_ge(w_added, LAST)
            sp.dma_start(w_sums, wa[:].rearrange("p c n -> p (c n)")).then_inc(w_sums_out, 16)
            sp.wait_ge(w_out, 16 * LAST)
            sp.wait_ge(w_sums_out, 16)

        @block.gpsimd
        def _(pool):
            pool.memset(not_slot0[:], 1.0 / DFT_SCALE).then_inc(const_set, 1)
            pool.memset(eps[:], EPS).then_inc(const_set, 1)
            pool.wait_ge(const_set, 2)
            pool.memset(not_slot0[0:1, :], 0.0).then_inc(const_set, 1)

            def step(it, k):
                h = chunk(it, k, AFTER_S)
                if h is not None:
                    kk = k - AFTER_S
                    s, c = kk % 2, kk % CH
                    if not isinstance(h, int) or h >= 2:
                        pool.wait_ge(v_mm, h - 1)
                    pool.wait_ge(xh_ok, h + 1)
                    pool.tensor_tensor(xs[s][:, 1, :, :], xn[(kk // CH) % 2][:, :, c * CW:(c + 1) * CW], xs[s][:, 0, :, :], ALU.subtract).then_inc(xl_ok, 1)
                    pool.wait_ge(ch_ok, h + 1)
                    pool.tensor_tensor(cs[s][:, 1, :, :], cx[s][:], cs[s][:, 0, :, :], ALU.subtract).then_inc(cl_ok, 1)
                h = chunk(it, k, AFTER_I)
                if h is None:
                    return
                s, c = (k - AFTER_I) % 2, (k - AFTER_I) % CH
                n_ready = counted(pool, h + 1)
                pool.wait_ge(const_set, 3)
                pool.wait_ge(x1_sum, n_ready)
                bb = (k - AFTER_I) // CH
                pool.dma_start(x1[bass.ds(it + bb // 2, 1), :, c * CT:(c + 1) * CT, bb % 2 * L:(bb % 2 + 1) * L].rearrange("a p j t -> p (a j) t"), xo[s][:]).then_inc(x1_out[s], 16)

            def sums_step(it, k):
                h = chunk(it, k, AFTER_Q)
                if h is None:
                    return
                kk = k - AFTER_Q
                s, c, bb = kk % 2, kk % CH, kk // CH
                b = 2 * it + bb
                total = sums[bb % 2]
                pool.wait_ge(sq1_ok, h + 1)
                pool.tensor_tensor(xt[s][:, 2:4, :], xt[s][:, 0:2, :], xt[s][:, 2:4, :], ALU.add).then_inc(halves_ok, 1)
                pool.wait_ge(halves_ok, 2 * h + 1)
                pool.tensor_tensor(xt[s][:, 0:2, :], xo[s][:, 0:2, :], xo[s][:, 2:4, :], ALU.add).then_inc(halves_ok, 1)
                both = xt[s][:].rearrange("p (w j) t -> p w j t", w=2)
                pool.wait_ge(halves_ok, 2 * h + 2)
                if c == 0:
                    if not isinstance(b, int) or b >= 2:
                        pool.wait_ge(sums_out[bb % 2], 16 * (it + bb // 2))
                    pool.tensor_tensor(total[:], both[:, :, 0, :], both[:, :, 1, :], ALU.add).then_inc(added_ok, 1)
                else:
                    pool.tensor_tensor(both[:, :, 0, :], both[:, :, 0, :], both[:, :, 1, :], ALU.add).then_inc(chunk_ok, 1)
                    pool.wait_ge(chunk_ok, (CH - 1) * b + c)
                    pool.wait_ge(added_ok, h)
                    pool.tensor_tensor(total[:], total[:], both[:, :, 0, :], ALU.add).then_inc(added_ok, 1)
                if c == CH - 1:
                    n_ready = counted(pool, h + 1)
                    pool.wait_ge(const_set, 3)
                    pool.wait_ge(added_ok, n_ready)
                    pool.dma_start(x1_sums[bass.ds(it + bb // 2, 1), :, :, bb % 2 * L:(bb % 2 + 1) * L].rearrange("a p w t -> p (a w) t"), total[:]).then_inc(sums_out[bb % 2], 16)

            def split_step(it, k):
                h = chunk(it, k, 1)
                if h is None:
                    return
                w = wf[(k - 1) % 2]
                c, r = block_of(it, k, 1)
                pool.wait_ge(w_hi, h + 1)
                pool.tensor_tensor(wp[:, :, 1, :], w[:].rearrange("p (j n) -> p j n", n=P), wp[:, :, 0, :], ALU.subtract).then_inc(w_lo, 1)
                if isinstance(r, int) and r == 0:
                    pool.tensor_copy(wa[:, c, :], w[:]).then_inc(w_added, 1)
                else:
                    if isinstance(h, int) and h == 2 * c + 1:
                        pool.wait_ge(w_added, h)
                    else:
                        pool.wait_ge(w_added, h - 1)
                    pool.tensor_tensor(wa[:, c, :], wa[:, c, :], w[:], ALU.add).then_inc(w_added, 1)

            def both_steps(it, k):
                step(it, k)
                sums_step(it, k)
                split_step(it, k)
            steps(pool, both_steps, AFTER_Q)
            for s in range(2):
                pool.wait_ge(sums_out[s], 16 * (NB // 2))
                pool.wait_ge(x1_out[s], 16 * (LAST // 2))

        @block.tensor
        def _(pe):
            pe.wait_ge(consts_in, 16 * N_CONST)

            pe.wait_ge(mats_ok, len(parts))

            def transform(out, mats, src, done):
                for m in range(2):
                    for a in range(TT):
                        for hm, hx in ((0, 0), (0, 1), (1, 0)):
                            mm = pe.matmul(out[:, m, :], mats[:, hm, a, m * P:(m + 1) * P], src[:, hx, a, :], start=a + hm + hx == 0, stop=a == TT - 1 and hm == 1)
                mm.then_inc(done, 1)

            def step(it, k):
                h = chunk(it, k, AFTER_F)
                if h is not None:
                    kk = k - AFTER_F
                    pe.wait_ge(xl_ok, h + 1)
                    if not isinstance(h, int) or h >= 2:
                        pe.wait_ge(c_sb, h - 1)
                    elif h == 1:
                        pe.wait_ge(q_sb, 1)
                    transform(bx, m_q, xs[kk % 2], q_mm)
                    pe.wait_ge(cl_ok, h + 1)
                    if not isinstance(h, int) or h >= 3:
                        pe.wait_ge(ze_mul, 2 * (h - 2))
                    elif h >= 1:
                        pe.wait_ge(k_sb, h)
                    transform(by, m_k, cs[kk % 2], k_mm)
                    if not isinstance(h, int) or h >= 3:
                        pe.wait_ge(zo_mul, 2 * (h - 2))
                    elif h >= 1:
                        pe.wait_ge(v_sb, h)
                    transform(bz, m_vo, cs[kk % 2], v_mm)
                h = chunk(it, k, AFTER_T)
                if h is not None:
                    s = (k - AFTER_T) % 2
                    pe.wait_ge(w_sb, CT * (h + 1))
                    if not isinstance(h, int) or h >= 2:
                        pe.wait_ge(x1_sum, h - 1)
                    elif h == 1:
                        pe.wait_ge(wl_ok, 1)
                    for a in range(TT):
                        for j in range(CT):
                            mm = pe.transpose(bu[:, a, j * P:(j + 1) * P], wk[s][:, j, a * P:(a + 1) * P], ident[:])
                    mm.then_inc(t_mm, 1)
                h = chunk(it, k, AFTER_C)
                if h is not None:
                    s = (k - AFTER_C) % 2
                    pe.wait_ge(p_sum, 2 * (h + 1))
                    g = chunk(it, k, AFTER_F)
                    if g is not None:
                        pe.wait_ge(q_sb, g + 1)
                    else:
                        pe.wait_ge(q_sb, LAST)
                        pe.wait_ge(c_sb, h)
                    for j in range(CT):
                        for a in range(TT):
                            mm = pe.matmul(bx[:, j // 2, (j % 2) * L:(j % 2 + 1) * L], pf[s][:, a, j * P:(j + 1) * P], m_ic[:, a, :], start=a == 0, stop=a == TT - 1)
                    mm.then_inc(c_mm, 1)
                h = chunk(it, k, AFTER_T)
                if h is not None:
                    g = chunk(it, k, AFTER_F)
                    n = LAST if g is None else g + 1
                    pe.wait_ge(wl_ok, h + 1)
                    if g is None:
                        pe.wait_ge(zo_mul, 2 * h)
                        pe.wait_ge(ze_mul, 2 * h)
                    pe.wait_ge(k_sb, n)
                    transform(by, m_we, ws, we_mm)
                    pe.wait_ge(v_sb, n)
                    transform(bz, m_wo, ws, wo_mm)
                h = chunk(it, k, AFTER_I)
                if h is not None:
                    s = (k - AFTER_I) % 2
                    pe.wait_ge(ze_sum, 2 * (h + 1))
                    pe.wait_ge(zo_sum, 2 * (h + 1))
                    g = chunk(it, k, AFTER_T)
                    pe.wait_ge(wl_ok, LAST if g is None else g + 1)
                    if g is None:
                        pe.wait_ge(x1_sum, h)
                    for j in range(CT):
                        for a in range(2 * TT):
                            mm = pe.matmul(bu[:, j // 2, (j % 2) * L:(j % 2 + 1) * L], zf[s][:, a, j * P:(j + 1) * P], m_iz[:, a, :], start=a == 0, stop=a == 2 * TT - 1)
                    mm.then_inc(i_mm, 1)
            steps(pe, step, AFTER_I)

        @block.scalar
        def _(act):
            act.wait_ge(const_set, 3)
            act.wait_ge(consts_in, 16 * N_CONST)
            for tile, whole in zip(parts, staged):
                act.activation(tile[:], whole, ACT.Copy).then_inc(mats_ok, 1)

            def step(it, k):
                h = chunk(it, k, AFTER_F)
                if h is not None:
                    kk = k - AFTER_F
                    s, s4 = kk % 2, kk % 4
                    act.wait_ge(q_mm, h + 1)
                    if not isinstance(h, int) or h >= 2:
                        act.wait_ge(p_mul, 2 * (h - 1))
                    act.activation(qf[s][:], bx[:], ACT.Copy, scale=1.0 / DFT_SCALE).then_inc(q_sb, 1)
                    act.wait_ge(k_mm, h + 1)
                    if not isinstance(h, int) or h >= 4:
                        act.wait_ge(ze_mul, 2 * (h - 3))
                    act.activation(kf[s4][:, 0, :], by[:, 0, :], ACT.Copy, scale=1.0 / DFT_SCALE).then_inc(k_part, 1)
                    act.activation(kf[s4][:, 2, :], by[:, 0, :], ACT.Copy, scale=1.0 / DFT_SCALE).then_inc(k_part, 1)
                    act.activation(kf[s4][:, 1, :], by[:, 1, :], ACT.Copy, scale=not_slot0[:]).then_inc(k_part, 1)
                    act.wait_ge(k_part, 3 * h + 3)
                    act.activation(kf[s4][0:1, 2, :], by[0:1, 1, :], ACT.Copy, scale=1.0 / DFT_SCALE).then_inc(k_sb, 1)
                    act.wait_ge(v_mm, h + 1)
                    if not isinstance(h, int) or h >= 4:
                        act.wait_ge(zo_mul, 2 * (h - 3))
                    act.activation(vf[s4][:], bz[:], ACT.Copy, scale=1.0 / DFT_SCALE).then_inc(v_sb, 1)
                h = chunk(it, k, AFTER_T)
                if h is not None:
                    act.wait_ge(t_mm, h + 1)
                    if not isinstance(h, int) or h >= 1:
                        act.wait_ge(wo_mm, h)
                    act.activation(ws[:, 0, :, :], bu[:], ACT.Copy).then_inc(wt_sb, 1)
                h = chunk(it, k, AFTER_C)
                if h is not None:
                    s = (k - AFTER_C) % 2
                    act.wait_ge(c_mm, h + 1)
                    if not isinstance(h, int) or h >= 2:
                        act.wait_ge(w_cut, CT * (h - 1))
                    act.activation(co[s][:].rearrange("p (a j) t -> p a (j t)", a=2), bx[:], ACT.Copy).then_inc(c_sb, 1)
                    act.wait_ge(c_sb, h + 1)
                    act.wait_ge(nmax_ok, h + 1)
                    for j in range(CT):
                        act.activation(wk[s][:, j, :], co[s][:, j, :], ACT.Exp, bias=nmax[s][:, j:j + 1]).then_inc(e_sb, 1)
                h = chunk(it, k, AFTER_Q)
                if h is not None:
                    s = (k - AFTER_Q) % 2
                    act.wait_ge(x1_sum, h + 1)
                    act.activation(xt[s][:], xo[s][:], ACT.Square).then_inc(sq1_ok, 1)
                b = batch(it, k - AFTER_LN) if k >= AFTER_LN else None
                if b is not None:
                    act.wait_ge(ln_scale, b + 1)
                    for a in range(TT):
                        tile = xn[((k - AFTER_LN) // CH) % 2][:, a, :]
                        act.activation(tile, tile, ACT.Identity, bias=nmr[:, a:a + 1], scale=rstd[:, a:a + 1]).then_inc(x_normed, 1)
                h = chunk(it, k, AFTER_S)
                if h is not None:
                    kk = k - AFTER_S
                    s, c = kk % 2, kk % CH
                    if not isinstance(h, int) or h >= 2:
                        act.wait_ge(v_mm, h - 1)
                    bb = 2 * it + kk // CH
                    act.wait_ge(x_normed, TT * (bb + 1))
                    act.activation(xs[s][:, 0, :, :], xn[(kk // CH) % 2][:, :, c * CW:(c + 1) * CW], ACT.Copy).then_inc(xh_ok, 1)
                    act.wait_ge(cx_in[s], 16 * (4 * it + kk // 2 + 1))
                    act.activation(cs[s][:, 0, :, :], cx[s][:], ACT.Copy).then_inc(ch_ok, 1)
                h = chunk(it, k, 1)
                if h is not None:
                    w = wf[(k - 1) % 2]
                    act.wait_ge(w_in[(k - 1) % 2], 16 * (4 * it + (k - 1) // 2 + 1))
                    act.activation(w[:], w[:], ACT.Copy, scale=W_SCALE).then_inc(w_scaled, 1)
                    act.wait_ge(w_scaled, h + 1)
                    if not isinstance(h, int) or h >= 1:
                        act.wait_ge(w_out, 16 * h)
                    act.activation(wp[:, :, 0, :], w[:].rearrange("p (j n) -> p j n", n=P), ACT.Copy).then_inc(w_hi, 1)
                h = chunk(it, k, AFTER_C)
                if h is not None:
                    s = (k - AFTER_C) % 2
                    act.wait_ge(w_rec, h + 1)
                    for j in range(CT):
                        act.activation(wk[s][:, j, :], wk[s][:, j, :], ACT.Copy, scale=wrec[s][:, j:j + 1]).then_inc(w_sb, 1)
                b = batch(it, k)
                if b is not None:
                    act.wait_ge(ln_mv, TT * (b + 1))
                    act.activation(std[:], mv[:, :, 1], ACT.Sqrt, bias=eps[:]).then_inc(ln_std, 1)
            steps(act, step, AFTER_Q)

        @block.vector
        def _(dve):
            def products(src, spectrum, scratch, out, mul, added, h):
                dve.tensor_tensor(scratch[:, 0:2, :], src, spectrum[:, 0:2, :], ALU.mult).then_inc(mul, 1)
                if spectrum.shape[1] == 3:
                    dve.tensor_tensor(scratch[:, 2:4, :], src, spectrum[:, 1:3, :], ALU.mult).then_inc(mul, 1)
                else:
                    dve.tensor_tensor(scratch[:, 2, :], src[:, 0, :], spectrum[:, 1, :], ALU.mult)
                    dve.tensor_tensor(scratch[:, 3, :], src[:, 1, :], spectrum[:, 0, :], ALU.mult).then_inc(mul, 1)
                dve.wait_ge(mul, 2 * h + 1)
                dve.tensor_tensor(out[:, 0, :], scratch[:, 0, :], scratch[:, 1, :], ALU.add).then_inc(added, 1)
                dve.wait_ge(mul, 2 * h + 2)
                dve.tensor_tensor(out[:, 1, :], scratch[:, 2, :], scratch[:, 3, :], ALU.subtract).then_inc(added, 1)

            def step(it, k):
                b = batch(it, k)
                if b is not None:
                    slot = (k // CH) % 2
                    dve.wait_ge(x_in[slot], 16 * (it + 1))
                    for a in range(TT):
                        for n in range(D // 512):
                            dve.bn_stats(st[:, a, n, :], xn[slot][:, a, n * 512:(n + 1) * 512]).then_inc(ln_bn, 1)
                    n_ready = counted(dve, TT * (D // 512) * (b + 1))
                    dve.wait_ge(consts_in, 16 * N_CONST)
                    dve.wait_ge(ln_bn, n_ready)
                    for a in range(TT):
                        dve.bn_aggr(mv[:, a, :], st[:, a, :, :]).then_inc(ln_mv, 1)
                b = batch(it, k - AFTER_LN) if k >= AFTER_LN else None
                if b is not None:
                    dve.wait_ge(ln_std, b + 1)
                    if not isinstance(b, int) or b >= 1:
                        dve.wait_ge(x_normed, TT * b)
                    dve.reciprocal(rstd[:], std[:]).then_inc(ln_rstd, 1)
                    dve.wait_ge(ln_rstd, b + 1)
                    dve.scalar_tensor_tensor(nmr[:], mv[:, :, 0], -1.0, rstd[:], ALU.mult, ALU.mult).then_inc(ln_scale, 1)
                h = chunk(it, k, AFTER_F)
                if h is not None:
                    kk = k - AFTER_F
                    dve.wait_ge(q_sb, h + 1)
                    dve.wait_ge(k_sb, h + 1)
                    if not isinstance(h, int) or h >= 3:
                        dve.wait_ge(zo_sum, 2 * (h - 2))
                    elif h >= 1:
                        dve.wait_ge(p_sum, 2 * h)
                    if not isinstance(h, int) or h >= 2:
                        dve.wait_ge(c_mm, h - 1)
                    products(qf[kk % 2][:], kf[kk % 4], pr, pf[kk % 2], p_mul, p_sum, h)
                h = chunk(it, k, AFTER_T)
                if h is not None:
                    dve.wait_ge(wt_sb, h + 1)
                    dve.tensor_tensor(ws[:, 1, :, :], bu[:], ws[:, 0, :, :], ALU.subtract).then_inc(wl_ok, 1)
                h = chunk(it, k, AFTER_C)
                if h is not None:
                    s = (k - AFTER_C) % 2
                    n_ready, n_used = counted(dve, h + 1), counted(dve, h - 1)
                    dve.wait_ge(consts_in, 16 * N_CONST)
                    if not isinstance(h, int) or h >= 2:
                        dve.wait_ge(t_mm, n_used)
                    dve.wait_ge(c_sb, n_ready)
                    for j in range(CT):
                        dve.max(top[s][:, j, 0:8], co[s][:, j, :]).then_inc(top_a, 1)
                    for j in range(CT):
                        n_ready = counted(dve, CT * h + j + 1)
                        dve.wait_ge(consts_in, 16 * N_CONST)
                        dve.wait_ge(top_a, n_ready)
                        dve.match_replace(wk[s][:, j, :], top[s][:, j, 0:8], co[s][:, j, :], NEG).then_inc(top_cut, 1)
                    for j in range(CT):
                        n_ready = counted(dve, CT * h + j + 1)
                        dve.wait_ge(consts_in, 16 * N_CONST)
                        dve.wait_ge(top_cut, n_ready)
                        dve.max(top[s][:, j, 8:16], wk[s][:, j, :]).then_inc(top_b, 1)
                    dve.wait_ge(top_b, CT * (h + 1))
                    dve.tensor_scalar(nmax[s][:], top[s][:, :, 0], -1.0, None, ALU.mult).then_inc(nmax_ok, 1)
                h = chunk(it, k, AFTER_T)
                if h is not None:
                    s4, s = (k - AFTER_T) % 4, (k - AFTER_T) % 2
                    g = chunk(it, k, AFTER_F)
                    dve.wait_ge(p_sum, 2 * LAST if g is None else 2 * (g + 1))
                    if not isinstance(h, int) or h >= 2:
                        dve.wait_ge(i_mm, h - 1)
                    dve.wait_ge(we_mm, h + 1)
                    products(by[:], kf[s4], pr, zf[s][:, 0:2, :], ze_mul, ze_sum, h)
                    dve.wait_ge(ze_sum, 2 * (h + 1))
                    dve.wait_ge(wo_mm, h + 1)
                    products(bz[:], vf[s4], pr, zf[s][:, 2:4, :], zo_mul, zo_sum, h)
                h = chunk(it, k, AFTER_C)
                if h is not None:
                    s = (k - AFTER_C) % 2
                    for j in range(CT):
                        dve.wait_ge(e_sb, CT * h + j + 1)
                        dve.scalar_tensor_tensor(wk[s][:, j, :], co[s][:, j, :], top[s][:, j, TOPK - 1:TOPK], wk[s][:, j, :], ALU.is_ge, ALU.mult, accum_out=wsum[s][:, j:j + 1]).then_inc(w_cut, 1)
                    dve.wait_ge(w_cut, CT * (h + 1))
                    dve.reciprocal(wrec[s][:], wsum[s][:]).then_inc(w_rec, 1)
                h = chunk(it, k, AFTER_I)
                if h is not None:
                    s = (k - AFTER_I) % 2
                    dve.wait_ge(i_mm, h + 1)
                    dve.wait_ge(xt_in[s], 16 * (4 * it + (k - AFTER_I) // 2 + 1))
                    if not isinstance(h, int) or h >= 2:
                        dve.wait_ge(x1_out[s], 16 * (4 * it + (k - AFTER_I) // 2))
                        dve.wait_ge(added_ok, h - 1)
                    dve.tensor_tensor(xo[s][:].rearrange("p (a j) t -> p a (j t)", a=2), bu[:], xt[s][:].rearrange("p (a j) t -> p a (j t)", a=2), ALU.add).then_inc(x1_sum, 1)
            steps(dve, step, AFTER_I)
    nc.clear_and_free_semaphores(sems)
    nc.all_engine_barrier()


def ffn_phase(nc, x1, x1_sums, w_split, w_sums, loraT, bias, gateT, gate_b, ctxT, ident_d, xn3, rows3, masks, feat, keep, bad):
    NPAIR, _, KT, T = x1.shape
    L = T // 2
    D = KT * P
    OT = KT
    R = loraT.shape[0]
    OG = w_split.shape[3]
    NG = gateT.shape[1] - R
    RANKS = (8, 16, 32, 64)
    QT = T // P
    LAG, RING = 2, 4
    WR = 2
    CR = 8
    NCH, CK = 4, KT // 4
    GT, GU = 4, 8
    NGRP = KT // GT
    MOVES = (1.0, 0.8, 0.6, 0.5, 0.4)
    COUNTS = len(MOVES) + 1
    WINDOW = 16
    FRAC = keep / L
    lo, hi = -9.0, 9.0
    for _ in range(60):
        z = (lo + hi) / 2
        lo, hi = (z, hi) if 0.5 * math.erfc(z / math.sqrt(2)) > FRAC else (lo, z)
    TOKENS_PER_STD = L * math.exp(-z * z / 2) / math.sqrt(2 * math.pi)
    AIM = 2.0 * (keep - WINDOW // 2) - L
    NEG = -3.0e38
    CHUNK_UNITS = 2 * CK
    UNITS = 2 * KT

    stack = ExitStack()
    sb = lambda name, shape, dt=FP32: stack.enter_context(nc.sbuf_tensor(name, shape, dt))
    sems = []

    def sem(name):
        sems.append(nc.alloc_semaphore(name))
        return sems[-1]
    with stack:
        xr = [sb(f"xr{i}", [P, KT, T]) for i in range(2)]
        xh, xl = sb("xh", [P, KT, T], FP16), sb("xl", [P, KT, T], FP16)
        sq = sb("sq", [P, CK, T])
        g32 = sq[:].rearrange("p k t -> p (k t)")[:, 0:KT * (R + NG)].rearrange("p (k r) -> p k r", k=KT)
        ws = [sb(f"ws{i}", [P, KT, 2, P], FP16) for i in range(WR)]
        mk = [sb(f"mk{i}", [P, KT, T], UINT8) for i in range(2)]
        ct = [sb(f"ct{i}", [P, T]) for i in range(CR)]
        cut = [sb(f"cut{i}", [P, 2, L]) for i in range(2)]
        top = sb("top2", [P, 2, WINDOW])
        rank, pick, vk = sb("rank", [P, WINDOW]), sb("pick_k", [P, 2, WINDOW]), sb("vk", [P, 2])
        st6, mv = sb("st6", [P, GU, 6]), sb("mv2", [P, GU, 2])
        std, guess = sb("std_c", [P, GU]), [sb(f"minus_guess{i}", [P, GU]) for i in range(2)]
        slope, off = [sb(f"slope{i}", [P, GU]) for i in range(2)], sb("off", [P, GU])
        above = [sb(f"above{i}", [P, GU]) for i in range(2)]
        limit, kth = [sb(f"limit{i}", [P, GU]) for i in range(2)], [sb(f"kth{i}", [P, GU]) for i in range(2)]
        kept, wrong = sb("kept", [P, UNITS]), sb("wrong", [P, 1])
        signs = [sb(f"signs{i}", [P, L], BF16) for i in range(2)]
        aug = sb("aug", [R + 1, OT * P])
        gh, gl = sb("gh", [P, KT, R + NG], FP16), sb("gl", [P, KT, R + NG], FP16)
        gsum = sb("gsum", [1, R + NG])
        gb = sb("gb", [P, NG])
        bcol = sb("bcol", [P, OT])
        ident = sb("ident2", [P, P])
        ones = sb("ones", [P, P])
        minus1 = sb("minus1", [P, 1], FP16)
        eps = sb("eps2", [P, 2])
        red2, red3 = sb("red2", [P, 2, T]), sb("red3", [P, 2, T])
        mean2, r2, msq = sb("mean2", [P, T]), [sb(f"r2_{i}", [P, T]) for i in range(2)], sb("msq", [P, T])
        part = msq
        mean3, s3, r3 = sb("mean3", [P, T]), sb("s3", [P, T]), sb("r3", [P, T])
        ev = sb("ev", [P, T])
        sf = [ev[:, b * L:(b + 1) * L] for b in range(2)]
        low = sb("low", [P, QT, R])
        rc, mx = sb("rc", [P, QT]), sb("mx", [P, QT])
        sc, nb = sb("sc", [P, QT, NG]), sb("nb", [P, QT, NG])
        arhs = sb("arhs", [R + 1, T])
        cf = [sb(f"cf{i}", [P, L]) for i in range(4)]
        fp = sb("feat_pair", [P, 4, 2, KT])
        acc = [stack.enter_context(nc.psum_tensor(f"acc{i}", [P, T], FP32)) for i in range(RING)]
        ps_s, ps_q, ps_g, ps_a = (stack.enter_context(nc.psum_tensor(n, [P, 512], FP32)) for n in ("ps_s", "ps_q", "ps_g", "ps_a"))
        unread = ps_a[:].rearrange("p (h l) -> p h l", h=2)
        raw = ps_g[:, 0:QT * (R + NG)].rearrange("p (q r) -> p q r", q=QT)
        rcol = ps_g[:, QT * (R + NG):QT * (R + NG) + QT]

        x_in = [[sem(f"x1_in{i}_{c}") for c in range(NCH)] for i in range(2)]
        w_in = [sem(f"w_in{i}") for i in range(WR)]
        c_in = [sem(f"c_in{i}") for i in range(CR)]
        x_out = [[sem(f"xn3_out{i}_{c}") for c in range(NCH)] for i in range(2)]
        m_out = [sem(f"mask_out{i}") for i in range(2)]
        (k_in, ws_in, wsum_mm, aug_ok, r_in, k_set, g_hi, g_lo, gsum_mm, gsum_ok, hi_ok, lo_ok, low2_ok, sq_ok, part_ok, sum_ok, st2_mm, mean2_ok, msq_ok, var2_ok,
         std2, r2_ok, g_mm, rcol_mm, rc_ok, sc_ok, low_ok, low_t, arhs_ok, arow_ok, main_mm, out_mm, ev_ok, x2_ok,
         st3_mm, mean3_ok, var3_ok, std3, r3_ok, cent_ok, xn3_ok, cmax_ok, smax_ok, csum_ok, xsum_ok,
         feat_ok, red_ok, row_out, bn_ok, mv_ok, std_ok, init_ok, guess_ok, off_ok, sign_ok, fin_ok, ind_ok, cut_ok, top_ok, kth_ok, mask_ok, bad_ok) = map(sem, (
             "k2_in", "w_sums_in", "w_sums_mm", "aug_ok", "red2_in", "k2_set", "g_hi", "g_lo", "gsum_mm", "gsum_ok", "x_hi", "x_lo", "x_lo2", "sq_ok", "part_ok", "sum_ok", "st2_mm", "mean2_ok", "msq_ok", "var2_ok",
             "std2", "r2_ok", "g_mm", "rcol_mm", "rc_ok", "sc_ok", "low_ok", "low_t", "arhs_ok", "arow_ok", "main_mm", "out_mm", "ev_ok", "x2_ok",
             "st3_mm", "mean3_ok", "var3_ok", "std3", "r3_ok", "cent_ok", "xn3_ok", "cmax_ok", "smax_ok", "csum_ok", "xsum_ok",
             "feat_ok", "red_ok", "row_out", "bn_ok", "mv_ok", "std_ok", "init_ok", "guess_ok", "off_ok", "sign_ok", "fin_ok", "ind_ok", "cut_ok", "top_ok", "kth_ok", "mask_ok", "bad_ok"))
        block = stack.enter_context(nc.Block())
        SC_STEPS = 6
        NORM3 = {2 + 2 * c: c for c in range(NCH)}
        FEAT = 4
        POOL_LOW = 2
        STATS2 = 8
        SUMS3 = {7: 0, 9: 1, 13: 2}

        def pairs(eng, pair, tail):
            pair(0, 0, 0)
            pair(1, 1, 0)
            if NPAIR > 4:
                with eng.Fori(1, NPAIR // 2 - 1) as it:
                    pair(2 * it, 0, it)
                    pair(2 * it + 1, 1, it)
            if NPAIR > 2:
                pair(NPAIR - 2, 0, NPAIR // 2 - 1)
                pair(NPAIR - 1, 1, NPAIR // 2 - 1)
            tail(NPAIR, 0, NPAIR // 2)

        least = lambda i, n: not isinstance(i, int) or i >= n
        first = lambda i: not least(i, 1)
        is_last = lambda i: isinstance(i, int) and i == NPAIR - 1
        ended = lambda i: isinstance(i, int) and i == NPAIR

        def square_at(i, c):
            return NCH * i + c

        @block.sync
        def _(sp):
            sp.dma_start(g32, gateT.rearrange("(k p) r -> p k r", p=P)).then_inc(k_in, 16)
            sp.dma_start(gb[:], gate_b.partition_broadcast(P)).then_inc(k_in, 16)
            with nc.allow_non_contiguous_dma(reason="a column of biases per output tile, once"):
                sp.dma_start(bcol[:], bias.rearrange("(o p) -> p o", p=P)).then_inc(k_in, 16)
            sp.dma_start(ident[:], ident_d).then_inc(k_in, 16)
            sp.dma_start(aug[0:R, :], loraT).then_inc(k_in, 16)
            sp.dma_start(xr[1][:, 0:OT // OG, :], w_sums.rearrange("p (c n) -> p c n", n=T)).then_inc(ws_in, 16)

            for c in range(NCH):
                k = slice(c * CK, (c + 1) * CK)
                sp.dma_start(xr[0][:, k, :], x1[0, :, k, :]).then_inc(x_in[0][c], 16)
            sp.dma_start(red2[:], x1_sums[0, :, :, :]).then_inc(r_in, 16)

            def pair(i, s, u):
                for o in range(OT):
                    if o == 2 and not is_last(i):
                        sp.wait_ge(st2_mm, i + 1)
                        sp.dma_start(red2[:], x1_sums[bass.ds(i + 1, 1), :, :, :].rearrange("a p w t -> p (a w) t")).then_inc(r_in, 16)
                    if o >= WR or not first(i):
                        sp.wait_ge(main_mm, OT * i + (o - WR + 1))
                    sp.dma_start(ws[o % WR][:].rearrange("p k a n -> p k (a n)"), w_split[o // OG, :, :, o % OG, :, :].rearrange("k p a n -> p k (a n)")).then_inc(w_in[o % WR], 16)
            pairs(sp, pair, lambda i, s, u: None)

        @block.gpsimd
        def _(pool):
            pool.memset(ones[:], 1.0).then_inc(k_set, 1)
            pool.memset(minus1[:], -1.0).then_inc(k_set, 1)
            pool.memset(eps[:, 0:1], EPS).then_inc(k_set, 1)
            pool.memset(eps[:, 1:2], EPS * W_SCALE ** 2).then_inc(k_set, 1)
            pool.memset(bad[:], 0.0).then_inc(k_set, 1)
            for w in range(WINDOW):
                pool.memset(rank[:, w:w + 1], w + 1.0).then_inc(k_set, 1)

            def load_ctx(i, n):
                pool.dma_start(ct[n % CR][:], ctxT[bass.ds(i, 1), :, n, :].rearrange("a p t -> p (a t)")).then_inc(c_in[n % CR], 16)
            for n in range(CR):
                load_ctx(0, n)

            def centre3(i, s, c):
                n_stats = counted(pool, i)
                v = xr[s][:, c * CK:(c + 1) * CK, :]
                pool.wait_ge(k_set, 5 + WINDOW)
                pool.wait_ge(mean3_ok, n_stats)
                pool.tensor_tensor(v, v, mean3[:].unsqueeze(1).broadcast_to([P, CK, T]), ALU.subtract).then_inc(cent_ok, 1)

            def scale3(i, s, c):
                n_stats, n_cent = counted(pool, i), counted(pool, NCH * (i - 1) + c + 1)
                v = xr[s][:, c * CK:(c + 1) * CK, :]
                pool.wait_ge(k_set, 5 + WINDOW)
                pool.wait_ge(r3_ok, n_stats)
                pool.wait_ge(cent_ok, n_cent)
                pool.tensor_tensor(v, v, r3[:].unsqueeze(1).broadcast_to([P, CK, T]), ALU.mult).then_inc(xn3_ok, 1)

            def low_part(i, s):
                k = slice(POOL_LOW * CK, (POOL_LOW + 1) * CK)
                n_hi = counted(pool, NCH * i + POOL_LOW + 1)
                pool.wait_ge(k_set, 5 + WINDOW)
                pool.wait_ge(hi_ok, n_hi)
                pool.tensor_tensor(xl[:, k, :], xr[s][:, k, :], xh[:, k, :], ALU.subtract).then_inc(low2_ok, 1)

            def cut_tile(i, o):
                g, n = (o // GT - 1) % 2, (o - GT) % KT
                at = KT * i + o - GT
                n_fin, n_top, n_ind = counted(pool, 2 * (NGRP * i + o // GT)), counted(pool, 6 * (at - 1)), counted(pool, 2 * at + 2)
                pool.wait_ge(k_set, 5 + WINDOW)
                pool.wait_ge(fin_ok, n_fin)
                if o >= GT + 2 or not first(i):
                    pool.wait_ge(top_ok, n_top)
                for bb in range(2):
                    u = 2 * (n % GT) + bb
                    pool.tensor_scalar(cut[n % 2][:, bb, :], ct[n % CR][:, bb * L:(bb + 1) * L], limit[g][:, u:u + 1], NEG, ALU.is_gt, ALU.mult).then_inc(ind_ok, 1)
                pool.wait_ge(k_set, 5 + WINDOW)
                pool.wait_ge(ind_ok, n_ind)
                c = cut[n % 2][:].rearrange("p b t -> p (b t)")
                pool.tensor_tensor(c, c, ct[n % CR][:], ALU.add).then_inc(cut_ok, 1)

            def load_next(i, o):
                if not (o + GT >= KT and is_last(i)) and not ended(i):
                    n_mask = counted(pool, 2 * (KT * i + o - GT + 1))
                    pool.wait_ge(k_set, 5 + WINDOW)
                    pool.wait_ge(mask_ok, n_mask)
                    load_ctx(i + (o + GT) // KT, (o + GT) % KT)

            def norm3(i, s, o):
                if not first(i) and o in NORM3:
                    scale3(i, s, NORM3[o])
                if not first(i) and o + 1 in NORM3:
                    centre3(i, s, NORM3[o + 1])

            def step(i, s, o):
                masked = (o >= GT or not first(i)) and not (ended(i) and o >= GT)
                if o == 12 and not is_last(i):
                    low_part(i + 1, 1 - s)
                if masked and o % GT == 0:
                    cut_tile(i, o)
                if o % GT < GT - 1:
                    if masked:
                        cut_tile(i, o + 1)
                    norm3(i, 1 - s, o)
                if masked:
                    load_next(i, o)
                if o % GT == GT - 1:
                    norm3(i, 1 - s, o)

            def pair(i, s, u):
                for o in range(OT):
                    step(i, s, o)

            def tail(i, s, u):
                for o in range(max(NORM3) + 1):
                    step(i, s, o)
            low_part(0, 0)
            pairs(pool, pair, tail)

        @block.tensor
        def _(pe):
            pe.wait_ge(k_in, 80)
            pe.wait_ge(k_set, 4)
            pe.wait_ge(ws_in, 16)
            for c in range(OT // OG):
                pe.matmul(acc[c][0:R + 1, :], ones[:, 0:R + 1], xr[1][:, c, :], start=True, stop=True).then_inc(wsum_mm, 1)
            pe.wait_ge(g_lo, 1)
            for part_, g in enumerate((gh, gl)):
                for k in range(KT):
                    mm = pe.matmul(ps_g[0:1, 0:R + NG], minus1[:], g[:, k, :], start=part_ == 0 and k == 0, stop=part_ == 1 and k == KT - 1)
            mm.then_inc(gsum_mm, 1)

            def main(i, o):
                b = o % RING
                pe.wait_ge(w_in[o % WR], 16 * (OT // WR) * i + 16 * (o // WR + 1))
                if o >= RING or not first(i):
                    pe.wait_ge(ev_ok, OT * i + o - RING + 1)
                product = lambda k, a, x, start: pe.matmul(acc[b][:], ws[o % WR][:, k, a, :], x[:, k, :], start=start, stop=False)
                if o == 0:
                    for k in range(KT):
                        if k % CK == 0:
                            pe.wait_ge(hi_ok, NCH * i + k // CK + 1)
                        product(k, 0, xh, k == 0)
                        product(k, 1, xh, False)
                    for k in range(KT):
                        c = k // CK
                        if k % CK == 0 and c == POOL_LOW:
                            pe.wait_ge(low2_ok, i + 1)
                        elif k % CK == 0:
                            pe.wait_ge(lo_ok, (NCH - 1) * i + c + (c < POOL_LOW))
                        mm = product(k, 0, xl, False)
                else:
                    for k in range(KT):
                        for a, x in ((0, xh), (1, xh), (0, xl)):
                            mm = product(k, a, x, k == 0 and a == 0 and x is xh)
                mm.then_inc(main_mm, 1)

            def correct(i, s, o):
                if o == 0:
                    pe.wait_ge(arhs_ok, i + 1)
                    pe.wait_ge(arow_ok, i + 1)
                pe.matmul(acc[o % RING][:], aug[:, o * P:(o + 1) * P], arhs[:], start=False, stop=True).then_inc(out_mm, 1)

            def stats(red, done):
                pe.matmul(ps_s[:], ones[:], red[:, 0, :], start=True, stop=True)
                pe.matmul(ps_q[:], ones[:], red[:, 1, :], start=True, stop=True).then_inc(done, 1)

            def stats2(i):
                if not first(i):
                    pe.wait_ge(arhs_ok, i)
                if least(i, 2):
                    pe.wait_ge(var3_ok, i - 1)
                    pe.wait_ge(mean3_ok, i - 1)
                pe.wait_ge(r_in, 16 * (i + 1))
                stats(red2, st2_mm)

            def stats3(i):
                pe.wait_ge(arhs_ok, NPAIR if ended(i) else i + 1)
                pe.wait_ge(sum_ok, 2 * square_at(i, 0))
                stats(red3, st3_mm)

            def gates(i, s):
                pe.wait_ge(mean2_ok, i + 1)
                pe.wait_ge(gsum_ok, 1)
                if not first(i):
                    pe.wait_ge(low_ok, 4 * i)
                for q in range(QT):
                    t = slice(q * P, (q + 1) * P)
                    for k in range(KT):
                        for x, g in ((xh, gh), (xh, gl), (xl, gh)):
                            pe.matmul(raw[:, q, :], x[:, k, t], g[:, k, :], start=k == 0 and x is xh and g is gh, stop=False)
                    mm = pe.matmul(raw[:, q, :], mean2[0:1, t], gsum[:], start=False, stop=True)
                mm.then_inc(g_mm, 1)
                pe.wait_ge(r2_ok, i + 1)
                for q in range(QT):
                    mm = pe.matmul(rcol[:, q:q + 1], r2[s][0:1, q * P:(q + 1) * P], ones[0:1, 0:1], start=True, stop=True)
                mm.then_inc(rcol_mm, 1)

            def pair(i, s, u):
                for o in range(OT):
                    if o > LAG:
                        correct(i, s, o - LAG - 1)
                    main(i, o)
                    if o == STATS2 and not is_last(i):
                        stats2(i + 1)
                    if o == 1:
                        gates(i, s)
                    if o == LAG:
                        n_low, n_var = counted(pe, 4 * (i + 1)), counted(pe, i + 1)
                        pe.wait_ge(k_set, 4)
                        pe.wait_ge(var2_ok, n_var)
                        pe.wait_ge(low_ok, n_low)
                        for q in range(QT):
                            mm = pe.transpose(ps_s[0:R, q * P:(q + 1) * P], low[:, q, :], ident[:])
                        mm.then_inc(low_t, 1)
                    if o == LAG + 1 and not first(i):
                        stats3(i)
                for o in range(OT - LAG - 1, OT):
                    correct(i, s, o)
            stats2(0)
            pe.wait_ge(aug_ok, OT // OG)
            pairs(pe, pair, lambda i, s, u: stats3(i))

        @block.scalar
        def _(act):
            act.wait_ge(k_in, 80)
            act.wait_ge(k_set, 4)
            act.activation(gh[:], g32, ACT.Copy, scale=W_SCALE).then_inc(g_hi, 1)

            def square(at, src, c):
                if isinstance(at, int) and at == 0:
                    act.wait_ge(g_lo, 1)
                else:
                    act.wait_ge(part_ok, at)
                act.activation(sq[:], src[:, c * CK:(c + 1) * CK, :], ACT.Square).then_inc(sq_ok, 1)

            def high(i, s, n_in):
                if not first(i):
                    act.wait_ge(main_mm, OT * i)
                    act.wait_ge(g_mm, i)
                for c in range(NCH):
                    k = slice(c * CK, (c + 1) * CK)
                    act.wait_ge(x_in[s][c], n_in)
                    act.activation(xh[:, k, :], xr[s][:, k, :], ACT.Copy).then_inc(hi_ok, 1)

            def deviation2(i, s):
                act.wait_ge(var2_ok, i + 1)
                act.activation(msq[:], r2[s][:], ACT.Sqrt, bias=eps[:, 1:2], scale=W_SCALE ** 2).then_inc(std2, 1)

            def lora(i, s):
                act.wait_ge(low_t, i + 1)
                if not first(i):
                    act.wait_ge(out_mm, OT * i)
                act.activation(arhs[0:R, :], ps_s[0:R, :], ACT.Copy).then_inc(arhs_ok, 1)

            def deviation3(i):
                act.wait_ge(var3_ok, i)
                if least(i, 2):
                    act.wait_ge(row_out, 32 * (i - 1))
                act.activation(s3[:], r3[:], ACT.Sqrt, bias=eps[:, 0:1]).then_inc(std3, 1)

            def sums(i, s, o):
                for n in range(4 * o, 4 * o + 4):
                    at = UNITS * (i - 1) + n
                    act.wait_ge(cmax_ok, at + 1)
                    if n or least(i, 2):
                        act.wait_ge(csum_ok, at)
                        act.wait_ge(xsum_ok, at)
                    act.activation(unread[:, 0, :], cf[n % 4][:], ACT.Copy, accum_out=fp[:, 1, n % 2, n // 2:n // 2 + 1]).then_inc(csum_ok, 1)
                    act.activation(unread[:, 1, :], xr[s][:, n // 2, (n % 2) * L:(n % 2 + 1) * L], ACT.Copy, accum_out=fp[:, 3, n % 2, n // 2:n // 2 + 1]).then_inc(xsum_ok, 1)
                if o == KT // 2 - 1:
                    act.wait_ge(xsum_ok, UNITS * i)
                    act.wait_ge(smax_ok, UNITS * i)
                    act.activation(feat[:, :, bass.ds(2 * (i - 1), 2), :], fp[:], ACT.Copy).then_inc(feat_ok, 1)

            def count(i, q, n):
                g = NGRP * i + q
                act.wait_ge(guess_ok, COUNTS * g + n + 1)
                for u in range(GU):
                    at = GU * COUNTS * g + GU * n + u
                    if not isinstance(at, int) or at >= 2:
                        act.wait_ge(sign_ok, at - 1)
                    k = GT * q + u // 2
                    act.activation(signs[u % 2][:], ct[k % CR][:, (u % 2) * L:(u % 2 + 1) * L], ACT.Sign, bias=guess[q % 2][:, u:u + 1], accum_out=above[q % 2][:, u:u + 1]).then_inc(sign_ok, 1)

            def store_x(i, s, c):
                k = slice(c * CK, (c + 1) * CK)
                act.wait_ge(xn3_ok, NCH * (i - 1) + c + 1)
                act.dma_start(xn3[bass.ds(i - 1, 1), :, k, :].rearrange("a p k t -> p (a k) t"), xr[s][:, k, :]).then_inc(x_out[s][c], 16)

            def stores(i, s):
                act.wait_ge(mask_ok, 2 * KT * i)
                act.wait_ge(std3, i)
                act.dma_start(masks[bass.ds(i - 1, 1), :, :, :].rearrange("a p k t -> p (a k) t"), mk[s][:]).then_inc(m_out[s], 16)
                act.dma_start(rows3[0:1, bass.ds(i - 1, 1), :].rearrange("r a t -> r (a t)"), mean3[0:1, :]).then_inc(row_out, 16)
                act.dma_start(rows3[1:2, bass.ds(i - 1, 1), :].rearrange("r a t -> r (a t)"), s3[0:1, :]).then_inc(row_out, 16)

            def load_x1(i, s, u, c):
                if first(i):
                    act.wait_ge(wsum_mm, OT // OG)
                else:
                    act.wait_ge(x_out[1 - s][c], 16 * (u + s))
                    act.wait_ge(xsum_ok, UNITS * (i - 1) + CHUNK_UNITS * (c + 1))
                    act.wait_ge(smax_ok, UNITS * (i - 1) + CHUNK_UNITS * (c + 1))
                k = slice(c * CK, (c + 1) * CK)
                act.dma_start(xr[1 - s][:, k, :], x1[bass.ds(i + 1, 1), :, k, :].rearrange("a p k t -> p (a k) t")).then_inc(x_in[1 - s][c], 16)

            def trail(i, s, o):
                if o == 0:
                    act.wait_ge(x2_ok, OT * i)
                    square(square_at(i, 0) - 1, xr[s], NCH - 1)
                if o == 1:
                    deviation3(i)
                if o - 2 in NORM3:
                    store_x(i, s, NORM3[o - 2])

            def step(i, s, u, o):
                q, r = o // GT, o % GT
                if not first(i):
                    trail(i, 1 - s, o)
                if not is_last(i) and o - FEAT - 2 in range(0, 2 * NCH, 2):
                    load_x1(i, s, u, (o - FEAT - 2) // 2)
                if not is_last(i) and o == 12:
                    high(i + 1, 1 - s, 16 * (u + s + 1))
                if r:
                    count(i, q, 2 * r - 1)
                if not first(i) and FEAT <= o < FEAT + KT // 2:
                    sums(i, 1 - s, o - FEAT)
                if r == 0:
                    act.wait_ge(mv_ok, GU * (NGRP * i + q + 1))
                    act.activation(std[:], mv[:, :, 1], ACT.Sqrt).then_inc(std_ok, 1)
                if r < 3:
                    count(i, q, 2 * r)
                if o == 6 and not first(i):
                    stores(i, 1 - s)
                if o in (4, 8, 12):
                    act.wait_ge(x2_ok, OT * i + o)
                    square(square_at(i, o // CK - 1), xr[s], o // CK - 1)
                if not is_last(i):
                    if o == STATS2 + 2:
                        deviation2(i + 1, 1 - s)
                    if o == 14:
                        lora(i + 1, 1 - s)

            def pair(i, s, u):
                for o in range(OT):
                    step(i, s, u, o)

            def tail(i, s, u):
                for o in range(FEAT + KT // 2):
                    trail(i, 1 - s, o)
                    if o >= FEAT:
                        sums(i, 1 - s, o - FEAT)
                stores(i, 1 - s)
                act.wait_ge(feat_ok, NPAIR)
                for p in range(2):
                    for c in range(NCH):
                        act.wait_ge(x_out[p][c], 16 * (NPAIR // 2))
                    act.wait_ge(m_out[p], 16 * (NPAIR // 2))
                act.wait_ge(row_out, 32 * NPAIR)
            high(0, 0, 16)
            act.wait_ge(gsum_mm, 1)
            act.activation(gsum[:], ps_g[0:1, 0:R + NG], ACT.Copy).then_inc(gsum_ok, 1)
            deviation2(0, 0)
            lora(0, 0)
            pairs(act, pair, tail)

        @block.vector
        def _(dve):
            dve.wait_ge(k_in, 80)
            for c in range(OT // OG):
                dve.wait_ge(wsum_mm, c + 1)
                dve.tensor_scalar(aug[R:R + 1, c * T:(c + 1) * T], acc[c][R:R + 1, :], -1.0, None, ALU.mult).then_inc(aug_ok, 1)
            dve.wait_ge(g_hi, 1)
            dve.scalar_tensor_tensor(gl[:], g32, W_SCALE, gh[:], ALU.mult, ALU.subtract).then_inc(g_lo, 1)

            def chunk_sums(at, src, c, red):
                if not isinstance(at, int) or at >= 1:
                    dve.wait_ge(sum_ok, 2 * at)
                dve.tensor_reduce(part[:], src[:, c * CK:(c + 1) * CK, :].rearrange("p k t -> p t k"), AX.X, ALU.add).then_inc(red_ok, 1)
                for which in range(2):
                    if which:
                        dve.wait_ge(sq_ok, at + 1)
                        dve.wait_ge(sum_ok, 2 * at + 1)
                        dve.tensor_reduce(part[:], sq[:].rearrange("p k t -> p t k"), AX.X, ALU.add).then_inc(part_ok, 1)
                        dve.wait_ge(part_ok, at + 1)
                    else:
                        dve.wait_ge(red_ok, at + 1)
                    if c:
                        dve.tensor_tensor(red[:, which, :], red[:, which, :], part[:], ALU.add).then_inc(sum_ok, 1)
                    else:
                        dve.tensor_copy(red[:, which, :], part[:]).then_inc(sum_ok, 1)

            def variance(mean, var, st, mean_ok, m_sq, var_ok, i, n):
                dve.wait_ge(st, i + 1)
                dve.tensor_scalar(mean[:], ps_s[:], 1.0 / D, None, ALU.mult).then_inc(mean_ok, 1)
                dve.wait_ge(mean_ok, i + 1)
                dve.tensor_tensor(msq[:], mean[:], mean[:], ALU.mult).then_inc(m_sq, 1)
                dve.wait_ge(m_sq, n + 1)
                dve.scalar_tensor_tensor(var[:], ps_q[:], 1.0 / D, msq[:], ALU.mult, ALU.subtract).then_inc(var_ok, 1)

            def low_parts(i, s):
                for c in range(NCH):
                    if c == POOL_LOW:
                        continue
                    k = slice(c * CK, (c + 1) * CK)
                    dve.wait_ge(hi_ok, NCH * i + c + 1)
                    dve.tensor_tensor(xl[:, k, :], xr[s][:, k, :], xh[:, k, :], ALU.subtract).then_inc(lo_ok, 1)

            def norm2(i, s):
                if not first(i):
                    dve.wait_ge(g_mm, i)
                    dve.wait_ge(arow_ok, i)
                variance(mean2, r2[s], st2_mm, mean2_ok, msq_ok, var2_ok, i, 0 if first(i) else 2 * i - 1)

            def scale2(i, s):
                dve.wait_ge(std2, i + 1)
                dve.reciprocal(r2[s][:], msq[:]).then_inc(r2_ok, 1)

            def means_row(i):
                if not first(i):
                    dve.wait_ge(out_mm, OT * i)
                dve.wait_ge(mean2_ok, i + 1)
                dve.tensor_copy(arhs[R:R + 1, :], mean2[R:R + 1, :]).then_inc(arow_ok, 1)

            def gates(i):
                dve.wait_ge(rcol_mm, i + 1)
                dve.tensor_copy(rc[:], rcol).then_inc(rc_ok, 1)
                dve.wait_ge(rc_ok, i + 1)
                n = SC_STEPS * i
                dve.tensor_tensor(sc[:], raw[:, :, R:R + NG], rc[:].unsqueeze(2).broadcast_to([P, QT, NG]), ALU.mult).then_inc(sc_ok, 1)
                dve.wait_ge(sc_ok, n + 1)
                dve.tensor_tensor(sc[:], sc[:], gb[:].unsqueeze(1).broadcast_to([P, QT, NG]), ALU.add).then_inc(sc_ok, 1)
                dve.wait_ge(sc_ok, n + 2)
                dve.tensor_reduce(mx[:], sc[:], AX.X, ALU.max).then_inc(sc_ok, 1)
                dve.wait_ge(sc_ok, n + 3)
                dve.tensor_tensor(nb[:], sc[:], mx[:].unsqueeze(2).broadcast_to([P, QT, NG]), ALU.is_lt).then_inc(sc_ok, 1)
                dve.wait_ge(sc_ok, n + 4)
                for r in (1, 2):
                    dve.tensor_tensor(nb[:, :, r], nb[:, :, r], nb[:, :, r - 1], ALU.mult).then_inc(sc_ok, 1)
                    dve.wait_ge(sc_ok, n + 4 + r)
                if not first(i):
                    dve.wait_ge(low_t, i)
                dve.tensor_copy(low[:, :, 0:RANKS[0]], raw[:, :, 0:RANKS[0]]).then_inc(low_ok, 1)
                for r in range(3):
                    w = RANKS[r + 1] - RANKS[r]
                    dve.tensor_tensor(low[:, :, RANKS[r]:RANKS[r + 1]], raw[:, :, RANKS[r]:RANKS[r + 1]], nb[:, :, r:r + 1].broadcast_to([P, QT, w]), ALU.mult).then_inc(low_ok, 1)

            def moments(i, q):
                g = NGRP * i + q
                ctx = lambda c: ct[(GT * q + c // 2) % CR][:, (c % 2) * L:(c % 2 + 1) * L]
                n_bn = counted(dve, GU * (g + 1))
                for c in range(GU):
                    n = GT * q + c // 2
                    dve.wait_ge(c_in[n % CR], 16 * (KT // CR) * i + 16 * (n // CR + 1))
                    dve.bn_stats(st6[:, c, :], ctx(c)).then_inc(bn_ok, 1)
                dve.wait_ge(k_in, 80)
                dve.wait_ge(bn_ok, n_bn)
                for c in range(GU):
                    dve.bn_aggr(mv[:, c, :], st6[:, c, :]).then_inc(mv_ok, 1)

            def first_guess(i, q):
                g = NGRP * i + q
                dve.wait_ge(std_ok, g + 1)
                dve.tensor_scalar(slope[q % 2][:], std[:], 0.5 / TOKENS_PER_STD, None, ALU.mult).then_inc(init_ok, 1)
                dve.scalar_tensor_tensor(guess[q % 2][:], std[:], -z, mv[:, :, 0], ALU.mult, ALU.subtract).then_inc(guess_ok, 1)

            def move_guess(i, q, n):
                g = NGRP * i + q
                dve.wait_ge(sign_ok, GU * COUNTS * g + GU * (n + 1))
                if n == 0:
                    dve.wait_ge(init_ok, g + 1)
                dve.scalar_tensor_tensor(off[:], above[q % 2][:], AIM, slope[q % 2][:], ALU.subtract, ALU.mult).then_inc(off_ok, 1)
                dve.wait_ge(off_ok, len(MOVES) * g + n + 1)
                dve.wait_ge(guess_ok, COUNTS * g + n + 1)
                dve.scalar_tensor_tensor(guess[q % 2][:], off[:], -MOVES[n], guess[q % 2][:], ALU.mult, ALU.add).then_inc(guess_ok, 1)

            def end_guess(i, q):
                g = NGRP * i + q
                dve.wait_ge(sign_ok, GU * COUNTS * (g + 1))
                if not isinstance(g, int) or g >= 2:
                    dve.wait_ge(cut_ok, GT * (g - 1))
                dve.tensor_scalar(limit[q % 2][:], guess[q % 2][:], -1.0, None, ALU.mult).then_inc(fin_ok, 1)
                dve.tensor_scalar(kth[q % 2][:], above[q % 2][:], -0.5, keep - 0.5 * L, ALU.mult, ALU.add).then_inc(fin_ok, 1)

            def mask_tile(i, s, u, o):
                at = KT * i + o - GT
                n, g = (o - GT) % KT, (o // GT - 1) % 2
                m = mk[s if o >= GT else 1 - s]
                n_cut, n_top = counted(dve, at + 1), counted(dve, 6 * at + 2)
                n_rep, n_all = counted(dve, 6 * at + 4), counted(dve, 6 * at + 6)
                dve.wait_ge(k_in, 80)
                dve.wait_ge(cut_ok, n_cut)
                for b in range(2):
                    dve.max(top[:, b, 0:8], cut[n % 2][:, b, :]).then_inc(top_ok, 1)
                dve.wait_ge(k_in, 80)
                dve.wait_ge(top_ok, n_top)
                for b in range(2):
                    dve.match_replace(cut[n % 2][:, b, :], top[:, b, 0:8], cut[n % 2][:, b, :], NEG).then_inc(top_ok, 1)
                k2 = kth[g][:, 2 * (n % GT):2 * (n % GT) + 2].unsqueeze(2).broadcast_to([P, 2, WINDOW])
                dve.wait_ge(fin_ok, 2 * (NGRP * i + o // GT))
                dve.tensor_tensor(pick[:], rank[:].unsqueeze(1).broadcast_to([P, 2, WINDOW]), k2, ALU.is_equal).then_inc(kth_ok, 1)
                dve.wait_ge(k_in, 80)
                dve.wait_ge(top_ok, n_rep)
                for b in range(2):
                    dve.max(top[:, b, 8:16], cut[n % 2][:, b, :]).then_inc(top_ok, 1)
                dve.wait_ge(top_ok, n_all)
                dve.wait_ge(kth_ok, 3 * at + 1)
                dve.tensor_tensor(pick[:], pick[:], top[:], ALU.mult).then_inc(kth_ok, 1)
                dve.wait_ge(kth_ok, 3 * at + 2)
                dve.tensor_reduce(vk[:], pick[:], AX.X, ALU.add).then_inc(kth_ok, 1)
                dve.wait_ge(kth_ok, 3 * at + 3)
                if o == GT and least(i, 2):
                    dve.wait_ge(m_out[s], 16 * u)
                for b in range(2):
                    dve.tensor_scalar(m[:, n, b * L:(b + 1) * L], ct[n % CR][:, b * L:(b + 1) * L], vk[:, b:b + 1], 0.0, ALU.is_ge, ALU.add, accum_out=kept[:, 2 * n + b:2 * n + b + 1]).then_inc(mask_ok, 1)

            def check_masks(i):
                dve.wait_ge(mask_ok, UNITS * i)
                dve.tensor_scalar(kept[:], kept[:], float(keep), None, ALU.not_equal).then_inc(bad_ok, 1)
                dve.wait_ge(bad_ok, 3 * i - 2)
                dve.tensor_reduce(wrong[:], kept[:], AX.X, ALU.max).then_inc(bad_ok, 1)
                dve.wait_ge(bad_ok, 3 * i - 1)
                dve.tensor_tensor(bad[:], bad[:], wrong[:], ALU.max).then_inc(bad_ok, 1)
                dve.wait_ge(bad_ok, 3 * i)

            def norm3(i):
                if least(i, 2):
                    dve.wait_ge(row_out, 32 * (i - 1))
                    dve.wait_ge(xn3_ok, NCH * (i - 1))
                variance(mean3, r3, st3_mm, mean3_ok, msq_ok, var3_ok, i - 1, 2 * i - (1 if ended(i) else 0))
                dve.wait_ge(std3, i)
                dve.reciprocal(r3[:], s3[:]).then_inc(r3_ok, 1)

            def features(i, s, n):
                at = UNITS * (i - 1) + n
                n_used, n_now, n_next = counted(dve, at - 2), counted(dve, at + 1), counted(dve, at + 2)
                n_x2 = counted(dve, OT * i + (0 if ended(i) else FEAT + n // 4))
                n_tile, n_pairs = counted(dve, NCH * (i - 1) + n // CHUNK_UNITS + 1), counted(dve, i - 1)
                k = n // 2
                dve.wait_ge(k_in, 80)
                if n == 0 and least(i, 2):
                    dve.wait_ge(feat_ok, n_pairs)
                dve.wait_ge(x2_ok, n_x2)
                dve.wait_ge(xn3_ok, n_tile)
                dve.wait_ge(mask_ok, n_next)
                if n >= 4 or least(i, 2):
                    dve.wait_ge(csum_ok, n_used)
                    dve.wait_ge(smax_ok, n_used)
                for b in range(2):
                    t = slice(b * L, (b + 1) * L)
                    dve.tensor_tensor_reduce(out=cf[(n + b) % 4][:], in0=mk[s][:, k, t], in1=xr[s][:, k, t], scale=1.0, scalar=NEG, op0=ALU.mult, op1=ALU.max,
                                             accum_out=fp[:, 0, b, k:k + 1]).then_inc(cmax_ok, 1)
                for b in range(2):
                    dve.wait_ge(k_in, 80)
                    dve.wait_ge(cmax_ok, (n_now, n_next)[b])
                    t = slice(b * L, (b + 1) * L)
                    dve.tensor_tensor_reduce(out=sf[b], in0=xr[s][:, k, t], in1=cf[(n + b) % 4][:], scale=1.0, scalar=NEG, op0=ALU.subtract, op1=ALU.max,
                                             accum_out=fp[:, 2, b, k:k + 1]).then_inc(smax_ok, 1)

            def trail(i, s, u, o):
                if o == 0:
                    dve.wait_ge(x2_ok, OT * i)
                    chunk_sums(square_at(i, 0) - 1, xr[s], NCH - 1, red3)
                if o == 1:
                    norm3(i)
                if FEAT <= o < FEAT + KT // 2:
                    for n in range(4 * (o - FEAT), 4 * (o - FEAT) + 4, 2):
                        features(i, s, n)

            def take(i, s, o):
                at = OT * i + o
                dve.wait_ge(out_mm, at + 1)
                if o >= 1 or not first(i):
                    dve.wait_ge(x2_ok, at)
                if not first(i) and FEAT <= o < FEAT + KT // 2:
                    dve.wait_ge(smax_ok, UNITS * (i - 1) + 4 * (o - FEAT + 1))
                dve.tensor_tensor(ev[:], acc[o % RING][:], r2[s][:], ALU.mult).then_inc(ev_ok, 1)
                dve.wait_ge(ev_ok, at + 1)
                dve.scalar_tensor_tensor(xr[s][:, o, :], ev[:], bcol[:, o:o + 1], xr[s][:, o, :], ALU.add, ALU.add).then_inc(x2_ok, 1)

            def step(i, s, u, o):
                q, r = o // GT, o % GT
                if not first(i):
                    trail(i, 1 - s, u, o)
                if r == 0:
                    moments(i, q)
                if r in (1, 2):
                    move_guess(i, q, 2 * r - 1)
                if o <= 12:
                    take(i, s, o)
                if not is_last(i) and o == 12:
                    low_parts(i + 1, 1 - s)
                if r == 0:
                    first_guess(i, q)
                if 12 <= o < OT - 1:
                    take(i, s, o + 1)
                if not is_last(i) and o == 14:
                    means_row(i + 1)
                    gates(i + 1)
                if o >= GT or not first(i):
                    mask_tile(i, s, u, o)
                if o == GT - 1 and not first(i):
                    check_masks(i)
                if o in SUMS3:
                    c = SUMS3[o]
                    if c == 0 and not first(i):
                        dve.wait_ge(st3_mm, i)
                    dve.wait_ge(x2_ok, OT * i + CK * (c + 1))
                    chunk_sums(square_at(i, c), xr[s], c, red3)
                if o == STATS2 + 2 and not is_last(i):
                    norm2(i + 1, 1 - s)
                if r < 3:
                    move_guess(i, q, 2 * r)
                else:
                    end_guess(i, q)
                if o == STATS2 + 3 and not is_last(i):
                    scale2(i + 1, 1 - s)

            def pair(i, s, u):
                for o in range(OT):
                    step(i, s, u, o)

            def tail(i, s, u):
                for o in range(FEAT + KT // 2):
                    trail(i, 1 - s, u, o)
                    if o < GT:
                        mask_tile(i, s, u, o)
                check_masks(i)
            low_parts(0, 0)
            norm2(0, 0)
            scale2(0, 0)
            means_row(0)
            gates(0)
            pairs(dve, pair, tail)
    nc.clear_and_free_semaphores(sems)
    nc.all_engine_barrier()


def exact_masks_phase(nc, ctxT, xn3, masks, feat, bad, keep):
    NPAIR, _, KT, T = ctxT.shape
    L = T // 2
    NEG = -3.0e38
    FULL, REST = keep // 8, keep % 8
    ROUNDS = FULL + (REST > 0)
    TAKES = 2 * (2 * ROUNDS + (REST > 0))
    FEATURES = 6

    stack = ExitStack()
    sb = lambda name, shape, dt=FP32: stack.enter_context(nc.sbuf_tensor(name, shape, dt))
    sems = []

    def sem(name):
        sems.append(nc.alloc_semaphore(name))
        return sems[-1]
    with stack:
        ones = sb("ones_e", [P, 1])
        flag = sb("flag", [1, 1], mybir.dt.int32)
        c, x = sb("ctx_e", [P, T]), sb("xn3_e", [P, T])
        left = sb("left", [P, T])
        m = sb("mask_e", [P, T], UINT8)
        top = sb("top_e", [P, 8])
        kept, other = sb("kept_e", [P, 2, L]), sb("other_e", [P, 2, L])
        four = sb("four_e", [P, 4, 2])
        any_bad = stack.enter_context(nc.psum_tensor("any_bad", [1, 1], FP32))
        ones_set, flag_mm, flag_ok, c_in, x_in, take_ok, mask_ok, stored, feat_ok, tile_ok = map(sem, (
            "ones_e_set", "flag_mm", "flag_ok", "ctx_e_in", "xn3_e_in", "take_e_ok", "mask_e_ok", "mask_e_out", "feat_e_ok", "tile_e_ok"))
        block = stack.enter_context(nc.Block())

        @block.gpsimd
        def _(pool):
            pool.memset(ones[:], 1.0).then_inc(ones_set, 1)

        @block.tensor
        def _(pe):
            pe.wait_ge(ones_set, 1)
            pe.matmul(any_bad[:], ones[:], bad[:], start=True, stop=True).then_inc(flag_mm, 1)

        @block.sync
        def _(sp):
            sp.wait_ge(flag_ok, 1)
            again = sp.value_load(flag[0:1, 0:1], min_val=0, max_val=P)
            with sp.If(again > 0):
                with sp.Fori(0, NPAIR) as i, sp.Fori(0, KT) as n:
                    tile = lambda ap: ap[bass.ds(i, 1), :, bass.ds(n, 1), :].rearrange("a p k t -> p (a k t)")
                    n_before, n_masks = counted(sp, KT * i + n), counted(sp, 2 * (KT * i + n) + 2)
                    sp.wait_ge(ones_set, 1)
                    sp.wait_ge(tile_ok, n_before)
                    sp.dma_start(c[:], tile(ctxT)).then_inc(c_in, 16)
                    sp.dma_start(x[:], tile(xn3)).then_inc(x_in, 16)
                    sp.wait_ge(ones_set, 1)
                    sp.wait_ge(mask_ok, n_masks)
                    sp.dma_start(tile(masks), m[:]).then_inc(stored, 16)
                sp.wait_ge(stored, 16 * NPAIR * KT)

        @block.vector
        def _(dve):
            dve.wait_ge(flag_mm, 1)
            dve.tensor_copy(flag[:], any_bad[:]).then_inc(flag_ok, 1)
            dve.wait_ge(flag_ok, 1)
            again = dve.value_load(flag[0:1, 0:1], min_val=0, max_val=P)
            with dve.If(again > 0):
                with dve.Fori(0, NPAIR) as i, dve.Fori(0, KT) as n:
                    at = KT * i + n
                    done = TAKES * at
                    n_in = counted(dve, 16 * at + 16)
                    dve.wait_ge(ones_set, 1)
                    dve.wait_ge(c_in, n_in)
                    for b in range(2):
                        t = slice(b * L, (b + 1) * L)
                        src = c[:, t]
                        for r in range(ROUNDS):
                            n_max = counted(dve, done + 1)
                            dve.max(top[:], src).then_inc(take_ok, 1)
                            dve.wait_ge(ones_set, 1)
                            dve.wait_ge(take_ok, n_max)
                            done = done + 1
                            if r == FULL:
                                n_cut = counted(dve, done + 1)
                                dve.memset(top[:, REST:8], NEG).then_inc(take_ok, 1)
                                dve.wait_ge(ones_set, 1)
                                dve.wait_ge(take_ok, n_cut)
                                done = done + 1
                            n_out = counted(dve, done + 1)
                            dve.match_replace(left[:, t], top[:], src, NEG).then_inc(take_ok, 1)
                            dve.wait_ge(ones_set, 1)
                            dve.wait_ge(take_ok, n_out)
                            done = done + 1
                            src = left[:, t]
                    dve.wait_ge(stored, 16 * at)
                    for b in range(2):
                        t = slice(b * L, (b + 1) * L)
                        dve.tensor_scalar(m[:, t], left[:, t], NEG, None, ALU.is_le).then_inc(mask_ok, 1)
                    x2 = x[:].rearrange("p (b t) -> p b t", b=2)
                    dve.wait_ge(mask_ok, 2 * at + 2)
                    dve.wait_ge(x_in, 16 * at + 16)
                    dve.tensor_tensor(kept[:], m[:].rearrange("p (b t) -> p b t", b=2), x2, ALU.mult).then_inc(feat_ok, 1)
                    dve.wait_ge(feat_ok, FEATURES * at + 1)
                    dve.tensor_tensor(other[:], x2, kept[:], ALU.subtract).then_inc(feat_ok, 1)
                    dve.tensor_reduce(four[:, 0, :], kept[:], AX.X, ALU.max).then_inc(feat_ok, 1)
                    dve.tensor_reduce(four[:, 1, :], kept[:], AX.X, ALU.add).then_inc(feat_ok, 1)
                    dve.wait_ge(feat_ok, FEATURES * at + 2)
                    dve.tensor_reduce(four[:, 2, :], other[:], AX.X, ALU.max).then_inc(feat_ok, 1)
                    dve.tensor_reduce(four[:, 3, :], x2, AX.X, ALU.add).then_inc(feat_ok, 1)
                    dve.wait_ge(feat_ok, FEATURES * at + 6)
                    dve.tensor_copy(feat[:, :, bass.ds(2 * i, 2), bass.ds(n, 1)].rearrange("p q b k -> p q (b k)"), four[:]).then_inc(tile_ok, 1)
                    dve.wait_ge(tile_ok, at + 1)
    nc.clear_and_free_semaphores(sems)
    nc.all_engine_barrier()


def channel_gates_phase(nc, feat, conv_w, gamma, beta, shift_d, ident_d, att, keep, L):
    _, _, NB, J = feat.shape
    G = J // 2
    W = 2 * P
    N = NB * G * W
    TAPS = 7
    PAD = TAPS // 2
    assert NB * G == P
    stack = ExitStack()
    sb = lambda name, shape, dt=FP32: stack.enter_context(nc.sbuf_tensor(name, shape, dt))
    sem = lambda name: stack.enter_context(nc.semaphore(name))
    with stack:
        fy = sb("fy", [P, 4, 2, NB, G])
        y = sb("y_pad", [P, 4, W + 2 * PAD])
        z = sb("z_conv", [P, 2, W])
        zz = sb("z_square", [P, W])
        zs, mu, var, rs = sb("z_sum", [P, 2]), sb("z_mu", [P, 2]), sb("z_var", [P, 2]), sb("z_rs", [P, 2])
        cw, gm, bt = sb("cw", [P, 2 * TAPS]), sb("bn_g", [P, 1]), sb("bn_b", [P, 1])
        shift = sb("shift", [P, 2, P])
        ident, ones, eps = sb("ident_b", [P, P]), sb("ones_b", [P, P]), sb("eps_b", [P, 1])
        yt = stack.enter_context(nc.psum_tensor("yt", [P, 4, W], FP32))
        halo = stack.enter_context(nc.psum_tensor("halo", [P, 2, 4, PAD], FP32))
        tot = stack.enter_context(nc.psum_tensor("tot", [P, 4], FP32))
        back = stack.enter_context(nc.psum_tensor("back", [P, 2, 2, P], FP32))
        (k_in, k_set, fy_ok, y_mm, y_ok, halo_mm, halo_ok, tap_ok, sum_ok, mu_mm, mu_ok, cen_ok, sq_ok, var_mm, std_ok,
         rs_ok, sc_ok, bn_ok, sig_ok, back_mm, a2_ok, att_ok) = map(sem, (
             "kb_in", "kb_set", "fy_ok", "y_mm", "y_ok", "halo_mm", "halo_ok", "tap_ok", "z_sum_ok", "mu_mm", "mu_ok", "cen_ok", "zsq_ok", "zvar_mm", "zstd_ok",
             "zrs_ok", "zsc_ok", "zbn_ok", "sig_ok", "back_mm", "a2_ok", "att_ok"))
        block = stack.enter_context(nc.Block())

        @block.sync
        def _(sp):
            sp.dma_start(cw[:], conv_w.rearrange("a c k -> (a c k)").partition_broadcast(P)).then_inc(k_in, 16)
            sp.dma_start(gm[:], gamma.partition_broadcast(P)).then_inc(k_in, 16)
            sp.dma_start(bt[:], beta.partition_broadcast(P)).then_inc(k_in, 16)
            sp.dma_start(shift[:], shift_d).then_inc(k_in, 16)
            sp.dma_start(ident[:], ident_d).then_inc(k_in, 16)

        @block.gpsimd
        def _(pool):
            pool.memset(ones[:], 1.0).then_inc(k_set, 1)
            pool.memset(eps[:], EPS).then_inc(k_set, 1)

        @block.tensor
        def _(pe):
            pe.wait_ge(k_in, 80)
            pe.wait_ge(k_set, 2)
            for q in range(4):
                pe.wait_ge(fy_ok, 5)
                for h in range(2):
                    mm = pe.transpose(yt[:, q, h * P:(h + 1) * P], fy[:, q, h, :, :].rearrange("p b g -> p (b g)"), ident[:])
            mm.then_inc(y_mm, 1)
            pe.wait_ge(y_ok, 1)
            pe.matmul(halo[:, 0, :, :], shift[:, 0, :], y[:, :, W:W + PAD], start=True, stop=True)
            pe.matmul(halo[:, 1, :, :], shift[:, 1, :], y[:, :, PAD:2 * PAD], start=True, stop=True).then_inc(halo_mm, 1)
            pe.wait_ge(sum_ok, 1)
            pe.matmul(tot[:, 0:2], ones[:], zs[:], start=True, stop=True).then_inc(mu_mm, 1)
            pe.wait_ge(sq_ok, 2)
            pe.matmul(tot[:, 2:4], ones[:], var[:], start=True, stop=True).then_inc(var_mm, 1)
            pe.wait_ge(sig_ok, 1)
            for c in range(2):
                for h in range(2):
                    mm = pe.transpose(back[:, c, h, :], z[:, c, h * P:(h + 1) * P], ident[:])
            mm.then_inc(back_mm, 1)

        @block.scalar
        def _(act):
            act.wait_ge(k_set, 2)
            act.wait_ge(y_mm, 1)
            act.activation(y[:, :, PAD:PAD + W], yt[:], ACT.Copy).then_inc(y_ok, 1)
            for c in range(2):
                act.wait_ge(cen_ok, c + 1)
                if c:
                    act.wait_ge(sq_ok, c)
                act.activation(zz[:], z[:, c, :], ACT.Square, accum_out=var[:, c:c + 1]).then_inc(sq_ok, 1)
            act.wait_ge(var_mm, 1)
            act.activation(rs[:], tot[:, 2:4], ACT.Sqrt, bias=eps[:], scale=1.0 / N).then_inc(std_ok, 1)
            act.wait_ge(bn_ok, 4)
            act.activation(z[:], z[:], ACT.Sigmoid).then_inc(sig_ok, 1)

        @block.vector
        def _(dve):
            dve.wait_ge(k_in, 80)
            split = lambda q: feat[:, q, :, :].rearrange("p b (g h) -> p h b g", h=2)
            dve.tensor_copy(fy[:, 0, :, :, :], split(0)).then_inc(fy_ok, 1)
            dve.tensor_scalar(fy[:, 1, :, :, :], split(1), 1.0 / keep, None, ALU.mult).then_inc(fy_ok, 1)
            dve.tensor_copy(fy[:, 2, :, :, :], split(2)).then_inc(fy_ok, 1)
            dve.tensor_tensor(fy[:, 3, :, :, :], split(3), split(1), ALU.subtract).then_inc(fy_ok, 1)
            dve.wait_ge(fy_ok, 4)
            dve.tensor_scalar(fy[:, 3, :, :, :], fy[:, 3, :, :, :], 1.0 / (L - keep), None, ALU.mult).then_inc(fy_ok, 1)
            dve.wait_ge(halo_mm, 1)
            dve.tensor_copy(y[:, :, 0:PAD], halo[:, 0, :, :]).then_inc(halo_ok, 1)
            dve.tensor_copy(y[:, :, PAD + W:], halo[:, 1, :, :]).then_inc(halo_ok, 1)
            dve.wait_ge(halo_ok, 2)
            for tap in range(2 * TAPS):
                ch, k = tap // TAPS, tap % TAPS
                for c in range(2):
                    src, w = y[:, 2 * c + ch, k:k + W], cw[:, tap:tap + 1]
                    if tap == 0:
                        dve.tensor_scalar(z[:, c, :], src, w, None, ALU.mult).then_inc(tap_ok, 1)
                    else:
                        dve.wait_ge(tap_ok, 2 * (tap - 1) + c + 1)
                        dve.scalar_tensor_tensor(z[:, c, :], src, w, z[:, c, :], ALU.mult, ALU.add).then_inc(tap_ok, 1)
            dve.wait_ge(tap_ok, 4 * TAPS)
            dve.tensor_reduce(zs[:], z[:], AX.X, ALU.add).then_inc(sum_ok, 1)
            dve.wait_ge(mu_mm, 1)
            dve.tensor_scalar(mu[:], tot[:, 0:2], 1.0 / N, None, ALU.mult).then_inc(mu_ok, 1)
            dve.wait_ge(mu_ok, 1)
            for c in range(2):
                dve.tensor_scalar(z[:, c, :], z[:, c, :], mu[:, c:c + 1], None, ALU.subtract).then_inc(cen_ok, 1)
            dve.wait_ge(std_ok, 1)
            dve.reciprocal(rs[:], rs[:]).then_inc(rs_ok, 1)
            dve.wait_ge(rs_ok, 1)
            dve.tensor_scalar(rs[:], rs[:], gm[:], None, ALU.mult).then_inc(sc_ok, 1)
            dve.wait_ge(sc_ok, 1)
            dve.wait_ge(sq_ok, 2)
            for c in range(2):
                dve.tensor_scalar(z[:, c, :], z[:, c, :], rs[:, c:c + 1], bt[:], ALU.mult, ALU.add).then_inc(bn_ok, 1)
            for c in range(2):
                dve.wait_ge(bn_ok, c + 1)
                dve.tensor_scalar(z[:, c, :], z[:, c, :], 0.0, None, ALU.max).then_inc(bn_ok, 1)
            dve.wait_ge(back_mm, 1)
            dve.tensor_copy(att[:, 1, :, :, :].rearrange("p h b g -> p h (b g)"), back[:, 1, :, :]).then_inc(a2_ok, 1)
            dve.wait_ge(a2_ok, 1)
            dve.tensor_tensor(att[:, 0, :, :, :].rearrange("p h b g -> p h (b g)"), back[:, 0, :, :], att[:, 1, :, :, :].rearrange("p h b g -> p h (b g)"), ALU.subtract).then_inc(att_ok, 1)
            dve.wait_ge(att_ok, 1)


def experts_phase(nc, xn3, rows3, masks, att, routerT, router_b, expert_b, tail_rows, ident_d, out):
    NPAIR, _, KT, T = xn3.shape
    L = T // 2
    D = KT * P
    QT = T // P
    E = routerT.shape[1]
    A = E + 2
    NCH = 4
    CK = KT // NCH
    TOP = 8
    RING = 4
    STEPS = 14 + 2 * QT

    stack = ExitStack()
    sb = lambda name, shape, dt=FP32: stack.enter_context(nc.sbuf_tensor(name, shape, dt))
    pb = lambda name, shape: stack.enter_context(nc.psum_tensor(name, shape, FP32))
    sem = lambda name: stack.enter_context(nc.semaphore(name))
    with stack:
        xr = [sb(f"x3_{i}", [P, KT, T]) for i in range(2)]
        mk = [sb(f"mk3_{i}", [P, KT, T], UINT8) for i in range(2)]
        m3 = [sb(f"m3_{i}", [P, T]) for i in range(2)]
        s3 = [sb(f"s3_{i}", [P, T]) for i in range(2)]
        gc = [sb(f"gc{i}", [P, CK, T]) for i in range(NCH)]
        sq = [sb(f"sq3_{i}", [P, CK, T]) for i in range(2)]
        sr = [sb(f"sq_sum{i}", [P, T]) for i in range(2)]
        ost = [sb(f"ost{i}", [P, CK, T]) for i in range(NCH)]
        rt = sb("rt", [P, KT, A])
        rsq = sb("rsq", [P, A])
        eb = sb("eb", [A, D])
        pick = sb("pick", [A, P])
        rb, rsum = sb("rb", [P, E]), sb("rsum", [P, E])
        ident, ones, eps = sb("ident3", [P, P]), sb("ones3", [P, P]), sb("eps3", [P, 1])
        lgs, wds = sb("lgs", [A, T]), [sb(f"wds{i}", [A, T]) for i in range(2)]
        a1 = [sb(f"a1_{i}", [P, T]) for i in range(2)]
        mean, msq, r4 = sb("mean4", [P, QT]), sb("msq4", [P, QT]), sb("r4", [P, QT])
        mx, ws, rw = sb("mx4", [P, QT]), sb("ws4", [P, QT]), sb("rw4", [P, QT])
        lt, sc, lm = sb("lt", [P, QT, E]), sb("sc4", [P, QT, E]), sb("lm", [P, QT, E])
        top = sb("top4", [P, QT, TOP])
        wd = sb("wd", [P, QT, A])
        lg, tr, wt, ab = pb("lg", [P, 512]), pb("tr", [P, 512]), pb("wt3", [P, 512]), pb("ab", [P, 512])
        po = [pb(f"po{i}", [P, T]) for i in range(RING)]
        raw = tr[:, 0:QT * A].rearrange("p (q e) -> p q e", q=QT)

        x_in = [[sem(f"x3_in{i}_{c}") for c in range(NCH)] for i in range(2)]
        mk_in, row_in = [sem(f"mk3_in{i}") for i in range(2)], [sem(f"rows_in{i}") for i in range(2)]
        stored = [sem(f"out_stored{i}") for i in range(NCH)]
        (k_in, k_set, rsum_mm, rsum_ok, g_ok, u_ok, v_ok, x3_ok, sq_ok, sr_ok, x_mm, lg_mm, lg_ok, tr_mm, step_ok, var_ok, std_ok, arg_ok, exp_ok, wd_ok,
         wt_mm, wds_ok, ab_mm, a1_ok, prod_ok, bias_mm, out_ok) = map(sem, (
             "k3_in", "k3_set", "rsum_mm", "rsum_ok", "g3_ok", "u3_ok", "v3_ok", "x3_ok", "sq3_ok", "sr_ok", "x3_mm", "lg_mm", "lg_ok", "tr_mm", "step_ok", "var4_ok", "std4_ok", "arg_ok", "exp_ok", "wd_ok",
             "wt3_mm", "wds_ok", "ab_mm", "a1_ok", "prod_ok", "bias_mm", "out_ok"))
        block = stack.enter_context(nc.Block())

        def pairs(eng, pair, tail):
            pair(0, 0, 0)
            pair(1, 1, 0)
            if NPAIR > 4:
                with eng.Fori(1, NPAIR // 2 - 1) as it:
                    pair(2 * it, 0, it)
                    pair(2 * it + 1, 1, it)
            if NPAIR > 2:
                pair(NPAIR - 2, 0, NPAIR // 2 - 1)
                pair(NPAIR - 1, 1, NPAIR // 2 - 1)
            tail()

        is_last = lambda i: isinstance(i, int) and i == NPAIR - 1
        least = lambda i, n: not isinstance(i, int) or i >= n

        @block.sync
        def _(sp):
            sp.dma_start(rt[:, :, 0:E], routerT.rearrange("(k p) e -> p k e", p=P)).then_inc(k_in, 16)
            sp.dma_start(rb[:], router_b.partition_broadcast(P)).then_inc(k_in, 16)
            sp.dma_start(eb[0:E, :], expert_b).then_inc(k_in, 16)
            sp.dma_start(eb[E:A, :], tail_rows[:, 0:D]).then_inc(k_in, 16)
            sp.dma_start(pick[E:A, :], tail_rows[:, D:D + P]).then_inc(k_in, 16)
            sp.dma_start(ident[:], ident_d).then_inc(k_in, 16)

            def store(i, c):
                sp.dma_start(out[bass.ds(i, 1), :, c * CK:(c + 1) * CK, :].rearrange("a p k t -> p (a k) t"), ost[c][:]).then_inc(stored[c], 16)

            def load_masks(i, s):
                sp.dma_start(mk[s][:], masks[bass.ds(i, 1), :, :, :].rearrange("a p k t -> p (a k) t")).then_inc(mk_in[s], 16)
                sp.dma_start(s3[s][:], rows3[1:2, bass.ds(i, 1), :].rearrange("r a t -> (r a t)").partition_broadcast(P)).then_inc(row_in[s], 16)
                sp.dma_start(m3[s][:], rows3[0:1, bass.ds(i, 1), :].rearrange("r a t -> (r a t)").partition_broadcast(P)).then_inc(row_in[s], 16)
            load_masks(0, 0)

            def pair(i, s, u):
                for c in range(NCH):
                    k = slice(c * CK, (c + 1) * CK)
                    if least(i, 2):
                        n_used = counted(sp, KT * (i - 2) + CK * (c + 1))
                        sp.wait_ge(k_in, 96)
                        sp.wait_ge(prod_ok, n_used)
                    sp.dma_start(xr[s][:, k, :], xn3[bass.ds(i, 1), :, k, :].rearrange("a p k t -> p (a k) t")).then_inc(x_in[s][c], 16)
                for c in range(NCH):
                    if least(i, 2):
                        n_out = counted(sp, KT * (i - 2) + CK * (c + 1))
                        sp.wait_ge(k_in, 96)
                        sp.wait_ge(out_ok, n_out)
                        store(i - 2, c)
                if not is_last(i):
                    if least(i, 1):
                        n_x3 = counted(sp, NCH * i)
                        sp.wait_ge(k_in, 96)
                        sp.wait_ge(x3_ok, n_x3)
                    load_masks(i + 1, 1 - s)

            def tail():
                for i in (NPAIR - 2, NPAIR - 1):
                    for c in range(NCH):
                        sp.wait_ge(out_ok, KT * i + CK * (c + 1))
                        store(i, c)
                for c in range(NCH):
                    sp.wait_ge(stored[c], 16 * NPAIR)
            pairs(sp, pair, tail)

        @block.gpsimd
        def _(pool):
            pool.memset(ones[:], 1.0).then_inc(k_set, 1)
            pool.memset(eps[:], EPS).then_inc(k_set, 1)
            pool.memset(rt[:, :, E:E + 1], 1.0).then_inc(k_set, 1)
            pool.memset(rt[:, :, E + 1:A], 0.0).then_inc(k_set, 1)
            pool.memset(rsq[:, 0:E + 1], 0.0).then_inc(k_set, 1)
            pool.memset(rsq[:, E + 1:A], 1.0).then_inc(k_set, 1)
            pool.memset(pick[0:E, :], 0.0).then_inc(k_set, 1)

            def products(i, s, c):
                pool.wait_ge(a1_ok, i)
                if least(i, 2):
                    pool.wait_ge(stored[c], 16 * (i - 1))
                for k in range(c * CK, (c + 1) * CK):
                    pool.tensor_tensor(ost[c][:, k - c * CK, :], xr[s][:, k, :], a1[s][:], ALU.mult).then_inc(prod_ok, 1)

            def add_deviation(i, s, c):
                pool.wait_ge(g_ok, NCH * i + c + 1)
                pool.tensor_tensor(gc[c][:], gc[c][:], s3[s][:].unsqueeze(1).broadcast_to([P, CK, T]), ALU.add).then_inc(u_ok, 1)
            pool.wait_ge(row_in[0], 32)
            for c in range(NCH):
                add_deviation(0, 0, c)

            def pair(i, s, u):
                for c in range(NCH):
                    if least(i, 1):
                        products(i, 1 - s, c)
                    if not is_last(i):
                        if c == 0:
                            pool.wait_ge(row_in[1 - s], 32 * (u + s + 1))
                        add_deviation(i + 1, 1 - s, c)

            def tail():
                for c in range(NCH):
                    products(NPAIR, 1, c)
            pairs(pool, pair, tail)

        @block.tensor
        def _(pe):
            pe.wait_ge(k_in, 96)
            pe.wait_ge(k_set, 7)
            for k in range(KT):
                mm = pe.matmul(tr[:, 0:E], ones[:], rt[:, k, 0:E], start=k == 0, stop=k == KT - 1)
            mm.then_inc(rsum_mm, 1)

            def biases(i, s, c):
                for k in range(c * CK, (c + 1) * CK):
                    if k < RING and least(i, 2):
                        pe.wait_ge(out_ok, KT * (i - 1) + k - RING + 1)
                    elif k >= RING:
                        pe.wait_ge(out_ok, KT * (i - 1) + k - RING + 1)
                    if k == 0:
                        pe.wait_ge(wds_ok, i)
                    pe.matmul(po[k % RING][:], eb[:, k * P:(k + 1) * P], wds[s][:], start=True, stop=True).then_inc(bias_mm, 1)

            def logits(i, s, c):
                pe.wait_ge(x3_ok, NCH * i + c + 1)
                for k in range(c * CK, (c + 1) * CK):
                    pe.matmul(lg[0:A, :], rt[:, k, :], xr[s][:, k, :], start=k == 0, stop=False)

            def squares(i, c):
                pe.wait_ge(sr_ok, NCH * i + c + 1)
                pe.matmul(lg[0:A, :], rsq[:], sr[c % 2][:], start=False, stop=c == NCH - 1).then_inc(lg_mm if c == NCH - 1 else x_mm, 1)

            def weights(i, s):
                pe.wait_ge(wd_ok, i + 1)
                if least(i, 1):
                    pe.wait_ge(wds_ok, i)
                for q in range(QT):
                    mm = pe.transpose(wt[0:A, q * P:(q + 1) * P], wd[:, q, :], ident[:])
                mm.then_inc(wt_mm, 1)
                pe.wait_ge(wds_ok, i + 1)
                if least(i, 1):
                    pe.wait_ge(a1_ok, i)
                pe.matmul(ab[:], pick[:], wds[s][:], start=True, stop=True).then_inc(ab_mm, 1)

            def pair(i, s, u):
                if least(i, 1):
                    biases(i, 1 - s, 0)
                    pe.wait_ge(lg_ok, i)
                logits(i, s, 0)
                for c in range(1, NCH):
                    logits(i, s, c)
                    squares(i, c - 1)
                squares(i, NCH - 1)
                if least(i, 1):
                    biases(i, 1 - s, 1)
                pe.wait_ge(lg_ok, i + 1)
                if least(i, 1):
                    pe.wait_ge(wd_ok, i)
                else:
                    pe.wait_ge(rsum_ok, 1)
                for q in range(QT):
                    mm = pe.transpose(raw[:, q, :], lgs[:, q * P:(q + 1) * P], ident[0:A, 0:A])
                mm.then_inc(tr_mm, 1)
                if least(i, 1):
                    biases(i, 1 - s, 2)
                    biases(i, 1 - s, 3)
                weights(i, s)

            def tail():
                for c in range(NCH):
                    biases(NPAIR, 1, c)
            pairs(pe, pair, tail)

        @block.scalar
        def _(act):
            act.wait_ge(k_set, 7)
            act.wait_ge(rsum_mm, 1)
            act.activation(rsum[:], tr[:, 0:E], ACT.Copy).then_inc(rsum_ok, 1)

            def gates(i, s, c):
                if least(i, 1):
                    act.wait_ge(x3_ok, NCH * (i - 1) + c + 1)
                for k in range(c * CK, (c + 1) * CK):
                    for bb in range(2):
                        b = 2 * i + bb
                        t = slice(bb * L, (bb + 1) * L)
                        g = act.activation(gc[c][:, k - c * CK, t], mk[s][:, k, t], ACT.Identity, bias=att[:, 1, k % 2, bass.ds(b, 1), k // 2], scale=att[:, 0, k % 2, bass.ds(b, 1), k // 2])
                g.then_inc(g_ok, 1)

            def squares(i, s, c):
                act.wait_ge(x3_ok, NCH * i + c + 1)
                if c >= 2 or least(i, 1):
                    act.wait_ge(sr_ok, NCH * i + c - 1)
                act.activation(sq[c % 2][:], xr[s][:, c * CK:(c + 1) * CK, :], ACT.Square).then_inc(sq_ok, 1)

            def weights(i, s):
                act.wait_ge(var_ok, i + 1)
                act.activation(r4[:], r4[:], ACT.Sqrt, bias=eps[:]).then_inc(std_ok, 1)
                act.wait_ge(arg_ok, i + 1)
                act.activation(sc[:], lt[:], ACT.Exp).then_inc(exp_ok, 1)
                act.wait_ge(wt_mm, i + 1)
                if least(i, 2):
                    act.wait_ge(bias_mm, KT * (i - 1))
                act.activation(wds[s][:], wt[0:A, :], ACT.Copy).then_inc(wds_ok, 1)
                act.wait_ge(ab_mm, i + 1)
                if least(i, 2):
                    act.wait_ge(prod_ok, KT * (i - 1))
                act.activation(a1[s][:], ab[:], ACT.Identity, bias=ones[:, 0:1]).then_inc(a1_ok, 1)

            def pair(i, s, u):
                for c in range(NCH):
                    squares(i, s, c)
                    if not is_last(i):
                        if c == 0:
                            act.wait_ge(mk_in[1 - s], 16 * (u + s + 1))
                        gates(i + 1, 1 - s, c)
                act.wait_ge(lg_mm, i + 1)
                if least(i, 1):
                    act.wait_ge(tr_mm, i)
                act.activation(lgs[:], lg[0:A, :], ACT.Copy).then_inc(lg_ok, 1)
                weights(i, s)
            act.wait_ge(mk_in[0], 16)
            for c in range(NCH):
                gates(0, 0, c)
            pairs(act, pair, lambda: None)

        @block.vector
        def _(dve):
            dve.wait_ge(k_in, 96)

            def x3(i, s, u, c):
                v = xr[s][:, c * CK:(c + 1) * CK, :]
                dve.wait_ge(u_ok, NCH * i + c + 1)
                dve.wait_ge(x_in[s][c], 16 * (u + 1))
                dve.tensor_tensor(gc[c][:], gc[c][:], v, ALU.mult).then_inc(v_ok, 1)
                dve.wait_ge(v_ok, NCH * i + c + 1)
                if c == 0:
                    dve.wait_ge(row_in[s], 32 * (u + 1))
                dve.tensor_tensor(v, gc[c][:], m3[s][:].unsqueeze(1).broadcast_to([P, CK, T]), ALU.add).then_inc(x3_ok, 1)

            def sum_squares(i, c):
                dve.wait_ge(sq_ok, NCH * i + c + 1)
                if c >= 2:
                    dve.wait_ge(x_mm, (NCH - 1) * i + c - 1)
                elif least(i, 1):
                    dve.wait_ge(lg_mm, i)
                dve.tensor_reduce(sr[c % 2][:], sq[c % 2][:].rearrange("p k t -> p t k"), AX.X, ALU.add).then_inc(sr_ok, 1)

            def outputs(i, s, c):
                for k in range(c * CK, (c + 1) * CK):
                    n = KT * (i - 1) + k
                    dve.wait_ge(bias_mm, n + 1)
                    dve.wait_ge(prod_ok, n + 1)
                    o = ost[c][:, k - c * CK, :]
                    dve.tensor_tensor(o, o, po[k % RING][:], ALU.add).then_inc(out_ok, 1)

            def routing(i):
                bc = lambda m: m[:].unsqueeze(2).broadcast_to([P, QT, E])
                row = lambda m: m[:].unsqueeze(1).broadcast_to([P, QT, E])
                dve.wait_ge(tr_mm, i + 1)
                n = STEPS * i
                if least(i, 1):
                    dve.wait_ge(wt_mm, i)
                dve.tensor_scalar(mean[:], raw[:, :, E], 1.0 / D, None, ALU.mult).then_inc(step_ok, 1)
                dve.wait_ge(step_ok, n + 1)
                dve.tensor_tensor(msq[:], mean[:], mean[:], ALU.mult).then_inc(step_ok, 1)
                dve.wait_ge(step_ok, n + 2)
                dve.scalar_tensor_tensor(r4[:], raw[:, :, E + 1], 1.0 / D, msq[:], ALU.mult, ALU.subtract).then_inc(var_ok, 1)
                dve.tensor_tensor(lm[:], bc(mean), row(rsum), ALU.mult).then_inc(step_ok, 1)
                dve.wait_ge(step_ok, n + 3)
                dve.tensor_tensor(lt[:], raw[:, :, 0:E], lm[:], ALU.subtract).then_inc(step_ok, 1)
                dve.wait_ge(step_ok, n + 4)
                dve.wait_ge(std_ok, i + 1)
                dve.reciprocal(r4[:], r4[:]).then_inc(step_ok, 1)
                dve.wait_ge(step_ok, n + 5)
                dve.tensor_tensor(lt[:], lt[:], bc(r4), ALU.mult).then_inc(step_ok, 1)
                dve.wait_ge(step_ok, n + 6)
                dve.tensor_tensor(lt[:], lt[:], row(rb), ALU.add).then_inc(step_ok, 1)
                dve.wait_ge(step_ok, n + 7)
                dve.tensor_reduce(mx[:], lt[:], AX.X, ALU.max).then_inc(step_ok, 1)
                dve.wait_ge(step_ok, n + 8)
                dve.tensor_tensor(lt[:], lt[:], bc(mx), ALU.subtract).then_inc(arg_ok, 1)
                dve.wait_ge(exp_ok, i + 1)
                dve.tensor_reduce(mx[:], sc[:], AX.X, ALU.add).then_inc(step_ok, 1)
                dve.wait_ge(step_ok, n + 9)
                dve.reciprocal(mx[:], mx[:]).then_inc(step_ok, 1)
                dve.wait_ge(step_ok, n + 10)
                dve.tensor_tensor(sc[:], sc[:], bc(mx), ALU.mult).then_inc(step_ok, 1)
                n_ready = counted(dve, n + 11)
                dve.wait_ge(k_in, 96)
                dve.wait_ge(step_ok, n_ready)
                for q in range(QT):
                    dve.max(top[:, q, :], sc[:, q, :]).then_inc(step_ok, 1)
                    n_ready = counted(dve, n + 11 + q + 1)
                    dve.wait_ge(k_in, 96)
                    dve.wait_ge(step_ok, n_ready)
                for q in range(QT):
                    dve.scalar_tensor_tensor(wd[:, q, 0:E], sc[:, q, :], top[:, q, TOP - 1:TOP], sc[:, q, :], ALU.is_ge, ALU.mult).then_inc(step_ok, 1)
                    dve.wait_ge(step_ok, n + 11 + QT + q + 1)
                dve.tensor_reduce(ws[:], top[:], AX.X, ALU.add).then_inc(step_ok, 1)
                dve.wait_ge(step_ok, n + 12 + 2 * QT)
                dve.tensor_tensor(rw[:], r4[:], ws[:], ALU.mult).then_inc(step_ok, 1)
                dve.wait_ge(step_ok, n + 13 + 2 * QT)
                dve.tensor_copy(wd[:, :, E + 1], rw[:]).then_inc(step_ok, 1)
                dve.wait_ge(step_ok, n + 14 + 2 * QT)
                dve.scalar_tensor_tensor(wd[:, :, E], mean[:], -1.0, rw[:], ALU.mult, ALU.mult).then_inc(wd_ok, 1)

            def pair(i, s, u):
                for c in range(NCH):
                    x3(i, s, u, c)
                    if c:
                        sum_squares(i, c - 1)
                if least(i, 1):
                    outputs(i, 1 - s, 0)
                sum_squares(i, NCH - 1)
                if least(i, 1):
                    for c in range(1, NCH - 1):
                        outputs(i, 1 - s, c)
                routing(i)
                if least(i, 1):
                    outputs(i, 1 - s, NCH - 1)

            def tail():
                for c in range(NCH):
                    outputs(NPAIR, 1, c)
            pairs(dve, pair, tail)


def autocorrelation_lora_ffn_channel_attention_experts(nc, t):
    NB, L, D = t["x"].shape
    KEEP = int(np.floor(0.6 * L))
    KEEP += KEEP % 2
    pairs_shape = (NB // 2, P, D // P, 2 * L)
    scratch = lambda name, shape, dt=FP32: nc.dram_tensor(name, shape, dt, kind="Internal").ap()
    x1, xn3 = scratch("x1_pairs", pairs_shape), scratch("xn3_pairs", pairs_shape)
    x1_sums = scratch("x1_sums", (NB // 2, P, 2, 2 * L))
    masks = scratch("mask_pairs", pairs_shape, UINT8)
    rows3 = scratch("rows3", (2, NB // 2, 2 * L))
    w_split = scratch("w_split", (D // 512, D // P, P, 512 // P, 2, P), FP16)
    w_sums = scratch("w_sums", (P, D))
    dft = [t[n] for n in ("dft_q", "dft_k", "dft_we", "dft_vo", "dft_wo", "dft_ic", "dft_iz", "identity")]
    attention_phase(nc, t["x"], t["ctx"], t["xT"], dft, x1, x1_sums, t["wT"], w_split, w_sums)
    with nc.sbuf_tensor("feat", [P, 4, NB, D // P], FP32) as feat, nc.sbuf_tensor("bad", [P, 1], FP32) as bad:
        ffn_phase(nc, x1, x1_sums, w_split, w_sums, t["loraT"], t["ffn_b"], t["gateT"], t["gate_b"], t["ctx_pairs"], t["identity"], xn3, rows3, masks, feat, KEEP, bad)
        exact_masks_phase(nc, t["ctx_pairs"], xn3, masks, feat, bad, KEEP)
        with nc.sbuf_tensor("att", [P, 2, 2, NB, D // P // 2], FP32) as att:
            channel_gates_phase(nc, feat, t["conv_w"], t["bn_gamma"], t["bn_beta"], t["neighbours"], t["identity"], att, KEEP, L)
            experts_phase(nc, xn3, rows3, masks, att, t["routerT"], t["router_b"], t["expert_b"], t["tail_rows"], t["identity"], t["out_pairs"])


def two_parts(m):
    high = m.astype(np.float16).astype(np.float64)
    return np.stack([high, (m - high).astype(np.float16)]).astype(np.float32)


def layouts(x, ctx_4096, L0_ffn_W, L0_ffn_b, L0_ffn_A, L0_ffn_B, L0_ffn_gate_w, L0_ffn_gate_b, L1_xattn_conv_w, L1_xattn_bn_gamma,
            L1_xattn_bn_beta, L1_ffn_router_weight, L1_ffn_router_bias, L1_ffn_expert_bias):
    NB, L, D = x.shape
    q, k, we, vo, wo, ic, ie, io = dft_constants(L)
    q, k, we, vo, wo = [two_parts(DFT_SCALE * m) for m in (q, k, we, vo, wo)]
    ic, iz = ic.astype(np.float32), (np.concatenate([ie, io]) / DFT_SCALE).astype(np.float32)
    segments = D // (2 * P)
    neighbours = np.zeros((P, 2, P), np.float32)
    for row in range(P):
        if row % segments:
            neighbours[row - 1, 0, row] = 1.0
        if row % segments != segments - 1:
            neighbours[row + 1, 1, row] = 1.0
    tail_rows = np.zeros((2, D + P), np.float32)
    tail_rows[0, :D] = 1.0
    tail_rows[1, D:] = 1.0
    return dict(
        x=x, ctx=ctx_4096, xT=x.transpose(0, 2, 1),
        ctx_pairs=ctx_4096.reshape(NB // 2, 2, L, D // P, P).transpose(0, 4, 3, 1, 2).reshape(NB // 2, P, D // P, 2 * L),
        wT=L0_ffn_W.T, loraT=L0_ffn_B.T, ffn_b=L0_ffn_b, gateT=np.concatenate([L0_ffn_A, L0_ffn_gate_w]).T, gate_b=L0_ffn_gate_b,
        conv_w=L1_xattn_conv_w, bn_gamma=L1_xattn_bn_gamma, bn_beta=L1_xattn_bn_beta,
        routerT=L1_ffn_router_weight.T, router_b=L1_ffn_router_bias, expert_b=L1_ffn_expert_bias,
        dft_q=q, dft_k=k, dft_we=we, dft_vo=vo, dft_wo=wo, dft_ic=ic, dft_iz=iz,
        identity=np.eye(P, dtype=np.float32), neighbours=neighbours, tail_rows=tail_rows)


def kernel(**inputs):
    import concourse.bacc as bacc
    from concourse.bass_utils import run_bass_kernel_spmd

    nc = bacc.Bacc("TRN2", target_bir_lowering=False, num_devices=1)
    arrays = {n: np.ascontiguousarray(a) for n, a in layouts(**{n: np.asarray(a) for n, a in inputs.items()}).items()}
    t = {n: nc.dram_tensor(n, a.shape, FP32, kind="ExternalInput").ap() for n, a in arrays.items()}
    NB, L, D = arrays["x"].shape
    t["out_pairs"] = nc.dram_tensor("out_pairs", (NB // 2, P, D // P, 2 * L), FP32, kind="ExternalOutput").ap()
    autocorrelation_lora_ffn_channel_attention_experts(nc, t)
    r = run_bass_kernel_spmd(nc, [arrays], core_ids=[0])
    out = r.results[0]["out_pairs"].reshape(NB // 2, P, D // P, 2, L)
    return np.ascontiguousarray(out.transpose(0, 3, 4, 2, 1).reshape(NB, L, D))
```
